# Optimizing a Trainium2 kernel written in Bass

```python
import numpy as np
import jax
import jax.numpy as jnp

def _softmax(x, axis=-1):
    return jax.nn.softmax(x, axis=axis)

def _gelu(x):
    return jax.nn.gelu(x, approximate=True)

def _silu(x):
    return jax.nn.silu(x)

def _sigmoid(x):
    return jax.nn.sigmoid(x)

def _layernorm(x, axis=-1, eps=1e-05):
    m = jnp.mean(x, axis=axis, keepdims=True)
    v = jnp.var(x, axis=axis, keepdims=True)
    return (x - m) / jnp.sqrt(v + eps)

def _scatter_add(tgt, idx, src, axis=0):
    return tgt.at[idx].add(src)

def _segment_sum(src, seg, n):
    return jax.ops.segment_sum(src, seg, n)
kernel_name = 'mk_flamingo_gated_d1_seqx_r8_ec2f2a'

def setup_inputs(seed: int=0):
    np.random.seed(seed)
    _w = jnp.asarray

    def _rec_inputs():
        import jax
        import jax.numpy as jnp
        _rk = jax.random.key(seed)
        x = -0.0003929 + 0.9999 * jax.random.normal(jax.random.fold_in(_rk, 1), (32, 56, 512), jnp.float32)
        _lenS = 56 - jax.random.randint(jax.random.fold_in(_rk, 7), (32,), 0, max(1, 56 // 4) + 1, jnp.int32)
        _lenS2 = 1500 - jax.random.randint(jax.random.fold_in(_rk, 8), (32,), 0, max(1, 1500 // 4) + 1, jnp.int32)
        _ctx_4096P = jax.random.normal(jax.random.fold_in(_rk, 11), (32, 16, 512), jnp.float32)
        _ctx_4096c = jax.random.dirichlet(jax.random.fold_in(_rk, 511), 0.3 * jnp.ones((16,), jnp.float32), (32, 1500))
        _ctx_4096t = jnp.einsum('bsk,bkd->bsd', _ctx_4096c, _ctx_4096P)
        _ctx_4096t = _ctx_4096t * jax.lax.rsqrt(jnp.mean(jnp.square(_ctx_4096t)) + 1e-12) * 0.953939
        ctx_4096 = 2.81802e-05 + 1.00001 * (_ctx_4096t + 0.3 * jax.random.normal(jax.random.fold_in(_rk, 611), (32, 1500, 512), jnp.float32))
        _validS = jnp.arange(56)[None, :] < _lenS[:, None]
        _validS2 = jnp.arange(1500)[None, :] < _lenS2[:, None]
        _causal = jnp.tril(jnp.ones((56, 56), dtype=bool))
        mask_SxS2_bk0 = jnp.logical_not(jnp.broadcast_to(_validS2[0:1, :], (56, 1500)))
        _g = jax.random.normal(jax.random.fold_in(_rk, 9001), (2, 1), jnp.float32)
        _g = jnp.sign(_g) * jnp.maximum(jnp.abs(_g), 1.0) + (_g == 0) * 1.0
        g_xattn = _g[0]
        g_ffn = _g[1]
        return (x, ctx_4096, mask_SxS2_bk0, g_xattn, g_ffn)
    x, ctx_4096, mask_SxS2_bk0, g_xattn, g_ffn = _rec_inputs()

    def _L0_xattn_setup():
        import jax, jax.numpy as jnp
        import numpy as np
        N_HEAD = 32
        D_MODEL = 512
        N_KV_GROUPS = 8
        D_HEAD = D_MODEL // N_HEAD
        H_PER_G = N_HEAD // N_KV_GROUPS
        KV_DIM = N_KV_GROUPS * D_HEAD
        B, S = (2, 256)
        key = jax.random.key(seed)
        ks = jax.random.split(key, 8)
        q = jax.random.normal(ks[0], (B, S, D_MODEL), dtype=jnp.float32)
        k = jax.random.normal(ks[1], (B, S, D_MODEL), dtype=jnp.float32)
        v = jax.random.normal(ks[2], (B, S, D_MODEL), dtype=jnp.float32)
        mask = jnp.tril(jnp.ones((S, S), dtype=bool))
        w_q = jax.random.uniform(ks[3], (D_MODEL, D_MODEL), dtype=jnp.float32) * 0.02
        w_k = jax.random.uniform(ks[4], (KV_DIM, D_MODEL), dtype=jnp.float32) * 0.02
        w_v = jax.random.uniform(ks[5], (KV_DIM, D_MODEL), dtype=jnp.float32) * 0.02
        w_out = jax.random.uniform(ks[6], (D_MODEL, D_MODEL), dtype=jnp.float32) * 0.02
        return {'q': q, 'k': k, 'v': v, 'w_q': w_q, 'w_k': w_k, 'w_v': w_v, 'w_out': w_out, 'mask': mask}
    _L0_xattn_all = _L0_xattn_setup()
    _L0_xattn_in = {k: v for k, v in _L0_xattn_all.items() if k in ('w_q', 'w_k', 'w_v', 'w_out')}
    del _L0_xattn_all

    def _L0_ffn_setup():
        import jax, jax.numpy as jnp
        import numpy as np
        B, S, D = (4, 256, 512)
        NUM_EXPERTS, TOP_K = (3, 2)

        def _expert_outputs(h, w1, b1, w2, b2):
            pre = jnp.einsum('bsd,edf->ebsf', h, w1) + b1[:, None, None, :]
            act = jnp.stack([jnp.tanh(pre[0]), jax.nn.gelu(pre[1], approximate=False), jax.nn.silu(pre[2])])
            return jnp.einsum('ebsf,efd->ebsd', act, w2) + b2[:, None, None, :]
        key = jax.random.key(seed)
        ks = jax.random.split(key, 8)
        scale_in = 1.0 / np.sqrt(D)
        scale_gate = 1.0 / np.sqrt(D + 1)
        return {'h': jax.random.normal(ks[0], (B, S, D), dtype=jnp.float32), 'gate_w': jax.random.uniform(ks[1], (D + 1, NUM_EXPERTS), minval=-scale_gate, maxval=scale_gate, dtype=jnp.float32), 'gate_b': jnp.zeros((NUM_EXPERTS,), dtype=jnp.float32), 'w1': jax.random.uniform(ks[2], (NUM_EXPERTS, D, D), minval=-scale_in, maxval=scale_in, dtype=jnp.float32), 'b1': jnp.zeros((NUM_EXPERTS, D), dtype=jnp.float32), 'w2': jax.random.uniform(ks[3], (NUM_EXPERTS, D, D), minval=-scale_in, maxval=scale_in, dtype=jnp.float32), 'b2': jnp.zeros((NUM_EXPERTS, D), dtype=jnp.float32)}
    _L0_ffn_all = _L0_ffn_setup()
    _L0_ffn_in = {k: v for k, v in _L0_ffn_all.items() if k in ('gate_w', 'gate_b', 'w1', 'b1', 'w2', 'b2')}
    del _L0_ffn_all
    return {'x': x, 'ctx_4096': ctx_4096, 'mask_SxS2_bk0': mask_SxS2_bk0, 'g_xattn': g_xattn, 'g_ffn': g_ffn, 'L0_xattn_w_q': _L0_xattn_in['w_q'], 'L0_xattn_w_k': _L0_xattn_in['w_k'], 'L0_xattn_w_v': _L0_xattn_in['w_v'], 'L0_xattn_w_out': _L0_xattn_in['w_out'], 'L0_ffn_gate_w': _L0_ffn_in['gate_w'], 'L0_ffn_gate_b': _L0_ffn_in['gate_b'], 'L0_ffn_w1': _L0_ffn_in['w1'], 'L0_ffn_b1': _L0_ffn_in['b1'], 'L0_ffn_w2': _L0_ffn_in['w2'], 'L0_ffn_b2': _L0_ffn_in['b2']}

def reference(x, ctx_4096, mask_SxS2_bk0, g_xattn, g_ffn, L0_xattn_w_q, L0_xattn_w_k, L0_xattn_w_v, L0_xattn_w_out, L0_ffn_gate_w, L0_ffn_gate_b, L0_ffn_w1, L0_ffn_b1, L0_ffn_w2, L0_ffn_b2):
    import jax
    import jax.numpy as jnp

    def _L0_xattn_ref(q, k, v, w_q, w_k, w_v, w_out, mask):
        import jax, jax.numpy as jnp
        import numpy as np
        N_HEAD = 32
        D_MODEL = 512
        N_KV_GROUPS = 8
        D_HEAD = D_MODEL // N_HEAD
        H_PER_G = N_HEAD // N_KV_GROUPS
        KV_DIM = N_KV_GROUPS * D_HEAD
        B, S = (2, 256)
        b, n, _ = q.shape
        s = k.shape[1]
        query = q @ w_q.T
        key = k @ w_k.T
        value = v @ w_v.T
        query = query.reshape(b, n, N_HEAD, D_HEAD).transpose(0, 2, 1, 3)
        query = query.reshape(b, N_KV_GROUPS, H_PER_G, n, D_HEAD)
        key = key.reshape(b, s, N_KV_GROUPS, D_HEAD).transpose(0, 2, 1, 3)
        value = value.reshape(b, s, N_KV_GROUPS, D_HEAD).transpose(0, 2, 1, 3)
        scores = jnp.einsum('bghnd,bgsd->bghns', query, key) / D_HEAD ** 0.5
        scores = jnp.where(mask, scores, jnp.finfo(scores.dtype).min)
        attention = jax.nn.softmax(scores, axis=-1)
        out = jnp.einsum('bghns,bgsd->bghnd', attention, value)
        out = out.transpose(0, 3, 1, 2, 4).reshape(b, n, D_MODEL)
        return out @ w_out.T

    def _L0_ffn_ref(h, gate_w, gate_b, w1, b1, w2, b2):
        import jax, jax.numpy as jnp
        import numpy as np
        B, S, D = (4, 256, 512)
        NUM_EXPERTS, TOP_K = (3, 2)

        def _expert_outputs(h, w1, b1, w2, b2):
            pre = jnp.einsum('bsd,edf->ebsf', h, w1) + b1[:, None, None, :]
            act = jnp.stack([jnp.tanh(pre[0]), jax.nn.gelu(pre[1], approximate=False), jax.nn.silu(pre[2])])
            return jnp.einsum('ebsf,efd->ebsd', act, w2) + b2[:, None, None, :]
        b, s, d = h.shape
        vision_len = int(s * 0.3)
        text_strength = jnp.mean(jnp.abs(h[:, vision_len:, :]), axis=(1, 2), keepdims=True)
        vision_strength = jnp.mean(jnp.abs(h[:, :vision_len, :]), axis=(1, 2), keepdims=True)
        modality_ratio = text_strength / (vision_strength + 1e-08)
        modality_ratio = jnp.broadcast_to(modality_ratio, (b, s, 1))
        router_input = jnp.concatenate([h, modality_ratio], axis=-1)
        gate_logits = router_input @ gate_w + gate_b
        gate_scores = jax.nn.softmax(gate_logits, axis=-1)
        top_val, top_idx = jax.lax.top_k(gate_scores, TOP_K)
        top_val = top_val / (jnp.sum(top_val, axis=-1, keepdims=True) + 1e-08)
        expert_out = _expert_outputs(h, w1, b1, w2, b2)
        moe_out = jnp.zeros_like(h)
        batch_idx = jnp.arange(b)
        for i in range(TOP_K):
            j = top_idx[:, 0, i]
            out_i = expert_out[j, batch_idx]
            moe_out = moe_out + top_val[..., i:i + 1] * out_i
        return moe_out
    x = x + jnp.tanh(g_xattn[0]) * _L0_xattn_ref(_layernorm(x, axis=-1), ctx_4096, ctx_4096, L0_xattn_w_q, L0_xattn_w_k, L0_xattn_w_v, L0_xattn_w_out, mask_SxS2_bk0)
    x = x + jnp.tanh(g_ffn[0]) * _L0_ffn_ref(_layernorm(x, axis=-1), L0_ffn_gate_w, L0_ffn_gate_b, L0_ffn_w1, L0_ffn_b1, L0_ffn_w2, L0_ffn_b2)
    return x

_drawn_inputs = setup_inputs


def setup_inputs(seed=0):
    import zlib

    import numpy as np

    out = dict(_drawn_inputs(seed))
    spreads = {'L0_ffn_gate_b': (0.0, 0.379), 'L0_ffn_b1': (0.0, 0.342), 'L0_ffn_b2': (0.0, 0.296)}
    factors = {'L0_xattn_w_q': 8.0, 'L0_xattn_w_k': 8.0, 'L0_xattn_w_out': 4.989}
    for name, (base, spread) in spreads.items():
        noise = np.random.default_rng([zlib.crc32(name.encode()), seed]).standard_normal(out[name].shape)
        drawn = base * np.exp(spread * noise) if base else spread * noise
        out[name] = jnp.asarray(drawn.astype(out[name].dtype))
    for name, factor in factors.items():
        out[name] = (out[name] * factor).astype(out[name].dtype)
    return out
```

```python
from contextlib import ExitStack

import concourse.bass as bass
from concourse import mybir

ALU = mybir.AluOpType
ACT = mybir.ActivationFunctionType
AX = mybir.AxisListType
F32 = mybir.dt.float32
BF16 = mybir.dt.bfloat16
I32 = mybir.dt.int32
U8 = mybir.dt.uint8

P = 128
WIN = 32
S = P // WIN
LN_EPS = 1e-5
BIG = 1e30

PLAN = (
    [(f"S{b}", b, "this") for b in range(4)]
    + [("hT0", 4, "prev"), ("hT1", 5, "prev"), ("ctxT", 6, "next"), ("gate", 7, "prev"), ("K", 4, "next")]
    + [("up0", 5, "prev"), ("up1", 6, "prev"), ("PT0", 0, "this"), ("PT1", 1, "this"), ("up2", 7, "prev")]
    + [("O0", 0, "this"), ("O1", 1, "this"), ("PT2", 2, "this"), ("PT3", 3, "this"), ("up3", 4, "prev")]
    + [("O2", 2, "this"), ("O3", 3, "this"), ("up4", 5, "prev"), ("up5", 6, "prev"), ("V", 7, "next")]
    + [("xT0", 4, "next"), ("xT1", 5, "next"), ("rank", 6, "prev"), ("dn0", 7, "prev")]
    + [("Q0", 4, "next"), ("Q1", 5, "next"), ("dn1", 6, "prev"), ("dn2", 7, "prev")]
    + [("OT0", 0, "this"), ("OT1", 2, "this"), ("dn3", 4, "prev"), ("dn4", 5, "prev"), ("dn5", 6, "prev")]
    + [("W0", 1, "this"), ("W1", 3, "this")]
)
BANK = {item: bank for item, bank, _ in PLAN}


def flamingo_block(nc, x, ctx_rows, mask, g_attn, g_ffn, wq, wk, wv, wo, gate_w, gate_r, gate_b, w1, b1, w2, b2, out):
    TOK, DM = x.shape
    NBATCH, KEYS, _ = ctx_rows.shape
    NQ = TOK // NBATCH
    U = 2 * NQ
    DUOS = TOK // (2 * U)
    NB = NBATCH // DUOS
    KC = DM // P
    NG, DH, HG = 8, 16, 4
    J = NG // S
    HP = HG // 2
    OC = S * DH + S
    NE = 3
    VIS = int(NQ * 0.3)
    LAST = KEYS - WIN
    assert NB == 4 and S * J == NG and HP * J * P == 512

    def present(duo_kind, D):
        return {"lead": ("next",), "first": ("this", "next"), "mid": ("this", "next", "prev"),
                "last": ("this", "prev"), "tail": ("prev",)}[D].count(duo_kind) > 0

    def in_turn(turn, bank, before=None):
        n = 0
        for item, b, kind in PLAN:
            if item == before:
                break
            n += b == bank and present(kind, turn)
        return n

    class Turn:

        def __init__(self, kind, D):
            self.kind, self.D = kind, D
            self.this, self.next, self.prev = (present(k, kind) for k in ("this", "next", "prev"))

        def before(self, item, bank=None):
            bank = BANK[item] if item else bank
            at = in_turn(self.kind, bank, item) if item else 0
            if self.kind == "lead":
                return at
            at += in_turn("lead", bank)
            if self.kind == "first":
                return at
            at += in_turn("first", bank)
            if self.kind == "mid":
                return (self.D - 1) * in_turn("mid", bank) + at
            at += (DUOS - 2) * in_turn("mid", bank)
            if self.kind == "last":
                return at
            return at + in_turn("last", bank)

    def over_turns(eng, body):
        body(Turn("lead", -1))
        body(Turn("first", 0))
        with eng.Fori(1, DUOS - 1) as D:
            body(Turn("mid", D))
        body(Turn("last", DUOS - 1))
        body(Turn("tail", DUOS))

    WINDOWS = KEYS // WIN
    OVERLAP = (WINDOWS + 1) * WIN - KEYS
    assert 0 < OVERLAP < WIN

    x_v = x.rearrange("(n u p) d -> n p u d", u=2, p=U)
    out_v = out.rearrange("(n u p) d -> n p u d", u=2, p=U)
    ctx_v = ctx_rows.rearrange("(n b) k d -> n b k d", b=NB)

    with ExitStack() as stack:
        def sb(name, shape, dt=F32):
            return stack.enter_context(nc.sbuf_tensor(name, shape, dt))

        def sem(name):
            return stack.enter_context(nc.semaphore(name))

        bank = [stack.enter_context(nc.psum_tensor(f"bank{i}", [P, 512], F32)) for i in range(8)]

        wq_sb = sb("wq_sb", [P, KC, HG, P])
        wk_sb = sb("wk_sb", [P, KC, P])
        wv_sb = sb("wv_sb", [P, KC, P])
        wo_sb = sb("wo_sb", [P, HG, DM])
        w1_sb = sb("w1_sb", [P, NE, KC, DM])
        w2_sb = sb("w2_sb", [P, NE, KC, DM])
        b1_sb = sb("b1_sb", [P, NE, KC])
        b1_half = sb("b1_half", [P, KC])
        b2_sb = sb("b2_sb", [U, NE, DM])
        gw_sb = sb("gw_sb", [P, KC, NE])
        gr_sb = sb("gr_sb", [U, NE])
        gb_sb = sb("gb_sb", [U, NE])
        gains = sb("gains", [U, 2])
        tanh_g = sb("tanh_g", [U, 2])
        ident = sb("ident", [P, P])
        pair_ident = sb("pair_ident", [NQ, U], BF16)
        group_sel = sb("group_sel", [P, NG])
        s_sel = sb("s_sel", [P, S])
        text_sel = sb("text_sel", [U, 2, NQ])
        vision_sel = sb("vision_sel", [U, 2, NQ])
        first_sel = sb("first_sel", [U, 2, NQ])
        minus_half = sb("minus_half", [U, 2])
        eps_col = sb("eps_col", [U, 2])
        early = w1_sb[:].rearrange("p e k n -> p (e k n)")
        key_down = early[0:NQ, 0:KEYS]
        key_up = early[0:NQ, KEYS:2 * KEYS]
        seen_at = early[0:NQ, 2 * KEYS:3 * KEYS]
        mask_sb = sb("mask_sb", [NQ, KEYS], U8)
        ends = sb("ends", [NQ, 3])
        row_any = sb("row_any", [NQ, 1])
        row_any_bf = sb("row_any_bf", [NQ, 1], BF16)
        alive = sb("alive", [U, 1])
        verdict = sb("verdict", [1, 8])
        verdict_i = sb("verdict_i", [1, 2], I32)
        bias_win = sb("bias_win", [NQ, WIN], BF16)
        ctx_sb = sb("ctx_sb", [P, DM])
        ctxT_sb = sb("ctxT_sb", [P, KC, P])
        KB = sb("KB", [P, NB, NG, WIN])
        VB = sb("VB", [P, NB, J, OC])
        x_sb = sb("x_sb", [U, 2, DM])
        ln1_st = sb("ln1_st", [U, 2, 6])
        ln1_mv = sb("ln1_mv", [U, 2, 2])
        ln1_r = sb("ln1_r", [U, 3, 2])
        xn = sb("xn", [U, 2, DM])
        xnT = sb("xnT", [P, 2, KC, U])
        QT = sb("QT", [P, NB, HG, NQ])
        top = sb("top", [U, NB, HP * J * S])
        probs = sb("probs", [U, NB, HP * J * S, WIN])
        PT = sb("PT", [P, NB, HP * J, U])
        O_sb = sb("O_sb", [U, NB, HP * J, OC])
        O_rec = sb("O_rec", [U, NB, HP * J, S])
        On = sb("On", [U, NB, HP * J, S, DH])
        OT = sb("OT", [P, 2, HG, 2, NQ])
        xr = sb("xr", [U, 2, DM])
        x1 = sb("x1", [U, 2, DM])
        ln2_st = sb("ln2_st", [U, 2, 6])
        ln2_mv = sb("ln2_mv", [U, 2, 2])
        ln2_r = sb("ln2_r", [U, 2, 2])
        h = sb("h", [U, 2, DM])
        h_abs = sb("h_abs", [U, 2, DM])
        h_sum = sb("h_sum", [U, 2])
        hT = sb("hT", [P, KC, 2, U])
        act = sb("act", [P, NE, KC, 2 * U])
        silu_t = sb("silu_t", [P, KC, 2 * U])
        silu_u = sb("silu_u", [P, KC, 2 * U])
        gt = sb("gt", [U, 16, 2])
        best = sb("best", [U, 2, 2])
        sc = sb("sc", [U, 2, NE])
        wins = sb("wins", [U, 2, NE])
        rank_hot = sb("rank_hot", [U, 2, 2, NE])
        picked = sb("picked", [U, 2, 2, NE])
        coef2 = sb("coef2", [U, 2, 2, NE])
        coef = sb("coef", [U, 2, NE])
        b2_part = sb("b2_part", [U, 2, DM])
        y = sb("y", [U, 2, DM])
        g_ctx = sb("g_ctx", [P, DM])
        g_ctxT = sb("g_ctxT", [P, KC, P])
        g_KB = sb("g_KB", [P, NB, NG, WIN])
        g_VB = sb("g_VB", [P, NB, J, OC])
        g_bias = sb("g_bias", [NQ, WIN], BF16)
        g_top = sb("g_top", [U, NB, HP * J * S])
        g_new = sb("g_new", [U, HP * J * S])
        g_decay = sb("g_decay", [U, HP * J * S])

        bank_full = [sem(f"bank_full{i}") for i in range(8)]
        bank_free = [sem(f"bank_free{i}") for i in range(8)]
        mask_loaded = sem("mask_loaded")
        wkv_loaded = sem("wkv_loaded")
        wq_loaded = sem("wq_loaded")
        wo_loaded = sem("wo_loaded")
        w1_loaded = sem("w1_loaded")
        w2_loaded = sem("w2_loaded")
        small_loaded = sem("small_loaded")
        setup_pool = sem("setup_pool")
        consts_ready = sem("consts_ready")
        mask_step = sem("mask_step")
        ends_ready = sem("ends_ready")
        ends_turned = sem("ends_turned")
        verdict_ready = sem("verdict_ready")
        alive_ready = sem("alive_ready")
        bias_ready = sem("bias_ready")
        gains_ready = sem("gains_ready")
        ctx_loaded = sem("ctx_loaded")
        ctx_read = sem("ctx_read")
        x_loaded = sem("x_loaded")
        xr_loaded = sem("xr_loaded")
        ln1_stats = sem("ln1_stats")
        ln1_mean = sem("ln1_mean")
        ln1_step = sem("ln1_step")
        ln1_rstd = sem("ln1_rstd")
        xn_ready = sem("xn_ready")
        top_ready = sem("top_ready")
        probs_ready = sem("probs_ready")
        sums_inverted = sem("sums_inverted")
        on_ready = sem("on_ready")
        ln2_stats = sem("ln2_stats")
        ln2_mean = sem("ln2_mean")
        ln2_step = sem("ln2_step")
        ln2_rstd = sem("ln2_rstd")
        h_ready = sem("h_ready")
        h_summed = sem("h_summed")
        gate_step = sem("gate_step")
        logits_ready = sem("logits_ready")
        gate_exp = sem("gate_exp")
        ranks_ready = sem("ranks_ready")
        coef_ready = sem("coef_ready")
        silu_tanh = sem("silu_tanh")
        silu_half = sem("silu_half")
        silu_ready = sem("silu_ready")
        b2_step = sem("b2_step")
        y_based = sem("y_based")
        y_stored = sem("y_stored")
        waits_carried = sem("waits_carried")
        g_loaded = sem("g_loaded")
        g_pe = sem("g_pe")
        g_act = sem("g_act")
        g_dve = sem("g_dve")
        g_cleared = sem("g_cleared")
        g_scaled = sem("g_scaled")

        block = stack.enter_context(nc.Block())

        def full(eng, turn, item):
            eng.wait_ge(bank_full[BANK[item]], turn.before(item) + 1)
            return bank_free[BANK[item]]

        def taken(eng, turn, item):
            eng.wait_ge(bank_free[BANK[item]], turn.before(item) + 1)

        G_PE = 3 + 3 * NB
        G_ACT = 1 + 2 * NB
        G_DVE = 3 + 6 * NB

        def carried(eng):
            eng.sem_inc(waits_carried, 1)

        def general(eng, flag, D, body):
            with eng.If(flag > 0):
                with eng.Fori(0, WINDOWS) as c:
                    body(D * (WINDOWS + 1) + c, c * WIN, False)
                body(D * (WINDOWS + 1) + WINDOWS, LAST, True)

        @block.sync
        def _(sp):
            sp.dma_start(mask_sb[:], mask).then_inc(mask_loaded, 16)
            sp.dma_start(wk_sb[:], wk).then_inc(wkv_loaded, 16)
            sp.dma_start(wv_sb[:], wv).then_inc(wkv_loaded, 16)
            sp.dma_start(wq_sb[:], wq).then_inc(wq_loaded, 16)
            sp.wait_ge(verdict_ready, 1)
            start = sp.value_load(verdict_i[0:1, 0:1], min_val=0, max_val=LAST)
            flag = sp.value_load(verdict_i[0:1, 1:2], min_val=0, max_val=1)

            def body(turn):
                D = turn.D
                if turn.next:
                    N = D + 1
                    if turn.kind != "lead":
                        sp.wait_ge(ctx_read, N)
                        carried(sp)
                        sp.wait_ge(xn_ready, 2 * N)
                        carried(sp)
                    for b in range(NB):
                        sp.dma_start(ctx_sb[WIN * b:WIN * (b + 1), :],
                                     ctx_v[N, b, bass.ds(start, WIN), :]).then_inc(ctx_loaded, 16)
                    sp.dma_start(x_sb[:], x_v[N]).then_inc(x_loaded, 16)
                if turn.kind == "lead":
                    sp.dma_start(wo_sb[:], wo).then_inc(wo_loaded, 16)
                    sp.dma_start(w1_sb[:], w1).then_inc(w1_loaded, 16)
                    sp.dma_start(w2_sb[:], w2).then_inc(w2_loaded, 16)
                if turn.this:
                    if turn.kind != "first":
                        sp.wait_ge(ln2_stats, 2 * D)
                        carried(sp)
                    sp.dma_start(xr[:], x_v[D]).then_inc(xr_loaded, 16)

                    def window(n, first_key, last):
                        sp.wait_ge(g_pe, n * G_PE + 1)
                        carried(sp)
                        for b in range(NB):
                            sp.dma_start(g_ctx[WIN * b:WIN * (b + 1), :],
                                         ctx_v[D, b, bass.ds(first_key, WIN), :]).then_inc(g_loaded, 16)

                    general(sp, flag, D, window)
                if turn.prev:
                    taken(sp, turn, "dn2")
                    carried(sp)
                    taken(sp, turn, "dn5")
                    carried(sp)
                    sp.dma_start(out_v[D - 1], y[:]).then_inc(y_stored, 16)

            sp.sem_inc(y_stored, 1)
            over_turns(sp, body)
            sp.wait_ge(y_stored, 16 * DUOS + 1)

        @block.gpsimd
        def _(pool):
            steps = [0]
            g = nc.gpsimd

            def made(ins):
                steps[0] += 1
                ins.then_inc(setup_pool, 1)
                pool.wait_ge(setup_pool, steps[0])

            def keep(t, op, fill, base, pattern, mult):
                made(g.affine_select(out=t, in_=t, compare_op=op, fill=fill, base=base, pattern=pattern,
                                     channel_multiplier=mult))

            g.iota(key_down, [[-1, KEYS]], base=KEYS, channel_multiplier=0, allow_small_or_imprecise_dtypes=True)
            made(g.iota(key_up, [[1, KEYS]], base=1, channel_multiplier=0, allow_small_or_imprecise_dtypes=True))
            g.memset(ident[:], 0.0)
            made(g.memset(pair_ident[:], 0.0))
            keep(ident[:], ALU.not_equal, 1.0, 0, [[-1, P]], 1)
            keep(pair_ident[:].rearrange("p (a q) -> p a q", a=2), ALU.not_equal, 1.0, 0, [[0, 2], [-1, NQ]], 1)
            for dst, src in ((b1_sb[:], b1), (gw_sb[:], gate_w), (gr_sb[:], gate_r.broadcast_to([U, NE])),
                             (gb_sb[:], gate_b.broadcast_to([U, NE])), (gains[:, 0:1], g_attn.broadcast_to([U, 1])),
                             (gains[:, 1:2], g_ffn.broadcast_to([U, 1])),
                             (b2_sb[:].rearrange("p e d -> p (e d)"), b2.broadcast_to([U, NE * DM]))):
                pool.dma_start(dst, src).then_inc(small_loaded, 16)
            g.memset(group_sel[:], 1.0)
            g.memset(s_sel[:], 1.0)
            g.memset(text_sel[:], 1.0 / ((NQ - VIS) * DM))
            g.memset(vision_sel[:], 1.0 / (VIS * DM))
            g.memset(first_sel[:], 0.0)
            g.memset(minus_half[:], -0.5)
            g.memset(eps_col[:], LN_EPS)
            g.memset(g_VB[:], 0.0)
            made(g.memset(VB[:], 0.0))
            keep(group_sel[:], ALU.is_ge, 0.0, 0, [[-DH, NG]], 1)
            keep(group_sel[:], ALU.is_ge, 0.0, DH - 1, [[DH, NG]], -1)
            keep(s_sel[:], ALU.is_ge, 0.0, 0, [[-WIN, S]], 1)
            keep(s_sel[:], ALU.is_ge, 0.0, WIN - 1, [[WIN, S]], -1)
            keep(text_sel[:], ALU.is_ge, 0.0, -VIS, [[-NQ, 2], [0, NQ]], 1)
            keep(text_sel[:], ALU.is_ge, 0.0, NQ - 1, [[NQ, 2], [0, NQ]], -1)
            keep(vision_sel[:], ALU.is_ge, 0.0, 0, [[-NQ, 2], [0, NQ]], 1)
            keep(vision_sel[:], ALU.is_ge, 0.0, VIS - 1, [[NQ, 2], [0, NQ]], -1)
            keep(first_sel[:], ALU.not_equal, 1.0, 0, [[-NQ, 2], [0, NQ]], 1)
            for values in (g_VB, VB):
                last = g.tensor_copy(values[:, :, :, S * DH:].rearrange("p b j s -> p (b j) s"),
                                     s_sel[:].unsqueeze(1).broadcast_to([P, NB * J, S]))
            last.then_inc(consts_ready, 1)
            pool.wait_ge(alive_ready, 1)

            def body(turn):
                D = turn.D
                if turn.next:
                    N = D + 1
                    pool.wait_ge(ln1_mean, 2 * N + 2)
                    g.tensor_tensor(ln1_r[:, 0, :], ln1_mv[:, :, 1], eps_col[:], ALU.add).then_inc(ln1_step, 1)
                    pool.wait_ge(ln1_step, 2 * N + 1)
                    g.tensor_tensor(ln1_r[:, 1, :], ln1_r[:, 0, :], minus_half[:], ALU.pow).then_inc(ln1_step, 1)
                    pool.wait_ge(ln1_step, 2 * N + 2)
                    g.tensor_tensor(ln1_r[:, 2, :], ln1_r[:, 1, :], alive[:].broadcast_to([U, 2]), ALU.mult).then_inc(ln1_rstd, 1)
                if turn.prev:
                    pool.wait_ge(coef_ready, D)
                    pool.wait_ge(y_stored, 16 * (D - 1) + 1)
                    for u in range(2):
                        for e in range(NE):
                            n = 10 * (D - 1) + 5 * u + 2 * e
                            g.tensor_tensor(b2_part[:, u, :], b2_sb[:, e, :], coef[:, u, e:e + 1].broadcast_to([U, DM]),
                                            ALU.mult).then_inc(b2_step, 1)
                            pool.wait_ge(b2_step, n + 1)
                            last = g.tensor_tensor(y[:, u, :], (x1 if e == 0 else y)[:, u, :], b2_part[:, u, :], ALU.add)
                            if e < NE - 1:
                                last.then_inc(b2_step, 1)
                                pool.wait_ge(b2_step, n + 2)
                        last.then_inc(y_based, 1)
                if turn.this:
                    for u in range(2):
                        pool.wait_ge(sums_inverted, 2 * D + u + 1)
                        for b in (2 * u, 2 * u + 1):
                            last = g.tensor_tensor(On[:, b],
                                                   O_sb[:, b, :, 0:S * DH].rearrange("p t (s d) -> p t s d", s=S),
                                                   O_rec[:, b].unsqueeze(3).broadcast_to([U, HP * J, S, DH]), ALU.mult)
                        last.then_inc(on_ready, 1)
                    for u in range(2):
                        pool.wait_ge(ln2_mean, 2 * D + u + 1)
                        g.tensor_tensor(ln2_r[:, u, 0:1], ln2_mv[:, u, 1:2], eps_col[:, 0:1], ALU.add).then_inc(ln2_step, 1)
                        pool.wait_ge(ln2_step, 2 * D + u + 1)
                        g.tensor_tensor(ln2_r[:, u, 1:2], ln2_r[:, u, 0:1], minus_half[:, 0:1], ALU.pow).then_inc(ln2_rstd, 1)

            over_turns(pool, body)

        @block.scalar
        def _(sca):
            a = nc.scalar
            sca.wait_ge(small_loaded, 16 * 7)
            a.activation(tanh_g[:], gains[:], ACT.Tanh).then_inc(gains_ready, 1)
            a.activation(b1_half[:], b1_sb[:, 2, :], ACT.Copy, scale=0.5).then_inc(gains_ready, 1)
            sca.wait_ge(gains_ready, 2)
            sca.wait_ge(verdict_ready, 1)
            flag = sca.value_load(verdict_i[0:1, 1:2], min_val=0, max_val=1)

            def body(turn):
                D = turn.D

                def exps(b):
                    taken(sca, turn, f"S{b}")
                    a.activation(probs[:, b], probs[:, b], ACT.Exp).then_inc(probs_ready, 1)

                def up(i, func, dst, bias, scale=1.0):
                    full(sca, turn, f"up{i}")
                    for m in range(2):
                        k = 2 * (i % 2) + m
                        ins = a.activation(dst[:, k, :], bank[BANK[f"up{i}"]][:, m * 2 * U:(m + 1) * 2 * U], func,
                                           bias=bias[:, k:k + 1], scale=scale)
                    return ins

                if turn.prev:
                    for u in range(2):
                        free = full(sca, turn, f"hT{u}")
                        a.activation(hT[:, :, u, :], bank[BANK[f"hT{u}"]][:, 0:KC * U].rearrange("p (k t) -> p k t", k=KC),
                                     ACT.Copy).then_inc(free, 1)
                if turn.next:
                    free = full(sca, turn, "ctxT")
                    a.activation(ctxT_sb[:].rearrange("p k n -> p (k n)"), bank[BANK["ctxT"]][:], ACT.Copy).then_inc(free, 1)
                if turn.this:
                    exps(0)
                    exps(1)
                if turn.prev:
                    for i in (0, 1):
                        up(i, ACT.Tanh, act[:, 0], b1_sb[:, 0, :]).then_inc(bank_free[BANK[f"up{i}"]], 1)
                if turn.this:
                    exps(2)
                    exps(3)
                if turn.prev:
                    sca.wait_ge(logits_ready, D)
                    a.activation(sc[:], sc[:], ACT.Exp).then_inc(gate_exp, 1)
                if turn.this:
                    def window(n, first_key, last):
                        sca.wait_ge(g_pe, n * G_PE + 2)
                        a.activation(g_ctxT[:].rearrange("p k n -> p (k n)"), bank[0][:], ACT.Copy).then_inc(g_act, 1)
                        for b in range(NB):
                            sca.wait_ge(g_dve, n * G_DVE + 3 + 6 * b + 5)
                            a.activation(g_decay[:], g_decay[:], ACT.Exp).then_inc(g_act, 1)
                            a.activation(probs[:, b], probs[:, b], ACT.Exp).then_inc(g_act, 1)

                    general(sca, flag, D, window)
                if turn.prev:
                    for i in (2, 3):
                        up(i, ACT.Gelu, act[:, 1], b1_sb[:, 1, :]).then_inc(bank_free[BANK[f"up{i}"]], 1)
                    for i in (4, 5):
                        up(i, ACT.Tanh, silu_t, b1_half, scale=0.5).then_inc(silu_tanh, 1)
                if turn.next:
                    for u in range(2):
                        free = full(sca, turn, f"xT{u}")
                        a.activation(xnT[:, u].rearrange("p k t -> p (k t)"), bank[BANK[f"xT{u}"]][:, 0:KC * U],
                                     ACT.Copy).then_inc(free, 1)
                    for u in range(2):
                        free = full(sca, turn, f"Q{u}")
                        a.activation(QT[:, 2 * u:2 * u + 2].rearrange("p b c q -> p c b q"),
                                     bank[BANK[f"Q{u}"]][:, 0:HG * U].rearrange("p (c b q) -> p c b q", c=HG, b=2),
                                     ACT.Copy, scale=DH ** -0.5).then_inc(free, 1)
                if turn.this:
                    for u in range(2):
                        free = full(sca, turn, f"OT{u}")
                        for b in range(2):
                            last = a.activation(OT[:, u, :, b, :],
                                                bank[BANK[f"OT{u}"]][:, b * HG * NQ:(b + 1) * HG * NQ].rearrange("p (c q) -> p c q", c=HG),
                                                ACT.Copy)
                        last.then_inc(free, 1)
                    for u in range(2):
                        sca.wait_ge(h_ready, 2 * D + u + 1)
                        a.activation(h_abs[:, u, :], h[:, u, :], ACT.Abs, accum_out=h_sum[:, u:u + 1]).then_inc(h_summed, 1)

            over_turns(sca, body)

        @block.vector
        def _(dve):
            v = nc.vector
            dve.sem_inc(g_dve, 1)
            steps = [0]

            def step(ins):
                steps[0] += 1
                ins.then_inc(mask_step, 1)
                dve.wait_ge(mask_step, steps[0])

            dve.wait_ge(mask_loaded, 16)
            dve.wait_ge(setup_pool, 1)
            step(v.tensor_tensor(seen_at, mask_sb[:], key_down, ALU.mult))
            step(v.tensor_reduce(ends[:, 0:1], seen_at, AX.X, ALU.max))
            step(v.tensor_tensor(seen_at, mask_sb[:], key_up, ALU.mult))
            step(v.tensor_reduce(ends[:, 1:2], seen_at, AX.X, ALU.max))
            step(v.tensor_scalar(row_any[:], ends[:, 1:2], 0.0, None, ALU.is_gt))
            v.tensor_copy(row_any_bf[:], row_any[:])
            v.tensor_scalar(ends[:, 2:3], row_any[:], -1.0, None, ALU.mult)
            v.memset(verdict[:], 0.0).then_inc(ends_ready, 1)
            dve.wait_ge(ends_turned, 1)
            step(v.tensor_reduce(verdict[:, 0:3], bank[0][0:1, 0:3 * NQ].rearrange("p (e q) -> p e q", e=3), AX.X, ALU.max))
            step(v.tensor_scalar(verdict[:, 3:4], verdict[:, 0:1], -1.0, float(KEYS), ALU.mult, ALU.add))
            step(v.tensor_scalar(verdict[:, 4:5], verdict[:, 3:4], float(LAST), None, ALU.min))
            step(v.tensor_tensor(verdict[:, 5:6], verdict[:, 0:1], verdict[:, 1:2], ALU.add))
            step(v.tensor_scalar(verdict[:, 5:6], verdict[:, 5:6], float(-KEYS - WIN), None, ALU.add))
            step(v.tensor_scalar(verdict[:, 6:7], verdict[:, 2:3], 1.0, None, ALU.add))
            step(v.tensor_tensor(verdict[:, 5:6], verdict[:, 5:6], verdict[:, 6:7], ALU.max))
            step(v.tensor_scalar(verdict[:, 5:6], verdict[:, 5:6], 0.0, None, ALU.is_gt))
            v.tensor_copy(verdict_i[:, 0:1], verdict[:, 4:5])
            v.tensor_copy(verdict_i[:, 1:2], verdict[:, 5:6]).then_inc(verdict_ready, 1)
            v.tensor_copy(alive[:], bank[0][0:U, 4 * NQ:4 * NQ + 1]).then_inc(alive_ready, 1)
            dve.wait_ge(verdict_ready, 1)
            start = dve.value_load(verdict_i[0:1, 0:1], min_val=0, max_val=LAST)
            flag = dve.value_load(verdict_i[0:1, 1:2], min_val=0, max_val=1)

            def take_bias(dst, first_key):
                return v.tensor_scalar(dst[:], mask_sb[:, bass.ds(first_key, WIN)], row_any[:, 0:1], BIG,
                                       ALU.subtract, ALU.mult)

            take_bias(bias_win, start).then_inc(bias_ready, 1)
            dve.wait_ge(gains_ready, 2)
            dve.wait_ge(consts_ready, 1)

            def norm_stats(u, src, st, mv, stats, mean, n):
                v.bn_stats(st[:, u, :], src[:, u, :]).then_inc(stats, 1)
                dve.wait_ge(stats, n)
                carried(dve)
                v.bn_aggr(mv[:, u, :], st[:, u, :]).then_inc(mean, 1)

            def spread_keys(dst, src):
                return v.tensor_tensor(dst[:], src[:, 0:P].rearrange("p (b k) -> p b k", b=NB).unsqueeze(2)
                                       .broadcast_to([P, NB, NG, WIN]),
                                       group_sel[:].unsqueeze(1).unsqueeze(3).broadcast_to([P, NB, NG, WIN]), ALU.mult)

            def spread_values(dst, src):
                src = src[:, 0:P].rearrange("p (j s d) -> p j s d", j=J, s=S)
                for b in range(NB):
                    for s in range(S):
                        last = v.tensor_copy(dst[WIN * s:WIN * (s + 1), b, :, DH * s:DH * (s + 1)],
                                             src[WIN * b:WIN * (b + 1), :, s, :])
                return last

            def body(turn):
                D = turn.D

                def scores(b):
                    src = bank[b][0:U, :].rearrange("p (t k) -> p t k", k=WIN)
                    free = full(dve, turn, f"S{b}")
                    v.tensor_reduce(top[:, b, :], src, AX.X, ALU.max).then_inc(top_ready, 1)
                    dve.wait_ge(top_ready, NB * D + b + 1)
                    v.tensor_tensor(probs[:, b], src, top[:, b, :].unsqueeze(2).broadcast_to([U, HP * J * S, WIN]),
                                    ALU.subtract).then_inc(free, 1)

                def take_probs(b):
                    free = full(dve, turn, f"PT{b}")
                    v.tensor_copy(PT[:, b].rearrange("p t q -> p (t q)"), bank[b][:, 0:HP * J * U]).then_inc(free, 1)

                def take_output(b):
                    free = full(dve, turn, f"O{b}")
                    v.tensor_copy(O_sb[:, b].rearrange("p t c -> p (t c)"), bank[b][0:U, 0:HP * J * OC]).then_inc(free, 1)

                def down(i):
                    u, e = divmod(i, NE)
                    free = full(dve, turn, f"dn{i}")
                    if e == 0:
                        dve.wait_ge(y_based, 2 * (D - 1) + u + 1)
                    else:
                        taken(dve, turn, f"dn{i - 1}")
                    v.scalar_tensor_tensor(y[:, u, :], bank[BANK[f"dn{i}"]][0:U, :], coef[:, u, e:e + 1], y[:, u, :],
                                           ALU.mult, ALU.add).then_inc(free, 1)

                gate_steps = [0]

                def gstep(ins):
                    gate_steps[0] += 1
                    ins.then_inc(gate_step, 1)
                    dve.wait_ge(gate_step, GATE_STEPS * (D - 1) + gate_steps[0])

                if turn.this:
                    for b in range(NB):
                        scores(b)
                if turn.prev:
                    free = full(dve, turn, "gate")
                    src = bank[BANK["gate"]]
                    gstep(v.tensor_scalar(gt[:, 0, :], src[0:U, 10:12], 1e-8, None, ALU.add))
                    gstep(v.reciprocal(gt[:, 1, :], gt[:, 0, :]))
                    gstep(v.tensor_tensor(gt[:, 2, :], src[0:U, 8:10], gt[:, 1, :], ALU.mult))
                    gstep(v.tensor_tensor(sc[:], gt[:, 2, :].unsqueeze(2).broadcast_to([U, 2, NE]),
                                          gr_sb[:].unsqueeze(1).broadcast_to([U, 2, NE]), ALU.mult))
                    v.tensor_tensor(sc[:], sc[:], src[0:U, 0:2 * NE].rearrange("p (u e) -> p u e", u=2),
                                    ALU.add).then_inc(free, 1)
                    taken(dve, turn, "gate")
                    gstep(v.tensor_tensor(sc[:], sc[:], gb_sb[:].unsqueeze(1).broadcast_to([U, 2, NE]), ALU.add))
                    gstep(v.tensor_reduce(gt[:, 3, :], sc[:], AX.X, ALU.max))
                    v.tensor_tensor(sc[:], sc[:], gt[:, 3, :].unsqueeze(2).broadcast_to([U, 2, NE]),
                                    ALU.subtract).then_inc(logits_ready, 1)
                if turn.next:
                    N = D + 1
                    free = full(dve, turn, "K")
                    spread_keys(KB, bank[BANK["K"]]).then_inc(free, 1)
                    dve.wait_ge(x_loaded, 16 * (N + 1))
                    for u in range(2):
                        norm_stats(u, x_sb, ln1_st, ln1_mv, ln1_stats, ln1_mean, 2 * N + u + 1)
                if turn.this:
                    take_probs(0)
                    take_probs(1)
                    take_output(0)
                    take_output(1)
                    take_probs(2)
                    take_probs(3)
                if turn.next:
                    dve.wait_ge(ln1_rstd, N + 1)
                    for u in range(2):
                        v.tensor_scalar(xn[:, u, :], x_sb[:, u, :], ln1_mv[:, u, 0:1], ln1_r[:, 2, u:u + 1],
                                        ALU.subtract, ALU.mult).then_inc(xn_ready, 1)
                if turn.this:
                    take_output(2)
                    take_output(3)
                    taken(dve, turn, "O2")
                    taken(dve, turn, "O3")
                    carried(dve)

                    def window(n, first_key, last):
                        k = [0]

                        def gdo(ins, wait=True):
                            k[0] += 1
                            ins.then_inc(g_dve, 1)
                            if wait:
                                dve.wait_ge(g_dve, n * G_DVE + k[0] + 1)

                        if last:
                            take_bias(g_bias, first_key).then_inc(bias_ready, 1)
                            dve.wait_ge(bias_ready, D + 2)
                            gdo(v.memset(g_bias[:, 0:OVERLAP], -BIG))
                        else:
                            gdo(take_bias(g_bias, first_key))
                        dve.wait_ge(g_pe, n * G_PE + 3)
                        gdo(spread_keys(g_KB, bank[1]))
                        dve.wait_ge(g_pe, n * G_PE + 4)
                        gdo(spread_values(g_VB, bank[2]))
                        for b in range(NB):
                            src = bank[3][0:U, :].rearrange("p (t k) -> p t k", k=WIN)
                            dve.wait_ge(g_pe, n * G_PE + 4 + 3 * b + 1)
                            gdo(v.tensor_reduce(g_new[:], src, AX.X, ALU.max))
                            gdo(v.tensor_tensor(g_new[:], g_new[:], g_top[:, b, :], ALU.max))
                            gdo(v.tensor_tensor(g_decay[:], g_top[:, b, :], g_new[:], ALU.subtract))
                            v.tensor_copy(g_top[:, b, :], g_new[:])
                            gdo(v.tensor_tensor(probs[:, b], src, g_new[:].unsqueeze(2).broadcast_to([U, HP * J * S, WIN]),
                                                ALU.subtract))
                            dve.wait_ge(g_pe, n * G_PE + 4 + 3 * b + 2)
                            gdo(v.tensor_copy(PT[:, b].rearrange("p t q -> p (t q)"), bank[0][:, 0:HP * J * U]))
                            dve.wait_ge(g_act, n * G_ACT + 1 + 2 * b + 1)
                            for t in range(HP * J):
                                v.tensor_tensor(O_sb[:, b, t, 0:S * DH].rearrange("p (s d) -> p s d", s=S),
                                                O_sb[:, b, t, 0:S * DH].rearrange("p (s d) -> p s d", s=S),
                                                g_decay[:, S * t:S * (t + 1)].unsqueeze(2).broadcast_to([U, S, DH]), ALU.mult)
                            v.tensor_tensor(O_sb[:, b, :, S * DH:], O_sb[:, b, :, S * DH:],
                                            g_decay[:].rearrange("p (t s) -> p t s", s=S), ALU.mult).then_inc(g_scaled, 1)
                            dve.wait_ge(g_scaled, n * NB + b + 1)
                            dve.wait_ge(g_pe, n * G_PE + 4 + 3 * b + 3)
                            gdo(v.tensor_tensor(O_sb[:, b].rearrange("p t c -> p (t c)"), O_sb[:, b].rearrange("p t c -> p (t c)"),
                                                bank[1][0:U, 0:HP * J * OC], ALU.add))
                        carried(dve)
                        assert k[0] == G_DVE

                    with dve.If(flag > 0):
                        v.memset(g_top[:], -3e38)
                        v.memset(O_sb[:], 0.0).then_inc(g_cleared, 1)
                        dve.wait_ge(g_cleared, D + 1)
                        carried(dve)
                        with dve.Fori(0, WINDOWS) as c:
                            window(D * (WINDOWS + 1) + c, c * WIN, False)
                        window(D * (WINDOWS + 1) + WINDOWS, LAST, True)
                    for u in range(2):
                        v.reciprocal(O_rec[:, 2 * u:2 * u + 2].rearrange("p b t s -> p (b t) s"),
                                     O_sb[:, 2 * u:2 * u + 2, :, S * DH:].rearrange("p b t s -> p (b t) s")).then_inc(sums_inverted, 1)
                if turn.prev:
                    dve.wait_ge(gate_exp, D)
                    gstep(v.tensor_reduce(gt[:, 4, :], sc[:], AX.X, ALU.add))
                    gstep(v.reciprocal(gt[:, 5, :], gt[:, 4, :]))
                    gstep(v.tensor_tensor(sc[:], sc[:], gt[:, 5, :].unsqueeze(2).broadcast_to([U, 2, NE]), ALU.mult))
                    v.tensor_tensor(gt[:, 6, :], sc[:, :, 0], sc[:, :, 1], ALU.is_ge)
                    v.tensor_tensor(gt[:, 7, :], sc[:, :, 1], sc[:, :, 2], ALU.is_ge)
                    gstep(v.tensor_tensor(gt[:, 8, :], sc[:, :, 0], sc[:, :, 2], ALU.is_ge))
                    v.tensor_tensor(wins[:, :, 0], gt[:, 6, :], gt[:, 8, :], ALU.add)
                    v.tensor_tensor(wins[:, :, 1], gt[:, 7, :], gt[:, 6, :], ALU.subtract)
                    gstep(v.tensor_tensor(wins[:, :, 2], gt[:, 7, :], gt[:, 8, :], ALU.add))
                    v.tensor_scalar(wins[:, :, 1], wins[:, :, 1], 1.0, None, ALU.add)
                    gstep(v.tensor_scalar(wins[:, :, 2], wins[:, :, 2], -1.0, 2.0, ALU.mult, ALU.add))
                    v.tensor_scalar(rank_hot[:, :, 0, :], wins[:], 2.0, None, ALU.is_equal)
                    v.tensor_scalar(rank_hot[:, :, 1, :], wins[:], 1.0, None, ALU.is_equal).then_inc(ranks_ready, 1)
                    dve.wait_ge(ranks_ready, D)
                    gstep(v.tensor_tensor(picked[:], rank_hot[:], sc[:].unsqueeze(2).broadcast_to([U, 2, 2, NE]), ALU.mult))
                    gstep(v.tensor_reduce(best[:], picked[:], AX.X, ALU.add))
                    gstep(v.tensor_tensor(gt[:, 11, :], best[:, :, 0], best[:, :, 1], ALU.add))
                    gstep(v.tensor_scalar(gt[:, 11, :], gt[:, 11, :], 1e-8, None, ALU.add))
                    gstep(v.reciprocal(gt[:, 12, :], gt[:, 11, :]))
                    gstep(v.tensor_scalar(gt[:, 12, :], gt[:, 12, :], tanh_g[:, 1:2], None, ALU.mult))
                    gstep(v.tensor_tensor(best[:], best[:], gt[:, 12, :].unsqueeze(2).broadcast_to([U, 2, 2]), ALU.mult))
                    for i in (4, 5):
                        dve.wait_ge(silu_tanh, 2 * (D - 1) + i - 3)
                        for m in range(2):
                            k = 2 * (i - 4) + m
                            ins = v.tensor_scalar(silu_u[:, k, :], bank[BANK[f"up{i}"]][:, m * 2 * U:(m + 1) * 2 * U], 0.5,
                                                  b1_half[:, k:k + 1], ALU.mult, ALU.add)
                        ins.then_inc(bank_free[BANK[f"up{i}"]], 1)
                        taken(dve, turn, f"up{i}")
                        k = 2 * (i - 4)
                        v.scalar_tensor_tensor(act[:, 2, k:k + 2, :], silu_t[:, k:k + 2, :], 1.0, silu_u[:, k:k + 2, :],
                                               ALU.add, ALU.mult).then_inc(silu_ready, 1)
                if turn.next:
                    free = full(dve, turn, "V")
                    spread_values(VB, bank[BANK["V"]]).then_inc(free, 1)
                if turn.prev:
                    free = full(dve, turn, "rank")
                    v.tensor_tensor(coef2[:], bank[BANK["rank"]][0:U, 0:4 * NE].rearrange("p (u r e) -> p u r e", u=2, r=2),
                                    best[:].unsqueeze(3).broadcast_to([U, 2, 2, NE]), ALU.mult).then_inc(free, 1)
                    taken(dve, turn, "rank")
                    v.tensor_tensor(coef[:], coef2[:, :, 0, :], coef2[:, :, 1, :], ALU.add).then_inc(coef_ready, 1)
                    dve.wait_ge(coef_ready, D)
                    for i in range(2 * NE):
                        down(i)
                if turn.this:
                    dve.wait_ge(xr_loaded, 16 * (D + 1))
                    for u in range(2):
                        free = full(dve, turn, f"W{u}")
                        v.scalar_tensor_tensor(x1[:, u, :], bank[BANK[f"W{u}"]][0:U, :], tanh_g[:, 0:1], xr[:, u, :],
                                               ALU.mult, ALU.add).then_inc(free, 1)
                        taken(dve, turn, f"W{u}")
                        norm_stats(u, x1, ln2_st, ln2_mv, ln2_stats, ln2_mean, 2 * D + u + 1)
                    for u in range(2):
                        dve.wait_ge(ln2_rstd, 2 * D + u + 1)
                        v.tensor_scalar(h[:, u, :], x1[:, u, :], ln2_mv[:, u, 0:1], ln2_r[:, u, 1:2],
                                        ALU.subtract, ALU.mult).then_inc(h_ready, 1)
                assert gate_steps[0] == GATE_STEPS * turn.prev

            GATE_STEPS = 19
            over_turns(dve, body)

        @block.tensor
        def _(pe):
            t = nc.tensor
            pe.sem_inc(g_pe, 1)
            pe.wait_ge(setup_pool, 4)
            pe.wait_ge(ends_ready, 1)
            for e in range(3):
                t.transpose(bank[0][0:1, e * NQ:(e + 1) * NQ], ends[:, e:e + 1], ident[0:NQ, 0:NQ])
            t.matmul(bank[0][0:U, 4 * NQ:4 * NQ + 1], pair_ident[:], row_any_bf[:], start=True, stop=True).then_inc(ends_turned, 1)
            pe.wait_ge(verdict_ready, 1)
            flag = pe.value_load(verdict_i[0:1, 1:2], min_val=0, max_val=1)
            pe.wait_ge(alive_ready, 1)
            pe.wait_ge(consts_ready, 1)
            pe.wait_ge(bias_ready, 1)
            pe.wait_ge(wkv_loaded, 32)
            pe.wait_ge(wq_loaded, 16)
            pe.wait_ge(small_loaded, 16 * 7)

            def transposes(dst, src, rows):
                for k in range(KC):
                    last = t.transpose(dst[:, k * rows:(k + 1) * rows], src[:, k * P:(k + 1) * P], ident[0:rows, 0:rows])
                return last

            def chain(dst, pairs):
                for i, (left, right) in enumerate(pairs):
                    last = t.matmul(dst, left, right, start=i == 0, stop=i == len(pairs) - 1)
                return last

            def score_item(dst, bias, keys, b):
                t.matmul(dst[0:U, :].rearrange("p (t k) -> p t k", k=WIN), pair_ident[:],
                         bias[:].unsqueeze(1).broadcast_to([NQ, HP * J * S, WIN]), start=True, stop=False,
                         skip_group_check=True)
                for hp in range(HP):
                    for j in range(J):
                        c = (hp * J + j) * P
                        last = t.matmul(dst[0:U, c:c + P], QT[:, b, 2 * hp:2 * hp + 2, :].rearrange("p c q -> p (c q)"),
                                        keys[:, b, S * j:S * (j + 1), :], start=False, stop=True, skip_group_check=True)
                return last

            def probs_item(dst, b):
                for i in range(HP * J):
                    last = t.transpose(dst[:, i * U:(i + 1) * U],
                                       probs[:, b, S * i:S * (i + 1), :].rearrange("p s k -> p (s k)"), ident[0:U, 0:U])
                return last

            def output_item(dst, values, b):
                for i in range(HP * J):
                    last = t.matmul(dst[0:U, i * OC:(i + 1) * OC], PT[:, b, i, :], values[:, b, i % J, :], start=True, stop=True)
                return last

            def key_item(dst, turned, context_read=None):
                for k in range(KC):
                    last = t.matmul(dst[:, 0:P], wk_sb[:, k, :], turned[:, k, :], start=k == 0, stop=k == KC - 1)
                    if k == 0 and context_read is not None:
                        last.then_inc(context_read, 1)
                return last

            def value_item(dst, turned):
                return chain(dst[:, 0:P], [(turned[:, k, :], wv_sb[:, k, :]) for k in range(KC)])

            def body(turn):
                D = turn.D

                def item(name):
                    at = turn.before(name)
                    if not (isinstance(at, int) and at == 0):
                        pe.wait_ge(bank_free[BANK[name]], at)
                    return bank[BANK[name]]

                def done(name, ins):
                    ins.then_inc(bank_full[BANK[name]], 1)

                def do_scores(b):
                    done(f"S{b}", score_item(item(f"S{b}"), bias_win, KB, b))

                def do_probs(b):
                    dst = item(f"PT{b}")
                    pe.wait_ge(probs_ready, NB * D + b + 1)
                    done(f"PT{b}", probs_item(dst, b))

                def do_output(b):
                    done(f"O{b}", output_item(item(f"O{b}"), VB, b))

                def do_up(i):
                    dst = item(f"up{i}")
                    e, half = divmod(i, 2)
                    for m in range(2):
                        k0 = 2 * half + m
                        last = chain(dst[:, m * 2 * U:(m + 1) * 2 * U],
                                     [(w1_sb[:, e, k, k0 * P:(k0 + 1) * P], hT[:, k, :, :].rearrange("p u t -> p (u t)"))
                                      for k in range(KC)])
                    done(f"up{i}", last)

                def do_down(i):
                    u, e = divmod(i, NE)
                    dst = item(f"dn{i}")
                    if i == NE - 1:
                        pe.wait_ge(silu_ready, 2 * D)
                    done(f"dn{i}", chain(dst[0:U, :], [(act[:, e, k, u * U:(u + 1) * U], w2_sb[:, e, k, :]) for k in range(KC)]))

                if turn.this:
                    for i in (4, 5, 7):
                        pe.wait_ge(bank_free[i], turn.before(None, i))
                    for b in range(NB):
                        do_scores(b)
                if turn.prev:
                    for u in range(2):
                        dst = item(f"hT{u}")
                        pe.wait_ge(h_ready, 2 * (D - 1) + u + 1)
                        done(f"hT{u}", transposes(dst, h[:, u, :], U))
                if turn.next:
                    N = D + 1
                    dst = item("ctxT")
                    pe.wait_ge(ctx_loaded, 16 * NB * (N + 1))
                    done("ctxT", transposes(dst, ctx_sb, P))
                if turn.prev:
                    dst = item("gate")
                    taken(pe, turn, "hT0")
                    taken(pe, turn, "hT1")
                    pe.wait_ge(h_summed, 2 * D)
                    for u in range(2):
                        chain(dst[0:U, u * NE:(u + 1) * NE], [(hT[:, k, u, :], gw_sb[:, k, :]) for k in range(KC)])
                    t.matmul(dst[0:U, 8:10], text_sel[:].rearrange("p a q -> p (a q)"), h_sum[:], start=True, stop=True)
                    done("gate", t.matmul(dst[0:U, 10:12], vision_sel[:].rearrange("p a q -> p (a q)"), h_sum[:],
                                          start=True, stop=True))
                if turn.next:
                    dst = item("K")
                    taken(pe, turn, "ctxT")
                    done("K", key_item(dst, ctxT_sb, ctx_read))
                if turn.prev:
                    pe.wait_ge(w1_loaded, 16)
                    do_up(0)
                    do_up(1)
                if turn.this:
                    do_probs(0)
                    do_probs(1)
                if turn.prev:
                    do_up(2)
                if turn.this:
                    do_output(0)
                    do_output(1)
                    do_probs(2)
                    do_probs(3)
                if turn.prev:
                    do_up(3)
                if turn.this:
                    do_output(2)
                    do_output(3)

                    def window(n, first_key, last):
                        pe.wait_ge(g_loaded, 16 * NB * (n + 1))
                        pe.wait_ge(g_dve, n * G_DVE + 1)
                        transposes(bank[0], g_ctx, P).then_inc(g_pe, 1)
                        pe.wait_ge(g_act, n * G_ACT + 1)
                        key_item(bank[1], g_ctxT).then_inc(g_pe, 1)
                        value_item(bank[2], g_ctxT).then_inc(g_pe, 1)
                        pe.wait_ge(g_dve, n * G_DVE + 3)
                        for b in range(NB):
                            score_item(bank[3], g_bias, g_KB, b).then_inc(g_pe, 1)
                            pe.wait_ge(g_act, n * G_ACT + 1 + 2 * b + 2)
                            probs_item(bank[0], b).then_inc(g_pe, 1)
                            pe.wait_ge(g_dve, n * G_DVE + 4 + 6 * b + 5)
                            output_item(bank[1], g_VB, b).then_inc(g_pe, 1)

                    with pe.If(flag > 0):
                        for b in range(NB):
                            taken(pe, turn, f"O{b}")
                        carried(pe)
                        with pe.Fori(0, WINDOWS) as c:
                            window(D * (WINDOWS + 1) + c, c * WIN, False)
                        window(D * (WINDOWS + 1) + WINDOWS, LAST, True)
                if turn.prev:
                    do_up(4)
                    do_up(5)
                if turn.next:
                    dst = item("V")
                    taken(pe, turn, "ctxT")
                    done("V", value_item(dst, ctxT_sb))
                    for u in range(2):
                        dst = item(f"xT{u}")
                        pe.wait_ge(xn_ready, 2 * N + u + 1)
                        done(f"xT{u}", transposes(dst, xn[:, u, :], U))
                if turn.prev:
                    dst = item("rank")
                    pe.wait_ge(ranks_ready, D)
                    done("rank", t.matmul(dst[0:U, 0:4 * NE], first_sel[:].rearrange("p a q -> p (a q)"),
                                          rank_hot[:].rearrange("p u r e -> p (u r e)"), start=True, stop=True))
                    taken(pe, turn, "up0")
                    taken(pe, turn, "up1")
                    pe.wait_ge(w2_loaded, 16)
                    do_down(0)
                if turn.next:
                    for u in range(2):
                        dst = item(f"Q{u}")
                        taken(pe, turn, f"xT{u}")
                        for c in range(HG):
                            last = chain(dst[:, c * U:(c + 1) * U], [(wq_sb[:, k, c, :], xnT[:, u, k, :]) for k in range(KC)])
                        done(f"Q{u}", last)
                if turn.prev:
                    taken(pe, turn, "up2")
                    taken(pe, turn, "up3")
                    do_down(1)
                    do_down(2)
                if turn.this:
                    for u in range(2):
                        dst = item(f"OT{u}")
                        pe.wait_ge(on_ready, 2 * D + u + 1)
                        for b in range(2):
                            for hp in range(HP):
                                c = (b * HP + hp) * U
                                last = t.transpose(dst[:, c:c + U],
                                                   On[:, 2 * u + b, J * hp:J * (hp + 1)].rearrange("p t s d -> p (t s d)"),
                                                   ident[0:U, 0:U])
                        done(f"OT{u}", last)
                if turn.prev:
                    for i in range(3, 6):
                        do_down(i)
                if turn.this:
                    if turn.kind == "first":
                        pe.wait_ge(wo_loaded, 16)
                    for u in range(2):
                        dst = item(f"W{u}")
                        taken(pe, turn, f"OT{u}")
                        done(f"W{u}", chain(dst[0:U, :], [(OT[:, u, c].rearrange("p b q -> p (b q)"), wo_sb[:, c, :])
                                                          for c in range(HG)]))

            over_turns(pe, body)


def kernel(**inputs):
    import numpy as np
    import concourse.bacc as bacc
    from concourse import mybir as mb
    from concourse.bass_utils import run_bass_kernel_spmd as run

    f = {n: np.asarray(a) for n, a in inputs.items()}
    x = f["x"]
    B, NQ, DM = x.shape
    NG, HG, DH = 8, 4, 16
    KC = DM // P

    def rows(a):
        return a.reshape(-1, P, a.shape[-1]).transpose(1, 0, 2)

    arrays = {
        "x": x.reshape(B * NQ, DM),
        "ctx_rows": f["ctx_4096"],
        "mask": f["mask_SxS2_bk0"],
        "g_attn": f["g_xattn"].reshape(1, 1),
        "g_ffn": f["g_ffn"].reshape(1, 1),
        "wq": rows(f["L0_xattn_w_q"].reshape(NG, HG, DH, DM).transpose(3, 1, 0, 2).reshape(DM, DM)).reshape(P, KC, HG, P),
        "wk": rows(f["L0_xattn_w_k"].T),
        "wv": rows(f["L0_xattn_w_v"].T),
        "wo": f["L0_xattn_w_out"].reshape(DM, NG, HG, DH).transpose(1, 3, 2, 0).reshape(P, HG, DM),
        "gate_w": rows(f["L0_ffn_gate_w"][:DM]),
        "gate_r": f["L0_ffn_gate_w"][DM:],
        "gate_b": f["L0_ffn_gate_b"].reshape(1, -1),
        "w1": f["L0_ffn_w1"].reshape(3, KC, P, DM).transpose(2, 0, 1, 3),
        "b1": f["L0_ffn_b1"].reshape(3, KC, P).transpose(2, 0, 1),
        "w2": f["L0_ffn_w2"].reshape(3, KC, P, DM).transpose(2, 0, 1, 3),
        "b2": f["L0_ffn_b2"].reshape(1, -1),
    }
    arrays = {n: np.ascontiguousarray(a) for n, a in arrays.items()}
    nc = bacc.Bacc("TRN2", target_bir_lowering=False, num_devices=1)
    args = [nc.dram_tensor(n, a.shape, mb.dt.from_np(a.dtype), kind="ExternalInput").ap() for n, a in arrays.items()]
    args.append(nc.dram_tensor("out", (B * NQ, DM), mb.dt.float32, kind="ExternalOutput").ap())
    flamingo_block(nc, *args)
    r = run(nc, [arrays], core_ids=[0])
    return r.results[0]["out"].reshape(B, NQ, DM)
```

```python
from contextlib import ExitStack

import concourse.bass as bass
from concourse import mybir

ALU = mybir.AluOpType
ACT = mybir.ActivationFunctionType
AX = mybir.AxisListType
F32 = mybir.dt.float32
BF16 = mybir.dt.bfloat16
I32 = mybir.dt.int32
U8 = mybir.dt.uint8
F16 = mybir.dt.float16
U32 = mybir.dt.uint32

P = 128
WIN = 32
S = P // WIN
LN_EPS = 1e-5
BIG = 1e30

LN_SCALE = 1024.0
TOP_SCALE = 2.0 ** 14
EXPONENT = 0x7F800000
TINY = 1e-30

PLAN = (
    [("ctxT", 6, "next"), ("S0", 0, "this"), ("S1", 1, "this"), ("hT0", 4, "prev"), ("hT1", 5, "prev")]
    + [("S2", 2, "this"), ("S3", 3, "this"), ("K", 7, "next"), ("norms_up", 4, "prep"), ("gate", 6, "prev"), ("up0", 4, "prev"), ("up1", 5, "prev")]
    + [("PT0", 0, "this"), ("PT1", 1, "this"), ("up2", 7, "prev"), ("O0", 0, "this"), ("O1", 1, "this")]
    + [("PT2", 2, "this"), ("PT3", 3, "this"), ("up3", 6, "prev"), ("O2", 2, "this"), ("O3", 3, "this")]
    + [("xT0", 0, "next"), ("xT1", 1, "next"), ("V", 4, "next")]
    + [("up4", 5, "prev"), ("up5", 7, "prev"), ("Q0", 3, "next"), ("Q1", 6, "next"), ("rank", 2, "prev")]
    + [("dn0", 4, "prev"), ("dn1", 2, "prev"), ("dn2", 5, "prev"), ("OT0", 0, "this"), ("OT1", 1, "this")]
    + [("dn3", 7, "prev"), ("dn4", 4, "prev"), ("W0", 2, "this"), ("W1", 3, "this"), ("dn5", 5, "prev")]
    + [("norms_down", 6, "prep")]
)
LEAD_PLAN = (
    [("norms_q", 2, "next"), ("xT0", 0, "next"), ("xT1", 1, "next"), ("Q0", 3, "next"), ("Q1", 6, "next")]
    + [("ctxT", 6, "next"), ("K", 7, "next"), ("V", 4, "next")]
)
BANK = {item: bank for item, bank, _ in PLAN + LEAD_PLAN}


def flamingo_block(nc, x, ctx_rows, mask, g_attn, g_ffn, wq, wk, wv, wo, gate_w, gate_r, gate_b, w1, b1, w2, b2, out):
    TOK, DM = x.shape
    NBATCH, KEYS, _ = ctx_rows.shape
    NQ = TOK // NBATCH
    U = 2 * NQ
    DUOS = TOK // (2 * U)
    NB = NBATCH // DUOS
    KC = DM // P
    NG, DH, HG = 8, 16, 4
    J = NG // S
    HP = HG // 2
    OC = S * DH + S
    NE = 3
    VIS = int(NQ * 0.3)
    LAST = KEYS - WIN
    assert NB == 4 and S * J == NG and HP * J * P == 512

    def present(duo_kind, D):
        return {"lead": ("next",), "first": ("this", "next", "prep"), "mid": ("this", "next", "prev"),
                "last": ("this", "prev"), "tail": ("prev",)}[D].count(duo_kind) > 0

    def in_turn(turn, bank, before=None):
        n = 0
        for item, b, kind in (LEAD_PLAN if turn == "lead" else PLAN):
            if item == before:
                break
            n += b == bank and present(kind, turn)
        return n

    class Turn:

        def __init__(self, kind, D):
            self.kind, self.D = kind, D
            self.this, self.next, self.prev = (present(k, kind) for k in ("this", "next", "prev"))

        def before(self, item, bank=None):
            bank = BANK[item] if item else bank
            at = in_turn(self.kind, bank, item) if item else 0
            if self.kind == "lead":
                return at
            at += in_turn("lead", bank)
            if self.kind == "first":
                return at
            at += in_turn("first", bank)
            if self.kind == "mid":
                return (self.D - 1) * in_turn("mid", bank) + at
            at += (DUOS - 2) * in_turn("mid", bank)
            if self.kind == "last":
                return at
            return at + in_turn("last", bank)

    def over_turns(eng, body):
        body(Turn("lead", -1))
        body(Turn("first", 0))
        with eng.Fori(1, DUOS - 1) as D:
            body(Turn("mid", D))
        body(Turn("last", DUOS - 1))
        body(Turn("tail", DUOS))

    WINDOWS = KEYS // WIN
    OVERLAP = (WINDOWS + 1) * WIN - KEYS
    assert 0 < OVERLAP < WIN

    x_v = x.rearrange("(n u p) d -> n p u d", u=2, p=U)
    out_v = out.rearrange("(n u p) d -> n p u d", u=2, p=U)
    ctx_v = ctx_rows.rearrange("(n b) k d -> n b k d", b=NB)

    with ExitStack() as stack:
        def sb(name, shape, dt=F32):
            return stack.enter_context(nc.sbuf_tensor(name, shape, dt))

        def sem(name):
            return stack.enter_context(nc.semaphore(name))

        bank = [stack.enter_context(nc.psum_tensor(f"bank{i}", [P, 512], F32)) for i in range(8)]

        WQ, W1, W2 = 0, KC, KC + NE * KC
        CHUNKS = KC + 2 * NE * KC
        w_slots = sb("w_slots", [P, CHUNKS + 2, DM])
        wk_sb = sb("wk_sb", [P, KC, P])
        wv_sb = sb("wv_sb", [P, KC, P])
        wo_sb = sb("wo_sb", [P, HG, DM])
        w_split = w_slots[:].bitcast(F16).rearrange("p c (s n) -> p c s n", s=2)
        b1_sb = sb("b1_sb", [P, NE, KC])
        b1_half = sb("b1_half", [P, KC])
        b2_sb = sb("b2_sb", [U, NE, DM])
        gw_sb = sb("gw_sb", [P, KC * NE])
        gw_split = sb("gw_split", [P, 2, KC * NE], F16)
        N_Q, N_W1, N_ACT, N_W2, NORMS = 0, 2, 2 + NE, 2 + 2 * NE, 2 + 3 * NE
        sq = sb("sq", [P, NORMS])
        sq_all = sb("sq_all", [P, NORMS])
        root = sb("root", [P, NORMS])
        scale = sb("scale", [P, NORMS])
        unscale = sb("unscale", [P, NORMS])
        un_q = sb("un_q", [P, 2])
        un_up = sb("un_up", [P, NE + 1])
        un_down = sb("un_down", [P, NE])
        ones = sb("ones", [P, P])
        gr_sb = sb("gr_sb", [U, NE])
        gb_sb = sb("gb_sb", [U, NE])
        gains = sb("gains", [U, 2])
        tanh_g = sb("tanh_g", [U, 2])
        ident = sb("ident", [P, P])
        pair_ident = sb("pair_ident", [NQ, U], BF16)
        group_sel = sb("group_sel", [P, NG])
        s_sel = sb("s_sel", [P, S])
        text_sel = sb("text_sel", [U, 2, NQ])
        vision_sel = sb("vision_sel", [U, 2, NQ])
        first_sel = sb("first_sel", [U, 2, NQ])
        minus_half = sb("minus_half", [P, NORMS])
        eps_col = sb("eps_col", [U, 2])
        early = w_slots[:, W2 + 2:CHUNKS + 2, :].rearrange("p c n -> p (c n)")
        key_up = early[0:NQ, 0:KEYS]
        seen_at = early[0:NQ, KEYS:2 * KEYS]
        mask_sb = sb("mask_sb", [NQ, KEYS], U8)
        ends = sb("ends", [NQ, 3])
        row_any = sb("row_any", [NQ, 1])
        row_any_bf = sb("row_any_bf", [NQ, 1], BF16)
        alive = sb("alive", [U, 1])
        verdict = sb("verdict", [1, 8])
        verdict_i = sb("verdict_i", [1, 2], I32)
        bias_win = sb("bias_win", [NQ, WIN], BF16)
        ctx_sb = sb("ctx_sb", [P, DM])
        ctxT_sb = sb("ctxT_sb", [P, KC, P])
        KB = sb("KB", [P, NB, NG, WIN])
        VB = sb("VB", [P, NB, J, OC])
        x_sb = sb("x_sb", [U, 2, DM])
        ln1_st = sb("ln1_st", [U, 2, 6])
        ln1_mv = sb("ln1_mv", [U, 2, 2])
        ln1_r = sb("ln1_r", [U, 3, 2])
        xn = sb("xn", [U, 2, DM])
        xnT = sb("xnT", [P, 2, 2, KC, U], F16)
        QT = sb("QT", [P, NB, HG, NQ])
        top = sb("top", [U, NB, HP * J * S])
        probs = sb("probs", [U, NB, HP * J * S, WIN])
        PT = sb("PT", [P, NB, HP * J, U])
        O_sb = sb("O_sb", [U, NB, HP * J, OC])
        O_rec = sb("O_rec", [U, NB, HP * J, S])
        On = sb("On", [U, NB, HP * J, S, DH])
        OT = sb("OT", [P, 2, HG, 2, NQ])
        xr = sb("xr", [U, 2, DM])
        x1 = sb("x1", [U, 2, DM])
        ln2_st = sb("ln2_st", [U, 2, 6])
        ln2_mv = sb("ln2_mv", [U, 2, 2])
        ln2_r = sb("ln2_r", [U, 2, 2])
        h = sb("h", [U, 2, DM])
        h_abs = sb("h_abs", [U, 2, DM], BF16)
        h_sum = sb("h_sum", [U, 2])
        hT = sb("hT", [P, 2, KC, 2, U], F16)
        act = sb("act", [P, 2, NE, KC, 2 * U], F16)
        squares = act[:].rearrange("p s e k t -> p (s e k t)").bitcast(F32)
        act_t = sb("act_t", [P, 2, 2, 2 * U])
        silu_u = sb("silu_u", [P, 2, 2, 2 * U])
        gt = sb("gt", [U, 16, 2])
        best = sb("best", [U, 2, 2])
        sc = sb("sc", [U, 2, NE])
        wins = sb("wins", [U, 2, NE])
        rank_hot = sb("rank_hot", [U, 2, 2, NE])
        picked = sb("picked", [U, 2, 2, NE])
        coef2 = sb("coef2", [U, 2, 2, NE])
        coef = sb("coef", [U, 2, NE])
        coef_down = sb("coef_down", [U, 2, NE])
        b2_part = sb("b2_part", [U, 2, DM])
        b2_sum = sb("b2_sum", [U, 2, DM])
        y = sb("y", [U, 2, DM])
        g_ctx = sb("g_ctx", [P, DM])
        g_ctxT = sb("g_ctxT", [P, KC, P])
        g_KB = sb("g_KB", [P, NB, NG, WIN])
        g_VB = sb("g_VB", [P, NB, J, OC])
        g_bias = sb("g_bias", [NQ, WIN], BF16)
        g_top = sb("g_top", [U, NB, HP * J * S])
        g_new = sb("g_new", [U, HP * J * S])
        g_decay = sb("g_decay", [U, HP * J * S])

        bank_full = [sem(f"bank_full{i}") for i in range(8)]
        bank_free = [sem(f"bank_free{i}") for i in range(8)]
        mask_loaded = sem("mask_loaded")
        wkv_loaded = sem("wkv_loaded")
        wq_loaded = sem("wq_loaded")
        wo_loaded = sem("wo_loaded")
        w1_loaded = sem("w1_loaded")
        norms_summed = sem("norms_summed")
        norm_step = sem("norm_step")
        norms_ready = sem("norms_ready")
        roots_ready = sem("roots_ready")
        scales_ready = sem("scales_ready")
        w_hi = sem("w_hi")
        w_lo = sem("w_lo")
        gate_weights = sem("gate_weights")
        xT_hi = sem("xT_hi")
        hT_hi = sem("hT_hi")
        acted = sem("acted")
        act_hi = sem("act_hi")
        w2_loaded = sem("w2_loaded")
        small_loaded = sem("small_loaded")
        setup_pool = sem("setup_pool")
        consts_ready = sem("consts_ready")
        mask_step = sem("mask_step")
        ends_ready = sem("ends_ready")
        ends_turned = sem("ends_turned")
        verdict_ready = sem("verdict_ready")
        row_any_ready = sem("row_any_ready")
        alive_turned = sem("alive_turned")
        alive_ready = sem("alive_ready")
        bias_ready = sem("bias_ready")
        gains_ready = sem("gains_ready")
        ctx_loaded = sem("ctx_loaded")
        ctx_read = sem("ctx_read")
        x_loaded = sem("x_loaded")
        xr_loaded = sem("xr_loaded")
        ln1_stats = sem("ln1_stats")
        ln1_mean = sem("ln1_mean")
        ln1_step = sem("ln1_step")
        ln1_rstd = sem("ln1_rstd")
        xn_ready = sem("xn_ready")
        top_ready = sem("top_ready")
        probs_ready = sem("probs_ready")
        sums_inverted = sem("sums_inverted")
        on_ready = sem("on_ready")
        ln2_stats = sem("ln2_stats")
        ln2_mean = sem("ln2_mean")
        ln2_step = sem("ln2_step")
        ln2_rstd = sem("ln2_rstd")
        h_ready = sem("h_ready")
        h_summed = sem("h_summed")
        gate_step = sem("gate_step")
        logits_ready = sem("logits_ready")
        gate_exp = sem("gate_exp")
        ranks_ready = sem("ranks_ready")
        coef_ready = sem("coef_ready")
        silu_tanh = sem("silu_tanh")
        silu_half = sem("silu_half")
        act_ready = sem("act_ready")
        b2_step = sem("b2_step")
        y_ready = sem("y_ready")
        y_stored = sem("y_stored")
        waits_carried = sem("waits_carried")
        g_loaded = sem("g_loaded")
        g_pe = sem("g_pe")
        g_act = sem("g_act")
        g_dve = sem("g_dve")
        g_cleared = sem("g_cleared")
        g_scaled = sem("g_scaled")

        block = stack.enter_context(nc.Block())

        def full(eng, turn, item):
            eng.wait_ge(bank_full[BANK[item]], turn.before(item) + 1)
            return bank_free[BANK[item]]

        def taken(eng, turn, item):
            eng.wait_ge(bank_free[BANK[item]], turn.before(item) + 1)

        G_PE = 3 + 3 * NB
        G_ACT = 1 + 2 * NB
        G_DVE = 3 + 6 * NB

        def carried(eng):
            eng.sem_inc(waits_carried, 1)

        def general(eng, flag, D, body):
            with eng.If(flag > 0):
                with eng.Fori(0, WINDOWS) as c:
                    body(D * (WINDOWS + 1) + c, c * WIN, False)
                body(D * (WINDOWS + 1) + WINDOWS, LAST, True)

        @block.sync
        def _(sp):
            sp.dma_start(mask_sb[:], mask).then_inc(mask_loaded, 16)
            sp.dma_start(x_sb[:], x_v[0]).then_inc(x_loaded, 16)
            sp.dma_start(w_slots[:, WQ + 2:W1 + 2, :], wq).then_inc(wq_loaded, 16)
            sp.dma_start(wk_sb[:], wk).then_inc(wkv_loaded, 16)
            sp.dma_start(wv_sb[:], wv).then_inc(wkv_loaded, 16)
            sp.dma_start(w_slots[:, W1 + 2:W2 + 2, :], w1).then_inc(w1_loaded, 16)
            sp.wait_ge(verdict_ready, 1)
            start = sp.value_load(verdict_i[0:1, 0:1], min_val=0, max_val=LAST)
            flag = sp.value_load(verdict_i[0:1, 1:2], min_val=0, max_val=1)

            def load_context(N):
                for b in range(NB):
                    sp.dma_start(ctx_sb[WIN * b:WIN * (b + 1), :], ctx_v[N, b, bass.ds(start, WIN), :]).then_inc(ctx_loaded, 16)

            def body(turn, ahead=True):
                D = turn.D
                if turn.this:
                    if turn.kind != "first":
                        sp.wait_ge(ln2_stats, 2 * D)
                        carried(sp)
                    sp.dma_start(xr[:], x_v[D]).then_inc(xr_loaded, 16)
                if turn.kind == "first":
                    sp.dma_start(wo_sb[:], wo).then_inc(wo_loaded, 16)
                    sp.dma_start(w_slots[:, W2 + 2:CHUNKS + 2, :], w2).then_inc(w2_loaded, 16)
                if ahead:
                    sp.wait_ge(ctx_read, D + 2)
                    carried(sp)
                    load_context(D + 2)
                    sp.wait_ge(xn_ready, 2 * (D + 2))
                    carried(sp)
                    sp.dma_start(x_sb[:], x_v[D + 2]).then_inc(x_loaded, 16)
                if turn.this:
                    def window(n, first_key, last):
                        sp.wait_ge(g_pe, n * G_PE + 1)
                        carried(sp)
                        for b in range(NB):
                            sp.dma_start(g_ctx[WIN * b:WIN * (b + 1), :],
                                         ctx_v[D, b, bass.ds(first_key, WIN), :]).then_inc(g_loaded, 16)

                    general(sp, flag, D, window)
                if turn.prev:
                    sp.wait_ge(y_ready, 2 * D)
                    carried(sp)
                    sp.dma_start(out_v[D - 1], y[:]).then_inc(y_stored, 16)

            sp.sem_inc(y_stored, 1)
            load_context(0)
            body(Turn("lead", -1))
            body(Turn("first", 0))
            with sp.Fori(1, DUOS - 2) as D:
                body(Turn("mid", D))
            body(Turn("mid", DUOS - 2), ahead=False)
            body(Turn("last", DUOS - 1), ahead=False)
            body(Turn("tail", DUOS), ahead=False)
            sp.wait_ge(y_stored, 16 * DUOS + 1)

        @block.gpsimd
        def _(pool):
            steps = [0]
            g = nc.gpsimd

            def norm_one(N):
                pool.wait_ge(ln1_mean, 2 * N + 2)
                g.tensor_tensor(ln1_r[:, 0, :], ln1_mv[:, :, 1], eps_col[:], ALU.add).then_inc(ln1_step, 1)
                pool.wait_ge(ln1_step, 2 * N + 1)
                g.tensor_tensor(ln1_r[:, 1, :], ln1_r[:, 0, :], minus_half[0:U, 0:2], ALU.pow).then_inc(ln1_step, 1)
                pool.wait_ge(ln1_step, 2 * N + 2)
                g.tensor_tensor(ln1_r[:, 2, :], ln1_r[:, 1, :], alive[:].broadcast_to([U, 2]), ALU.mult).then_inc(ln1_rstd, 1)

            def roots(n, a, b):
                pool.wait_ge(norms_ready, n + 1)
                g.tensor_tensor(root[:, a:b], sq_all[:, a:b], minus_half[:, a:b], ALU.pow).then_inc(roots_ready, 1)

            def lead_norm():
                pool.wait_ge(alive_ready, 1)
                norm_one(0)
                roots(0, N_Q, N_W1)

            def made(ins):
                steps[0] += 1
                ins.then_inc(setup_pool, 1)
                pool.wait_ge(setup_pool, steps[0])

            def keep(t, op, fill, base, pattern, mult):
                made(g.affine_select(out=t, in_=t, compare_op=op, fill=fill, base=base, pattern=pattern,
                                     channel_multiplier=mult))

            g.memset(minus_half[:], -0.5)
            g.memset(eps_col[:], LN_EPS)
            g.memset(ident[:], 0.0)
            g.memset(ones[:], 1.0)
            made(g.memset(pair_ident[:], 0.0))
            keep(pair_ident[:].rearrange("p (a q) -> p a q", a=2), ALU.not_equal, 1.0, 0, [[0, 2], [-1, NQ]], 1)
            made(g.iota(key_up, [[1, KEYS]], base=1, channel_multiplier=0, allow_small_or_imprecise_dtypes=True))
            keep(ident[:], ALU.not_equal, 1.0, 0, [[-1, P]], 1)
            lead_norm()
            g.memset(group_sel[:], 1.0)
            g.memset(s_sel[:], 1.0)
            g.memset(text_sel[:], 1.0 / ((NQ - VIS) * DM))
            g.memset(vision_sel[:], 1.0 / (VIS * DM))
            g.memset(first_sel[:], 0.0)
            g.memset(g_VB[:], 0.0)
            made(g.memset(VB[:], 0.0))
            keep(group_sel[:], ALU.is_ge, 0.0, 0, [[-DH, NG]], 1)
            keep(group_sel[:], ALU.is_ge, 0.0, DH - 1, [[DH, NG]], -1)
            keep(s_sel[:], ALU.is_ge, 0.0, 0, [[-WIN, S]], 1)
            keep(s_sel[:], ALU.is_ge, 0.0, WIN - 1, [[WIN, S]], -1)
            keep(text_sel[:], ALU.is_ge, 0.0, -VIS, [[-NQ, 2], [0, NQ]], 1)
            keep(text_sel[:], ALU.is_ge, 0.0, NQ - 1, [[NQ, 2], [0, NQ]], -1)
            keep(vision_sel[:], ALU.is_ge, 0.0, 0, [[-NQ, 2], [0, NQ]], 1)
            keep(vision_sel[:], ALU.is_ge, 0.0, VIS - 1, [[NQ, 2], [0, NQ]], -1)
            keep(first_sel[:], ALU.not_equal, 1.0, 0, [[-NQ, 2], [0, NQ]], 1)
            for values in (g_VB, VB):
                last = g.tensor_copy(values[:, :, :, S * DH:].rearrange("p b j s -> p (b j) s"),
                                     s_sel[:].unsqueeze(1).broadcast_to([P, NB * J, S]))
            last.then_inc(consts_ready, 1)

            def body(turn):
                D = turn.D

                def finish(u):
                    taken(pool, turn, f"dn{NE * u + NE - 1}")
                    g.tensor_tensor(y[:, u, :], y[:, u, :], b2_sum[:, u, :], ALU.add).then_inc(y_ready, 1)

                if turn.next and turn.kind != "lead":
                    norm_one(D + 1)
                if turn.kind == "first":
                    roots(1, N_W1, N_W2)
                if turn.this:
                    for u in range(2):
                        pool.wait_ge(sums_inverted, 2 * D + u + 1)
                        for b in (2 * u, 2 * u + 1):
                            last = g.tensor_tensor(On[:, b],
                                                   O_sb[:, b, :, 0:S * DH].rearrange("p t (s d) -> p t s d", s=S),
                                                   O_rec[:, b].unsqueeze(3).broadcast_to([U, HP * J, S, DH]), ALU.mult)
                        last.then_inc(on_ready, 1)
                if turn.prev:
                    pool.wait_ge(coef_ready, D)
                    for u in range(2):
                        for e in range(NE):
                            n = 10 * (D - 1) + 5 * u + 2 * e
                            g.tensor_tensor((b2_part if e else b2_sum)[:, u, :], b2_sb[:, e, :],
                                            coef[:, u, e:e + 1].broadcast_to([U, DM]), ALU.mult).then_inc(b2_step, 1)
                            if e == 0:
                                pool.wait_ge(b2_step, n + 1)
                            else:
                                pool.wait_ge(b2_step, n)
                                g.tensor_tensor(b2_sum[:, u, :], b2_sum[:, u, :], b2_part[:, u, :], ALU.add).then_inc(b2_step, 1)
                                pool.wait_ge(b2_step, n + 1)
                    finish(0)
                if turn.this:
                    for u in range(2):
                        pool.wait_ge(ln2_mean, 2 * D + u + 1)
                        g.tensor_tensor(ln2_r[:, u, 0:1], ln2_mv[:, u, 1:2], eps_col[:, 0:1], ALU.add).then_inc(ln2_step, 1)
                        pool.wait_ge(ln2_step, 2 * D + u + 1)
                        g.tensor_tensor(ln2_r[:, u, 1:2], ln2_r[:, u, 0:1], minus_half[0:U, 0:1], ALU.pow).then_inc(ln2_rstd, 1)
                if turn.prev:
                    finish(1)
                if turn.kind == "first":
                    roots(2, N_W2, NORMS)

            over_turns(pool, body)

        @block.scalar
        def _(sca):
            a = nc.scalar
            for dst, src in ((b1_sb[:], b1), (gw_sb[:], gate_w), (gr_sb[:], gate_r.broadcast_to([U, NE])),
                             (gb_sb[:], gate_b.broadcast_to([U, NE])), (gains[:, 0:1], g_attn.broadcast_to([U, 1])),
                             (gains[:, 1:2], g_ffn.broadcast_to([U, 1])),
                             (b2_sb[:].rearrange("p e d -> p (e d)"), b2.broadcast_to([U, NE * DM]))):
                sca.dma_start(dst, src).then_inc(small_loaded, 16)

            squared = [0]

            def square_sum(col, src):
                n = src.free_size()
                if squared[0]:
                    sca.wait_ge(norms_summed, squared[0])
                a.activation(squares[:, 0:n], src, ACT.Square, accum_out=sq[:, col:col + 1]).then_inc(norms_summed, 1)
                squared[0] += 1

            def slots(c0, n):
                return w_slots[:, c0 + 2:c0 + 2 + n, :].rearrange("p c n -> p (c n)")

            def round_weights(c0, c1, col, n):
                sca.wait_ge(scales_ready, n)
                for c in range(c0, c1):
                    if c >= 2:
                        sca.wait_ge(w_lo, c - 1)
                    a.activation(w_split[:, c, 0, :], w_slots[:, c + 2, :], ACT.Copy,
                                 scale=scale[:, col(c):col(c) + 1]).then_inc(w_hi, 1)

            sca.wait_ge(small_loaded, 16 * 7)
            a.activation(tanh_g[:], gains[:], ACT.Tanh).then_inc(gains_ready, 1)
            a.activation(b1_half[:], b1_sb[:, 2, :], ACT.Copy, scale=0.5).then_inc(gains_ready, 1)
            square_sum(N_Q + 1, gw_sb[:])
            sca.wait_ge(wq_loaded, 16)
            square_sum(N_Q, slots(WQ, KC))
            sca.wait_ge(gains_ready, 2)
            round_weights(WQ, W1, lambda c: N_Q, 1)

            def body(turn):
                D = turn.D

                def exps(b):
                    taken(sca, turn, f"S{b}")
                    a.activation(probs[:, b], probs[:, b], ACT.Exp).then_inc(probs_ready, 1)

                def up(i, func, bias, unscale):
                    full(sca, turn, f"up{i}")
                    if i >= 2:
                        sca.wait_ge(act_ready, 6 * (D - 1) + i - 1)
                    for m in range(2):
                        k = 2 * (i % 2) + m
                        ins = a.activation(act_t[:, i % 2, m, :], bank[BANK[f"up{i}"]][:, m * 2 * U:(m + 1) * 2 * U], func,
                                           bias=bias[:, k:k + 1], scale=unscale)
                    return ins

                def round_act(i, src):
                    e, half = divmod(i, 2)
                    a.activation(act[:, 0, e, 2 * half:2 * half + 2, :].rearrange("p m t -> p (m t)"),
                                 src[:, i % 2].rearrange("p m t -> p (m t)"), ACT.Copy,
                                 scale=scale[:, N_ACT + e:N_ACT + e + 1]).then_inc(act_hi, 1)

                def turned_x():
                    for u in range(2):
                        full(sca, turn, f"xT{u}")
                        a.activation(xnT[:, 0, u].rearrange("p k t -> p (k t)"), bank[BANK[f"xT{u}"]][:, 0:KC * U],
                                     ACT.Copy, scale=LN_SCALE).then_inc(xT_hi, 1)

                def queries():
                    for u in range(2):
                        free = full(sca, turn, f"Q{u}")
                        a.activation(QT[:, 2 * u:2 * u + 2].rearrange("p b c q -> p c b q"),
                                     bank[BANK[f"Q{u}"]][:, 0:HG * U].rearrange("p (c b q) -> p c b q", c=HG, b=2),
                                     ACT.Copy, scale=un_q[:, 0:1]).then_inc(free, 1)

                if turn.kind == "lead":
                    turned_x()
                    sca.wait_ge(w1_loaded, 16)
                    for e in range(NE):
                        square_sum(N_W1 + e, slots(W1 + e * KC, KC))
                        square_sum(N_ACT + e, b1_sb[:, e, :])
                    queries()
                    sca.wait_ge(verdict_ready, 1)
                    flags.append(sca.value_load(verdict_i[0:1, 1:2], min_val=0, max_val=1))

                if turn.next:
                    free = full(sca, turn, "ctxT")
                    a.activation(ctxT_sb[:].rearrange("p k n -> p (k n)"), bank[BANK["ctxT"]][:], ACT.Copy).then_inc(free, 1)
                if turn.prev:
                    for u in range(2):
                        full(sca, turn, f"hT{u}")
                        a.activation(hT[:, 0, :, u, :], bank[BANK[f"hT{u}"]][:, 0:KC * U].rearrange("p (k t) -> p k t", k=KC),
                                     ACT.Copy, scale=LN_SCALE).then_inc(hT_hi, 1)
                if turn.this:
                    exps(0)
                    exps(1)
                if turn.prev:
                    for i in (0, 1):
                        up(i, ACT.Tanh, b1_sb[:, 0, :], un_up[:, 0:1]).then_inc(bank_free[BANK[f"up{i}"]], 1)
                    for i in (0, 1):
                        taken(sca, turn, f"up{i}")
                        round_act(i, act_t)
                if turn.this:
                    exps(2)
                    exps(3)
                if turn.prev:
                    sca.wait_ge(logits_ready, D)
                    a.activation(sc[:], sc[:], ACT.Exp).then_inc(gate_exp, 1)
                if turn.this:
                    def window(n, first_key, last):
                        sca.wait_ge(g_pe, n * G_PE + 2)
                        a.activation(g_ctxT[:].rearrange("p k n -> p (k n)"), bank[0][:], ACT.Copy).then_inc(g_act, 1)
                        for b in range(NB):
                            sca.wait_ge(g_dve, n * G_DVE + 3 + 6 * b + 5)
                            a.activation(g_decay[:], g_decay[:], ACT.Exp).then_inc(g_act, 1)
                            a.activation(probs[:, b], probs[:, b], ACT.Exp).then_inc(g_act, 1)

                    general(sca, flags[0], D, window)
                if turn.prev:
                    for i in (2, 3):
                        up(i, ACT.Gelu, b1_sb[:, 1, :], un_up[:, 1:2]).then_inc(bank_free[BANK[f"up{i}"]], 1)
                    for i in (2, 3):
                        taken(sca, turn, f"up{i}")
                        round_act(i, act_t)
                if turn.next and turn.kind != "lead":
                    turned_x()
                if turn.prev:
                    for i in (4, 5):
                        up(i, ACT.Tanh, b1_half, un_up[:, NE:NE + 1]).then_inc(silu_tanh, 1)
                    for i in (4, 5):
                        sca.wait_ge(acted, 2 * (D - 1) + i - 3)
                        round_act(i, silu_u)
                if turn.kind == "first":
                    round_weights(W1, W2, lambda c: N_W1 + (c - W1) // KC, 2)
                if turn.next and turn.kind != "lead":
                    queries()
                if turn.this:
                    for u in range(2):
                        free = full(sca, turn, f"OT{u}")
                        for b in range(2):
                            last = a.activation(OT[:, u, :, b, :],
                                                bank[BANK[f"OT{u}"]][:, b * HG * NQ:(b + 1) * HG * NQ].rearrange("p (c q) -> p c q", c=HG),
                                                ACT.Copy)
                        last.then_inc(free, 1)
                if turn.kind == "first":
                    sca.wait_ge(w2_loaded, 16)
                    for e in range(NE):
                        square_sum(N_W2 + e, slots(W2 + e * KC, KC))
                if turn.this:
                    for u in range(2):
                        sca.wait_ge(h_ready, 2 * D + u + 1)
                        a.activation(h_abs[:, u, :], h[:, u, :], ACT.Abs, accum_out=h_sum[:, u:u + 1]).then_inc(h_summed, 1)
                if turn.kind == "first":
                    round_weights(W2, CHUNKS, lambda c: N_W2 + (c - W2) // KC, 3)

            flags = []
            over_turns(sca, body)

        @block.vector
        def _(dve):
            v = nc.vector
            dve.sem_inc(g_dve, 1)
            steps = [0]

            def step(ins):
                steps[0] += 1
                ins.then_inc(mask_step, 1)
                dve.wait_ge(mask_step, steps[0])

            def norm_stats(u, src, st, mv, stats, mean, n):
                v.bn_stats(st[:, u, :], src[:, u, :]).then_inc(stats, 1)
                dve.wait_ge(stats, n)
                carried(dve)
                v.bn_aggr(mv[:, u, :], st[:, u, :]).then_inc(mean, 1)

            norm_steps = [0]

            def nstep(ins):
                norm_steps[0] += 1
                ins.then_inc(norm_step, 1)
                dve.wait_ge(norm_step, norm_steps[0])

            def scales(n, a, b):
                dve.wait_ge(roots_ready, n + 1)
                nstep(v.tensor_scalar(scale[:, a:b].bitcast(U32), root[:, a:b].bitcast(U32), EXPONENT, None, ALU.bitwise_and))
                nstep(v.tensor_scalar(scale[:, a:b], scale[:, a:b], TOP_SCALE, None, ALU.mult))
                nstep(v.reciprocal(unscale[:, a:b], scale[:, a:b]))

            def split_weights(c0, c1, col):
                for c in range(c0, c1):
                    dve.wait_ge(w_hi, c + 1)
                    v.scalar_tensor_tensor(w_split[:, c, 1, :], w_slots[:, c + 2, :], scale[:, col(c):col(c) + 1],
                                           w_split[:, c, 0, :], ALU.mult, ALU.subtract).then_inc(w_lo, 1)

            def normalise(N):
                dve.wait_ge(ln1_rstd, N + 1)
                for u in range(2):
                    v.tensor_scalar(xn[:, u, :], x_sb[:, u, :], ln1_mv[:, u, 0:1], ln1_r[:, 2, u:u + 1],
                                    ALU.subtract, ALU.mult).then_inc(xn_ready, 1)

            lead = Turn("lead", -1)
            dve.wait_ge(mask_loaded, 16)
            step(v.tensor_reduce(row_any[:], mask_sb[:], AX.X, ALU.max))
            v.tensor_copy(row_any_bf[:], row_any[:]).then_inc(row_any_ready, 1)
            v.tensor_scalar(ends[:, 2:3], row_any[:], -1.0, None, ALU.mult)
            dve.wait_ge(x_loaded, 16)
            for u in range(2):
                norm_stats(u, x_sb, ln1_st, ln1_mv, ln1_stats, ln1_mean, u + 1)
            dve.wait_ge(alive_turned, 1)
            v.tensor_copy(alive[:], bank[5][0:U, 0:1]).then_inc(alive_ready, 1)
            dve.wait_ge(setup_pool, 3)
            step(v.scalar_tensor_tensor(seen_at, key_up, float(-KEYS - 1), mask_sb[:], ALU.add, ALU.mult))
            step(v.tensor_reduce(ends[:, 0:1], seen_at, AX.X, ALU.min))
            step(v.tensor_scalar(ends[:, 0:1], ends[:, 0:1], -1.0, None, ALU.mult))
            free = full(dve, lead, "norms_q")
            v.tensor_scalar(sq_all[:, N_Q:N_W1], bank[BANK["norms_q"]][:, 0:2], TINY, None, ALU.max).then_inc(free, 1)
            taken(dve, lead, "norms_q")
            dve.sem_inc(norms_ready, 1)
            step(v.tensor_tensor(seen_at, mask_sb[:], key_up, ALU.mult))
            scales(0, N_Q, N_W1)
            v.tensor_scalar(un_q[:, 0:1], unscale[:, N_Q:N_Q + 1], DH ** -0.5 / LN_SCALE, None, ALU.mult)
            v.tensor_scalar(un_q[:, 1:2], unscale[:, N_Q + 1:N_Q + 2], 1.0 / LN_SCALE, None, ALU.mult).then_inc(scales_ready, 1)
            step(v.tensor_reduce(ends[:, 1:2], seen_at, AX.X, ALU.max))
            v.memset(verdict[:], 0.0).then_inc(ends_ready, 1)
            normalise(0)
            dve.wait_ge(ends_turned, 1)
            step(v.tensor_reduce(verdict[:, 0:3], bank[7][0:1, 0:3 * NQ].rearrange("p (e q) -> p e q", e=3), AX.X, ALU.max))
            step(v.tensor_scalar(verdict[:, 3:4], verdict[:, 0:1], -1.0, float(KEYS), ALU.mult, ALU.add))
            step(v.tensor_scalar(verdict[:, 4:5], verdict[:, 3:4], float(LAST), None, ALU.min))
            step(v.tensor_tensor(verdict[:, 5:6], verdict[:, 0:1], verdict[:, 1:2], ALU.add))
            step(v.tensor_scalar(verdict[:, 5:6], verdict[:, 5:6], float(-KEYS - WIN), None, ALU.add))
            step(v.tensor_scalar(verdict[:, 6:7], verdict[:, 2:3], 1.0, None, ALU.add))
            step(v.tensor_tensor(verdict[:, 5:6], verdict[:, 5:6], verdict[:, 6:7], ALU.max))
            step(v.tensor_scalar(verdict[:, 5:6], verdict[:, 5:6], 0.0, None, ALU.is_gt))
            v.tensor_copy(verdict_i[:, 0:1], verdict[:, 4:5])
            v.tensor_copy(verdict_i[:, 1:2], verdict[:, 5:6]).then_inc(verdict_ready, 1)
            dve.wait_ge(verdict_ready, 1)
            start = dve.value_load(verdict_i[0:1, 0:1], min_val=0, max_val=LAST)
            flag = dve.value_load(verdict_i[0:1, 1:2], min_val=0, max_val=1)

            def take_bias(dst, first_key):
                return v.tensor_scalar(dst[:], mask_sb[:, bass.ds(first_key, WIN)], row_any[:, 0:1], BIG,
                                       ALU.subtract, ALU.mult)

            take_bias(bias_win, start).then_inc(bias_ready, 1)
            dve.wait_ge(gains_ready, 2)

            def spread_keys(dst, src):
                return v.tensor_tensor(dst[:], src[:, 0:P].rearrange("p (b k) -> p b k", b=NB).unsqueeze(2)
                                       .broadcast_to([P, NB, NG, WIN]),
                                       group_sel[:].unsqueeze(1).unsqueeze(3).broadcast_to([P, NB, NG, WIN]), ALU.mult)

            def spread_values(dst, src):
                src = src[:, 0:P].rearrange("p (j s d) -> p j s d", j=J, s=S)
                for b in range(NB):
                    for s in range(S):
                        last = v.tensor_copy(dst[WIN * s:WIN * (s + 1), b, :, DH * s:DH * (s + 1)],
                                             src[WIN * b:WIN * (b + 1), :, s, :])
                return last

            def body(turn):
                D = turn.D

                def scores(b):
                    src = bank[b][0:U, :].rearrange("p (t k) -> p t k", k=WIN)
                    free = full(dve, turn, f"S{b}")
                    v.tensor_reduce(top[:, b, :], src, AX.X, ALU.max).then_inc(top_ready, 1)
                    dve.wait_ge(top_ready, NB * D + b + 1)
                    v.tensor_tensor(probs[:, b], src, top[:, b, :].unsqueeze(2).broadcast_to([U, HP * J * S, WIN]),
                                    ALU.subtract).then_inc(free, 1)

                def take_probs(b):
                    free = full(dve, turn, f"PT{b}")
                    v.tensor_copy(PT[:, b].rearrange("p t q -> p (t q)"), bank[b][:, 0:HP * J * U]).then_inc(free, 1)

                def take_output(b):
                    free = full(dve, turn, f"O{b}")
                    v.tensor_copy(O_sb[:, b].rearrange("p t c -> p (t c)"), bank[b][0:U, 0:HP * J * OC]).then_inc(free, 1)

                def down(i):
                    u, e = divmod(i, NE)
                    free = full(dve, turn, f"dn{i}")
                    if e:
                        taken(dve, turn, f"dn{i - 1}")
                    v.scalar_tensor_tensor(y[:, u, :], bank[BANK[f"dn{i}"]][0:U, :], coef_down[:, u, e:e + 1],
                                           (y if e else x1)[:, u, :],
                                           ALU.mult, ALU.add).then_inc(free, 1)

                def next_keys():
                    free = full(dve, turn, "K")
                    spread_keys(KB, bank[BANK["K"]]).then_inc(free, 1)

                def next_values():
                    free = full(dve, turn, "V")
                    spread_values(VB, bank[BANK["V"]]).then_inc(free, 1)

                def turned_x():
                    for u in range(2):
                        free = full(dve, turn, f"xT{u}")
                        dve.wait_ge(xT_hi, 2 * (D + 1) + u + 1)
                        v.scalar_tensor_tensor(xnT[:, 1, u].rearrange("p k t -> p (k t)"), bank[BANK[f"xT{u}"]][:, 0:KC * U],
                                               LN_SCALE, xnT[:, 0, u].rearrange("p k t -> p (k t)"),
                                               ALU.mult, ALU.subtract).then_inc(free, 1)

                def split_act(i, src):
                    e, half = divmod(i, 2)
                    hi, lo = (act[:, s, e, 2 * half:2 * half + 2, :].rearrange("p m t -> p (m t)") for s in range(2))
                    dve.wait_ge(act_hi, 6 * (D - 1) + i + 1)
                    v.scalar_tensor_tensor(lo, src[:, i % 2].rearrange("p m t -> p (m t)"), scale[:, N_ACT + e:N_ACT + e + 1],
                                           hi, ALU.mult, ALU.subtract).then_inc(act_ready, 1)

                if turn.kind == "lead":
                    split_weights(WQ, W1, lambda c: N_Q)
                    turned_x()
                    nstep(v.tensor_scalar(gw_split[:, 0, :], gw_sb[:], scale[:, N_Q + 1:N_Q + 2], None, ALU.mult))
                    v.scalar_tensor_tensor(gw_split[:, 1, :], gw_sb[:], scale[:, N_Q + 1:N_Q + 2], gw_split[:, 0, :],
                                           ALU.mult, ALU.subtract).then_inc(gate_weights, 1)
                    dve.wait_ge(consts_ready, 1)
                    next_keys()
                    next_values()

                gate_steps = [0]

                def gstep(ins):
                    gate_steps[0] += 1
                    ins.then_inc(gate_step, 1)
                    dve.wait_ge(gate_step, GATE_STEPS * (D - 1) + gate_steps[0])

                if turn.this:
                    scores(0)
                    scores(1)
                if turn.prev:
                    for u in range(2):
                        free = full(dve, turn, f"hT{u}")
                        dve.wait_ge(hT_hi, 2 * (D - 1) + u + 1)
                        v.scalar_tensor_tensor(hT[:, 1, :, u, :],
                                               bank[BANK[f"hT{u}"]][:, 0:KC * U].rearrange("p (k t) -> p k t", k=KC),
                                               LN_SCALE, hT[:, 0, :, u, :], ALU.mult, ALU.subtract).then_inc(free, 1)
                if turn.this:
                    scores(2)
                    scores(3)
                if turn.prev:
                    free = full(dve, turn, "gate")
                    src = bank[BANK["gate"]]
                    gstep(v.tensor_scalar(gt[:, 0, :], src[0:U, 10:12], 1e-8, None, ALU.add))
                    gstep(v.reciprocal(gt[:, 1, :], gt[:, 0, :]))
                    gstep(v.tensor_tensor(gt[:, 2, :], src[0:U, 8:10], gt[:, 1, :], ALU.mult))
                    gstep(v.tensor_tensor(sc[:], gt[:, 2, :].unsqueeze(2).broadcast_to([U, 2, NE]),
                                          gr_sb[:].unsqueeze(1).broadcast_to([U, 2, NE]), ALU.mult))
                    v.scalar_tensor_tensor(sc[:], src[0:U, 0:2 * NE].rearrange("p (u e) -> p u e", u=2), un_q[0:U, 1:2],
                                           sc[:], ALU.mult, ALU.add).then_inc(free, 1)
                    taken(dve, turn, "gate")
                    gstep(v.tensor_tensor(sc[:], sc[:], gb_sb[:].unsqueeze(1).broadcast_to([U, 2, NE]), ALU.add))
                    gstep(v.tensor_reduce(gt[:, 3, :], sc[:], AX.X, ALU.max))
                    v.tensor_tensor(sc[:], sc[:], gt[:, 3, :].unsqueeze(2).broadcast_to([U, 2, NE]),
                                    ALU.subtract).then_inc(logits_ready, 1)
                if turn.next and turn.kind != "lead":
                    N = D + 1
                    next_keys()
                    dve.wait_ge(x_loaded, 16 * (N + 1))
                    for u in range(2):
                        norm_stats(u, x_sb, ln1_st, ln1_mv, ln1_stats, ln1_mean, 2 * N + u + 1)
                if turn.kind == "first":
                    free = full(dve, turn, "norms_up")
                    src = bank[BANK["norms_up"]]
                    v.tensor_scalar(sq_all[:, N_W1:N_ACT], src[:, 0:NE], TINY, None, ALU.max)
                    nstep(v.tensor_scalar(sq_all[:, N_ACT:N_W2], src[:, 0:NE], 2.0 * DM, None, ALU.mult))
                    v.scalar_tensor_tensor(sq_all[:, N_ACT:N_W2], src[:, NE:2 * NE], 2.0, sq_all[:, N_ACT:N_W2],
                                           ALU.mult, ALU.add).then_inc(free, 1)
                    taken(dve, turn, "norms_up")
                    nstep(v.tensor_scalar(sq_all[:, N_ACT:N_W2], sq_all[:, N_ACT:N_W2], TINY, None, ALU.max))
                    v.tensor_scalar(sq_all[:, N_ACT:N_ACT + 1], sq_all[:, N_ACT:N_ACT + 1], 1.0, None, ALU.min).then_inc(norms_ready, 1)
                    scales(1, N_W1, N_W2)
                    v.tensor_scalar(un_up[:, 0:NE], unscale[:, N_W1:N_ACT], 1.0 / LN_SCALE, None, ALU.mult)
                    v.tensor_scalar(un_up[:, NE:NE + 1], unscale[:, N_ACT - 1:N_ACT], 0.5 / LN_SCALE, None,
                                    ALU.mult).then_inc(scales_ready, 1)
                if turn.this:
                    take_probs(0)
                    take_probs(1)
                    take_output(0)
                    take_output(1)
                    take_probs(2)
                    take_probs(3)
                if turn.next and turn.kind != "lead":
                    normalise(D + 1)
                if turn.prev:
                    split_act(0, act_t)
                    split_act(1, act_t)
                if turn.this:
                    take_output(2)
                    take_output(3)
                    taken(dve, turn, "O2")
                    taken(dve, turn, "O3")
                    carried(dve)

                    def window(n, first_key, last):
                        k = [0]

                        def gdo(ins, wait=True):
                            k[0] += 1
                            ins.then_inc(g_dve, 1)
                            if wait:
                                dve.wait_ge(g_dve, n * G_DVE + k[0] + 1)

                        if last:
                            take_bias(g_bias, first_key).then_inc(bias_ready, 1)
                            dve.wait_ge(bias_ready, D + 2)
                            gdo(v.memset(g_bias[:, 0:OVERLAP], -BIG))
                        else:
                            gdo(take_bias(g_bias, first_key))
                        dve.wait_ge(g_pe, n * G_PE + 3)
                        gdo(spread_keys(g_KB, bank[1]))
                        dve.wait_ge(g_pe, n * G_PE + 4)
                        gdo(spread_values(g_VB, bank[2]))
                        for b in range(NB):
                            src = bank[3][0:U, :].rearrange("p (t k) -> p t k", k=WIN)
                            dve.wait_ge(g_pe, n * G_PE + 4 + 3 * b + 1)
                            gdo(v.tensor_reduce(g_new[:], src, AX.X, ALU.max))
                            gdo(v.tensor_tensor(g_new[:], g_new[:], g_top[:, b, :], ALU.max))
                            gdo(v.tensor_tensor(g_decay[:], g_top[:, b, :], g_new[:], ALU.subtract))
                            v.tensor_copy(g_top[:, b, :], g_new[:])
                            gdo(v.tensor_tensor(probs[:, b], src, g_new[:].unsqueeze(2).broadcast_to([U, HP * J * S, WIN]),
                                                ALU.subtract))
                            dve.wait_ge(g_pe, n * G_PE + 4 + 3 * b + 2)
                            gdo(v.tensor_copy(PT[:, b].rearrange("p t q -> p (t q)"), bank[0][:, 0:HP * J * U]))
                            dve.wait_ge(g_act, n * G_ACT + 1 + 2 * b + 1)
                            for t in range(HP * J):
                                v.tensor_tensor(O_sb[:, b, t, 0:S * DH].rearrange("p (s d) -> p s d", s=S),
                                                O_sb[:, b, t, 0:S * DH].rearrange("p (s d) -> p s d", s=S),
                                                g_decay[:, S * t:S * (t + 1)].unsqueeze(2).broadcast_to([U, S, DH]), ALU.mult)
                            v.tensor_tensor(O_sb[:, b, :, S * DH:], O_sb[:, b, :, S * DH:],
                                            g_decay[:].rearrange("p (t s) -> p t s", s=S), ALU.mult).then_inc(g_scaled, 1)
                            dve.wait_ge(g_scaled, n * NB + b + 1)
                            dve.wait_ge(g_pe, n * G_PE + 4 + 3 * b + 3)
                            gdo(v.tensor_tensor(O_sb[:, b].rearrange("p t c -> p (t c)"), O_sb[:, b].rearrange("p t c -> p (t c)"),
                                                bank[1][0:U, 0:HP * J * OC], ALU.add))
                        carried(dve)
                        assert k[0] == G_DVE

                    with dve.If(flag > 0):
                        v.memset(g_top[:], -3e38)
                        v.memset(O_sb[:], 0.0).then_inc(g_cleared, 1)
                        dve.wait_ge(g_cleared, D + 1)
                        carried(dve)
                        with dve.Fori(0, WINDOWS) as c:
                            window(D * (WINDOWS + 1) + c, c * WIN, False)
                        window(D * (WINDOWS + 1) + WINDOWS, LAST, True)
                    for u in range(2):
                        v.reciprocal(O_rec[:, 2 * u:2 * u + 2].rearrange("p b t s -> p (b t) s"),
                                     O_sb[:, 2 * u:2 * u + 2, :, S * DH:].rearrange("p b t s -> p (b t) s")).then_inc(sums_inverted, 1)
                if turn.next and turn.kind != "lead":
                    turned_x()
                    next_values()
                if turn.prev:
                    dve.wait_ge(gate_exp, D)
                    gstep(v.tensor_reduce(gt[:, 4, :], sc[:], AX.X, ALU.add))
                    gstep(v.reciprocal(gt[:, 5, :], gt[:, 4, :]))
                    gstep(v.tensor_tensor(sc[:], sc[:], gt[:, 5, :].unsqueeze(2).broadcast_to([U, 2, NE]), ALU.mult))
                    v.tensor_tensor(gt[:, 6, :], sc[:, :, 0], sc[:, :, 1], ALU.is_ge)
                    v.tensor_tensor(gt[:, 7, :], sc[:, :, 1], sc[:, :, 2], ALU.is_ge)
                    gstep(v.tensor_tensor(gt[:, 8, :], sc[:, :, 0], sc[:, :, 2], ALU.is_ge))
                    v.tensor_tensor(wins[:, :, 0], gt[:, 6, :], gt[:, 8, :], ALU.add)
                    v.tensor_tensor(wins[:, :, 1], gt[:, 7, :], gt[:, 6, :], ALU.subtract)
                    gstep(v.tensor_tensor(wins[:, :, 2], gt[:, 7, :], gt[:, 8, :], ALU.add))
                    v.tensor_scalar(wins[:, :, 1], wins[:, :, 1], 1.0, None, ALU.add)
                    gstep(v.tensor_scalar(wins[:, :, 2], wins[:, :, 2], -1.0, 2.0, ALU.mult, ALU.add))
                    v.tensor_scalar(rank_hot[:, :, 0, :], wins[:], 2.0, None, ALU.is_equal)
                    v.tensor_scalar(rank_hot[:, :, 1, :], wins[:], 1.0, None, ALU.is_equal).then_inc(ranks_ready, 1)
                    dve.wait_ge(ranks_ready, D)
                    gstep(v.tensor_tensor(picked[:], rank_hot[:], sc[:].unsqueeze(2).broadcast_to([U, 2, 2, NE]), ALU.mult))
                    gstep(v.tensor_reduce(best[:], picked[:], AX.X, ALU.add))
                    gstep(v.tensor_tensor(gt[:, 11, :], best[:, :, 0], best[:, :, 1], ALU.add))
                    gstep(v.tensor_scalar(gt[:, 11, :], gt[:, 11, :], 1e-8, None, ALU.add))
                    gstep(v.reciprocal(gt[:, 12, :], gt[:, 11, :]))
                    gstep(v.tensor_scalar(gt[:, 12, :], gt[:, 12, :], tanh_g[:, 1:2], None, ALU.mult))
                    gstep(v.tensor_tensor(best[:], best[:], gt[:, 12, :].unsqueeze(2).broadcast_to([U, 2, 2]), ALU.mult))
                    split_act(2, act_t)
                    split_act(3, act_t)
                    for i in (4, 5):
                        dve.wait_ge(silu_tanh, 2 * (D - 1) + i - 3)
                        for m in range(2):
                            k = 2 * (i - 4) + m
                            ins = v.tensor_scalar(silu_u[:, i % 2, m, :], bank[BANK[f"up{i}"]][:, m * 2 * U:(m + 1) * 2 * U],
                                                  un_up[:, NE:NE + 1], b1_half[:, k:k + 1], ALU.mult, ALU.add)
                        ins.then_inc(bank_free[BANK[f"up{i}"]], 1)
                        taken(dve, turn, f"up{i}")
                        v.scalar_tensor_tensor(silu_u[:, i % 2], act_t[:, i % 2], 1.0, silu_u[:, i % 2],
                                               ALU.add, ALU.mult).then_inc(acted, 1)
                if turn.kind == "first":
                    split_weights(W1, W2, lambda c: N_W1 + (c - W1) // KC)
                if turn.prev:
                    split_act(4, silu_u)
                    split_act(5, silu_u)
                if turn.prev:
                    free = full(dve, turn, "rank")
                    v.tensor_tensor(coef2[:], bank[BANK["rank"]][0:U, 0:4 * NE].rearrange("p (u r e) -> p u r e", u=2, r=2),
                                    best[:].unsqueeze(3).broadcast_to([U, 2, 2, NE]), ALU.mult).then_inc(free, 1)
                    taken(dve, turn, "rank")
                    v.tensor_tensor(coef[:], coef2[:, :, 0, :], coef2[:, :, 1, :], ALU.add).then_inc(coef_ready, 1)
                    dve.wait_ge(coef_ready, D)
                    gstep(v.tensor_tensor(coef_down[:], coef[:], un_down[0:U, :].unsqueeze(1).broadcast_to([U, 2, NE]), ALU.mult))
                    dve.wait_ge(y_stored, 16 * (D - 1) + 1)
                    carried(dve)
                    for i in range(2 * NE - 1):
                        down(i)
                if turn.this:
                    dve.wait_ge(xr_loaded, 16 * (D + 1))
                    for u in range(2):
                        free = full(dve, turn, f"W{u}")
                        v.scalar_tensor_tensor(x1[:, u, :], bank[BANK[f"W{u}"]][0:U, :], tanh_g[:, 0:1], xr[:, u, :],
                                               ALU.mult, ALU.add).then_inc(free, 1)
                        taken(dve, turn, f"W{u}")
                        norm_stats(u, x1, ln2_st, ln2_mv, ln2_stats, ln2_mean, 2 * D + u + 1)
                if turn.prev:
                    down(2 * NE - 1)
                if turn.this:
                    for u in range(2):
                        dve.wait_ge(ln2_rstd, 2 * D + u + 1)
                        v.tensor_scalar(h[:, u, :], x1[:, u, :], ln2_mv[:, u, 0:1], ln2_r[:, u, 1:2],
                                        ALU.subtract, ALU.mult).then_inc(h_ready, 1)
                if turn.kind == "first":
                    free = full(dve, turn, "norms_down")
                    v.tensor_scalar(sq_all[:, N_W2:NORMS], bank[BANK["norms_down"]][:, 0:NE], TINY, None,
                                    ALU.max).then_inc(free, 1)
                    taken(dve, turn, "norms_down")
                    dve.sem_inc(norms_ready, 1)
                    scales(2, N_W2, NORMS)
                    v.tensor_tensor(un_down[:], unscale[:, N_W2:NORMS], unscale[:, N_ACT:N_W2], ALU.mult).then_inc(scales_ready, 1)
                    split_weights(W2, CHUNKS, lambda c: N_W2 + (c - W2) // KC)
                assert gate_steps[0] == GATE_STEPS * turn.prev

            GATE_STEPS = 20
            over_turns(dve, body)

        @block.tensor
        def _(pe):
            t = nc.tensor
            pe.sem_inc(g_pe, 1)
            pe.wait_ge(setup_pool, 2)
            pe.wait_ge(row_any_ready, 1)
            t.matmul(bank[5][0:U, 0:1], pair_ident[:], row_any_bf[:], start=True, stop=True).then_inc(alive_turned, 1)
            pe.wait_ge(setup_pool, 4)

            def find_window():
                pe.wait_ge(ends_ready, 1)
                for e in range(3):
                    last = t.transpose(bank[7][0:1, e * NQ:(e + 1) * NQ], ends[:, e:e + 1], ident[0:NQ, 0:NQ])
                last.then_inc(ends_turned, 1)

            def transposes(dst, src, rows):
                for k in range(KC):
                    last = t.transpose(dst[:, k * rows:(k + 1) * rows], src[:, k * P:(k + 1) * P], ident[0:rows, 0:rows])
                return last

            def chain(dst, pairs):
                for i, (left, right) in enumerate(pairs):
                    last = t.matmul(dst, left, right, start=i == 0, stop=i == len(pairs) - 1)
                return last

            def split_chain(dst, pairs):
                for i, (left, right) in enumerate(pairs):
                    t.matmul(dst, left(0), right(0), start=i == 0, stop=False)
                    t.matmul(dst, left(0), right(1), start=False, stop=False)
                    last = t.matmul(dst, left(1), right(0), start=False, stop=i == len(pairs) - 1)
                return last

            def score_item(dst, bias, keys, b):
                t.matmul(dst[0:U, :].rearrange("p (t k) -> p t k", k=WIN), pair_ident[:],
                         bias[:].unsqueeze(1).broadcast_to([NQ, HP * J * S, WIN]), start=True, stop=False,
                         skip_group_check=True)
                for hp in range(HP):
                    for j in range(J):
                        c = (hp * J + j) * P
                        last = t.matmul(dst[0:U, c:c + P], QT[:, b, 2 * hp:2 * hp + 2, :].rearrange("p c q -> p (c q)"),
                                        keys[:, b, S * j:S * (j + 1), :], start=False, stop=True, skip_group_check=True)
                return last

            def probs_item(dst, b):
                for i in range(HP * J):
                    last = t.transpose(dst[:, i * U:(i + 1) * U],
                                       probs[:, b, S * i:S * (i + 1), :].rearrange("p s k -> p (s k)"), ident[0:U, 0:U])
                return last

            def output_item(dst, values, b):
                for i in range(HP * J):
                    last = t.matmul(dst[0:U, i * OC:(i + 1) * OC], PT[:, b, i, :], values[:, b, i % J, :], start=True, stop=True)
                return last

            def key_item(dst, turned, context_read=None):
                for k in range(KC):
                    last = t.matmul(dst[:, 0:P], wk_sb[:, k, :], turned[:, k, :], start=k == 0, stop=k == KC - 1)
                    if k == 0 and context_read is not None:
                        last.then_inc(context_read, 1)
                return last

            def value_item(dst, turned):
                return chain(dst[:, 0:P], [(turned[:, k, :], wv_sb[:, k, :]) for k in range(KC)])

            def body(turn):
                D = turn.D

                def item(name):
                    at = turn.before(name)
                    if not (isinstance(at, int) and at == 0):
                        pe.wait_ge(bank_free[BANK[name]], at)
                    return bank[BANK[name]]

                def done(name, ins):
                    ins.then_inc(bank_full[BANK[name]], 1)

                def do_scores(b):
                    done(f"S{b}", score_item(item(f"S{b}"), bias_win, KB, b))

                def do_probs(b):
                    dst = item(f"PT{b}")
                    pe.wait_ge(probs_ready, NB * D + b + 1)
                    done(f"PT{b}", probs_item(dst, b))

                def do_output(b):
                    done(f"O{b}", output_item(item(f"O{b}"), VB, b))

                def do_up(i):
                    dst = item(f"up{i}")
                    e, half = divmod(i, 2)
                    if half == 0:
                        pe.wait_ge(w_lo, W1 + (e + 1) * KC)
                    for m in range(2):
                        k0 = 2 * half + m
                        last = split_chain(dst[:, m * 2 * U:(m + 1) * 2 * U],
                                           [(lambda s, k=k: w_split[:, W1 + e * KC + k, s, k0 * P:(k0 + 1) * P],
                                             lambda s, k=k: hT[:, s, k, :, :].rearrange("p u t -> p (u t)"))
                                            for k in range(KC)])
                    done(f"up{i}", last)

                def do_down(i):
                    u, e = divmod(i, NE)
                    dst = item(f"dn{i}")
                    if u == 0:
                        pe.wait_ge(w_lo, W2 + (e + 1) * KC)
                        pe.wait_ge(act_ready, 6 * (D - 1) + 2 * e + 2)
                    done(f"dn{i}", split_chain(dst[0:U, :], [(lambda s, k=k: act[:, s, e, k, u * U:(u + 1) * U],
                                                              lambda s, k=k: w_split[:, W2 + e * KC + k, s, :])
                                                             for k in range(KC)]))

                def do_queries():
                    for u in range(2):
                        dst = item(f"Q{u}")
                        taken(pe, turn, f"xT{u}")
                        for c in range(HG):
                            last = split_chain(dst[:, c * U:(c + 1) * U],
                                               [(lambda s, k=k: w_split[:, WQ + k, s, c * P:(c + 1) * P],
                                                 lambda s, k=k: xnT[:, s, u, k, :]) for k in range(KC)])
                        done(f"Q{u}", last)

                def do_norms(name, a, b):
                    dst = item(name)
                    pe.wait_ge(norms_summed, b)
                    done(name, t.matmul(dst[:, 0:b - a], ones[:], sq[:, a:b], start=True, stop=True))

                def turn_x():
                    for u in range(2):
                        dst = item(f"xT{u}")
                        pe.wait_ge(xn_ready, 2 * (D + 1) + u + 1)
                        done(f"xT{u}", transposes(dst, xn[:, u, :], U))

                def turn_context():
                    dst = item("ctxT")
                    pe.wait_ge(ctx_loaded, 16 * NB * (D + 2))
                    done("ctxT", transposes(dst, ctx_sb, P))

                def do_keys():
                    dst = item("K")
                    taken(pe, turn, "ctxT")
                    done("K", key_item(dst, ctxT_sb, ctx_read))

                def do_values():
                    dst = item("V")
                    taken(pe, turn, "ctxT")
                    done("V", value_item(dst, ctxT_sb))

                if turn.kind == "lead":
                    do_norms("norms_q", N_Q, N_W1)
                    find_window()
                    turn_x()
                    pe.wait_ge(w_lo, W1)
                    do_queries()
                    pe.wait_ge(verdict_ready, 1)
                    flags.append(pe.value_load(verdict_i[0:1, 1:2], min_val=0, max_val=1))
                    pe.wait_ge(wkv_loaded, 32)
                    turn_context()
                    do_keys()
                    do_values()
                    pe.wait_ge(consts_ready, 1)
                    pe.wait_ge(bias_ready, 1)
                    return

                if turn.next:
                    turn_context()
                if turn.this:
                    for name in ("Q0", "K", "V") + (() if turn.next else ("Q1",)):
                        pe.wait_ge(bank_free[BANK[name]], turn.before(None, BANK[name]))
                    do_scores(0)
                    do_scores(1)
                if turn.prev:
                    for u in range(2):
                        dst = item(f"hT{u}")
                        pe.wait_ge(h_ready, 2 * (D - 1) + u + 1)
                        done(f"hT{u}", transposes(dst, h[:, u, :], U))
                if turn.this:
                    do_scores(2)
                    do_scores(3)
                if turn.next:
                    do_keys()
                if turn.kind == "first":
                    do_norms("norms_up", N_W1, N_W2)
                if turn.prev:
                    dst = item("gate")
                    taken(pe, turn, "hT0")
                    taken(pe, turn, "hT1")
                    pe.wait_ge(h_summed, 2 * D)
                    for u in range(2):
                        split_chain(dst[0:U, u * NE:(u + 1) * NE], [(lambda s, k=k: hT[:, s, k, u, :],
                                                                     lambda s, k=k: gw_split[:, s, k * NE:(k + 1) * NE])
                                                                    for k in range(KC)])
                    t.matmul(dst[0:U, 8:10], text_sel[:].rearrange("p a q -> p (a q)"), h_sum[:], start=True, stop=True)
                    done("gate", t.matmul(dst[0:U, 10:12], vision_sel[:].rearrange("p a q -> p (a q)"), h_sum[:],
                                          start=True, stop=True))
                if turn.prev:
                    do_up(0)
                    do_up(1)
                if turn.this:
                    do_probs(0)
                    do_probs(1)
                if turn.prev:
                    do_up(2)
                if turn.this:
                    do_output(0)
                    do_output(1)
                    do_probs(2)
                    do_probs(3)
                if turn.prev:
                    do_up(3)
                if turn.this:
                    do_output(2)
                    do_output(3)

                    def window(n, first_key, last):
                        pe.wait_ge(g_loaded, 16 * NB * (n + 1))
                        pe.wait_ge(g_dve, n * G_DVE + 1)
                        transposes(bank[0], g_ctx, P).then_inc(g_pe, 1)
                        pe.wait_ge(g_act, n * G_ACT + 1)
                        key_item(bank[1], g_ctxT).then_inc(g_pe, 1)
                        value_item(bank[2], g_ctxT).then_inc(g_pe, 1)
                        pe.wait_ge(g_dve, n * G_DVE + 3)
                        for b in range(NB):
                            score_item(bank[3], g_bias, g_KB, b).then_inc(g_pe, 1)
                            pe.wait_ge(g_act, n * G_ACT + 1 + 2 * b + 2)
                            probs_item(bank[0], b).then_inc(g_pe, 1)
                            pe.wait_ge(g_dve, n * G_DVE + 4 + 6 * b + 5)
                            output_item(bank[1], g_VB, b).then_inc(g_pe, 1)

                    with pe.If(flags[0] > 0):
                        for b in range(NB):
                            taken(pe, turn, f"O{b}")
                        carried(pe)
                        with pe.Fori(0, WINDOWS) as c:
                            window(D * (WINDOWS + 1) + c, c * WIN, False)
                        window(D * (WINDOWS + 1) + WINDOWS, LAST, True)
                        pe.wait_ge(g_dve, (D + 1) * (WINDOWS + 1) * G_DVE + 1)
                        carried(pe)
                if turn.next:
                    turn_x()
                    do_values()
                if turn.prev:
                    do_up(4)
                    do_up(5)
                if turn.next:
                    do_queries()
                if turn.prev:
                    dst = item("rank")
                    pe.wait_ge(ranks_ready, D)
                    done("rank", t.matmul(dst[0:U, 0:4 * NE], first_sel[:].rearrange("p a q -> p (a q)"),
                                          rank_hot[:].rearrange("p u r e -> p (u r e)"), start=True, stop=True))
                    for i in range(3):
                        do_down(i)
                if turn.this:
                    for u in range(2):
                        dst = item(f"OT{u}")
                        pe.wait_ge(on_ready, 2 * D + u + 1)
                        for b in range(2):
                            for hp in range(HP):
                                c = (b * HP + hp) * U
                                last = t.transpose(dst[:, c:c + U],
                                                   On[:, 2 * u + b, J * hp:J * (hp + 1)].rearrange("p t s d -> p (t s d)"),
                                                   ident[0:U, 0:U])
                        done(f"OT{u}", last)
                if turn.prev:
                    do_down(3)
                    do_down(4)
                if turn.this:
                    if turn.kind == "first":
                        pe.wait_ge(wo_loaded, 16)
                    for u in range(2):
                        dst = item(f"W{u}")
                        taken(pe, turn, f"OT{u}")
                        done(f"W{u}", chain(dst[0:U, :], [(OT[:, u, c].rearrange("p b q -> p (b q)"), wo_sb[:, c, :])
                                                          for c in range(HG)]))
                if turn.prev:
                    do_down(5)
                if turn.kind == "first":
                    do_norms("norms_down", N_W2, NORMS)

            flags = []
            over_turns(pe, body)


def kernel(**inputs):
    import numpy as np
    import concourse.bacc as bacc
    from concourse import mybir as mb
    from concourse.bass_utils import run_bass_kernel_spmd as run

    f = {n: np.asarray(a) for n, a in inputs.items()}
    x = f["x"]
    B, NQ, DM = x.shape
    NG, HG, DH = 8, 4, 16
    KC = DM // P

    def rows(a):
        return a.reshape(-1, P, a.shape[-1]).transpose(1, 0, 2)

    arrays = {
        "x": x.reshape(B * NQ, DM),
        "ctx_rows": f["ctx_4096"],
        "mask": f["mask_SxS2_bk0"],
        "g_attn": f["g_xattn"].reshape(1, 1),
        "g_ffn": f["g_ffn"].reshape(1, 1),
        "wq": rows(f["L0_xattn_w_q"].reshape(NG, HG, DH, DM).transpose(3, 1, 0, 2).reshape(DM, DM)),
        "wk": rows(f["L0_xattn_w_k"].T),
        "wv": rows(f["L0_xattn_w_v"].T),
        "wo": f["L0_xattn_w_out"].reshape(DM, NG, HG, DH).transpose(1, 3, 2, 0).reshape(P, HG, DM),
        "gate_w": rows(f["L0_ffn_gate_w"][:DM]).reshape(P, -1),
        "gate_r": f["L0_ffn_gate_w"][DM:],
        "gate_b": f["L0_ffn_gate_b"].reshape(1, -1),
        "w1": f["L0_ffn_w1"].reshape(3 * KC, P, DM).transpose(1, 0, 2),
        "b1": f["L0_ffn_b1"].reshape(3, KC, P).transpose(2, 0, 1),
        "w2": f["L0_ffn_w2"].reshape(3 * KC, P, DM).transpose(1, 0, 2),
        "b2": f["L0_ffn_b2"].reshape(1, -1),
    }
    arrays = {n: np.ascontiguousarray(a) for n, a in arrays.items()}
    nc = bacc.Bacc("TRN2", target_bir_lowering=False, num_devices=1)
    args = [nc.dram_tensor(n, a.shape, mb.dt.from_np(a.dtype), kind="ExternalInput").ap() for n, a in arrays.items()]
    args.append(nc.dram_tensor("out", (B * NQ, DM), mb.dt.float32, kind="ExternalOutput").ap())
    flamingo_block(nc, *args)
    r = run(nc, [arrays], core_ids=[0])
    return r.results[0]["out"].reshape(B, NQ, DM)
```

```python
from contextlib import ExitStack

import concourse.bass as bass
from concourse import mybir

ALU = mybir.AluOpType
ACT = mybir.ActivationFunctionType
AX = mybir.AxisListType
F32 = mybir.dt.float32
BF16 = mybir.dt.bfloat16
I32 = mybir.dt.int32
U8 = mybir.dt.uint8
F16 = mybir.dt.float16
U32 = mybir.dt.uint32

P = 128
WIN = 32
S = P // WIN
LN_EPS = 1e-5
BIG = 1e30

LN_SCALE = 1024.0
TOP_SCALE = 2.0 ** 14
EXPONENT = 0x7F800000
TINY = 1e-30

PLAN = (
    [("ctxT", 6, "next"), ("S0", 0, "this"), ("S1", 1, "this"), ("hT0", 4, "prev"), ("hT1", 5, "prev")]
    + [("S2", 2, "this"), ("S3", 3, "this"), ("K", 7, "next"), ("gate", 6, "prev"), ("up0", 4, "prev"), ("up1", 5, "prev")]
    + [("PT0", 0, "this"), ("PT1", 1, "this"), ("up2", 7, "prev"), ("O0", 0, "this"), ("O1", 1, "this")]
    + [("PT2", 2, "this"), ("PT3", 3, "this"), ("up3", 6, "prev"), ("O2", 2, "this"), ("O3", 3, "this")]
    + [("xT0", 0, "next"), ("xT1", 1, "next"), ("V", 4, "next"), ("norms_up", 5, "prep")]
    + [("up4", 5, "prev"), ("up5", 7, "prev"), ("Q0", 3, "next"), ("Q1", 6, "next"), ("rank", 2, "prev")]
    + [("dn0", 4, "prev"), ("on_norm", 1, "this"), ("dn1", 0, "prev"), ("dn2", 5, "prev"), ("OT0", 0, "this"), ("OT1", 1, "this")]
    + [("dn3", 7, "prev"), ("dn4", 4, "prev"), ("W0", 2, "this"), ("W1", 3, "this"), ("dn5", 5, "prev")]
    + [("norms_down", 6, "prep")]
)
LEAD_PLAN = (
    [("norms_q", 2, "next"), ("xT0", 0, "next"), ("xT1", 1, "next"), ("ctxT", 6, "next"), ("Q0", 3, "next")]
    + [("K", 7, "next"), ("V", 4, "next"), ("Q1", 6, "next")]
)
BANK = {item: bank for item, bank, _ in PLAN + LEAD_PLAN}


def flamingo_block(nc, x, ctx_rows, mask, g_attn, g_ffn, wq, wk, wv, wo, gate_w, gate_r, gate_b, w1, b1, w2, b2, out):
    TOK, DM = x.shape
    NBATCH, KEYS, _ = ctx_rows.shape
    NQ = TOK // NBATCH
    U = 2 * NQ
    DUOS = TOK // (2 * U)
    NB = NBATCH // DUOS
    KC = DM // P
    NG, DH, HG = 8, 16, 4
    J = NG // S
    HP = HG // 2
    HALF = P // J
    OC = S * DH + S
    NE = 3
    VIS = int(NQ * 0.3)
    LAST = KEYS - WIN
    KH = KEYS // 2
    assert NB == 4 and S * J == NG and HP * J * P == 512

    def present(duo_kind, D):
        return {"lead": ("next",), "first": ("this", "next", "prep"), "mid": ("this", "next", "prev"),
                "last": ("this", "prev"), "tail": ("prev",)}[D].count(duo_kind) > 0

    def in_turn(turn, bank, before=None):
        n = 0
        for item, b, kind in (LEAD_PLAN if turn == "lead" else PLAN):
            if item == before:
                break
            n += b == bank and present(kind, turn)
        return n

    class Turn:

        def __init__(self, kind, D, second=False):
            self.kind, self.D, self.second = kind, D, second
            self.this, self.next, self.prev = (present(k, kind) for k in ("this", "next", "prev"))

        def before(self, item, bank=None):
            bank = BANK[item] if item else bank
            at = in_turn(self.kind, bank, item) if item else 0
            if self.kind == "lead":
                return at
            at += in_turn("lead", bank)
            if self.kind == "first":
                return at
            at += in_turn("first", bank)
            if self.kind == "mid":
                return (self.D - 1) * in_turn("mid", bank) + at
            at += (DUOS - 2) * in_turn("mid", bank)
            if self.kind == "last":
                return at
            return at + in_turn("last", bank)

    def over_turns(eng, body):
        body(Turn("lead", -1))
        body(Turn("first", 0))
        body(Turn("mid", 1, second=True))
        with eng.Fori(2, DUOS - 1) as D:
            body(Turn("mid", D))
        body(Turn("last", DUOS - 1))
        body(Turn("tail", DUOS))

    WINDOWS = KEYS // WIN
    OVERLAP = (WINDOWS + 1) * WIN - KEYS
    assert 0 < OVERLAP < WIN

    x_v = x.rearrange("(n u p) d -> n p u d", u=2, p=U)
    out_v = out.rearrange("(n u p) d -> n p u d", u=2, p=U)
    ctx_v = ctx_rows.rearrange("(n b) k d -> n b k d", b=NB)

    with ExitStack() as stack:
        def sb(name, shape, dt=F32):
            return stack.enter_context(nc.sbuf_tensor(name, shape, dt))

        def sem(name):
            return stack.enter_context(nc.semaphore(name))

        bank = [stack.enter_context(nc.psum_tensor(f"bank{i}", [P, 512], F32)) for i in range(8)]

        WQ, WO, W1, W2 = 0, KC, KC + HG, KC + HG + NE * KC
        CHUNKS = W2 + NE * KC
        w_slots = sb("w_slots", [P, CHUNKS + 2, DM])
        wk_sb = sb("wk_sb", [P, KC, P])
        wv_sb = sb("wv_sb", [P, KC, P])
        w_split = w_slots[:].bitcast(F16).rearrange("p c (s n) -> p c s n", s=2)
        b1_sb = sb("b1_sb", [P, NE, KC])
        b1_half = sb("b1_half", [P, KC])
        b2_sb = sb("b2_sb", [U, NE, DM])
        gw_sb = sb("gw_sb", [P, KC * NE])
        gw_split = sb("gw_split", [P, 2, KC * NE], F16)
        N_Q, N_O, N_W1, N_ACT, N_W2, NORMS = 0, 2, 3, 3 + NE, 3 + 2 * NE, 3 + 3 * NE
        sq = sb("sq", [P, NORMS])
        sq_all = sb("sq_all", [P, NORMS])
        root = sb("root", [P, NORMS])
        scale = sb("scale", [P, NORMS])
        unscale = sb("unscale", [P, NORMS])
        un_q = sb("un_q", [P, 2])
        un_up = sb("un_up", [P, NE + 1])
        un_down = sb("un_down", [P, NE])
        un_o = sb("un_o", [P, 1])
        ones = sb("ones", [P, P])
        gr_sb = sb("gr_sb", [U, NE])
        gb_sb = sb("gb_sb", [U, NE])
        gains = sb("gains", [U, 2])
        tanh_g = sb("tanh_g", [U, 2])
        ident = sb("ident", [P, P])
        pair_ident = sb("pair_ident", [NQ, U], BF16)
        half_ident = sb("half_ident", [NQ, J, HALF], BF16)
        group_sel = sb("group_sel", [P, NG])
        s_sel = sb("s_sel", [P, S])
        text_sel = sb("text_sel", [U, 2, NQ])
        vision_sel = sb("vision_sel", [U, 2, NQ])
        first_sel = sb("first_sel", [U, 2, NQ])
        minus_half = sb("minus_half", [P, NORMS])
        eps_col = sb("eps_col", [U, 2])
        early = w_slots[:, W2 + 2:CHUNKS + 2, :].rearrange("p c n -> p (c n)")
        key_up = early[:, 0:KH]
        seen_at = early[:, KH:2 * KH]
        rows_junk = early[0:NQ, 2 * KH:2 * KH + KEYS]
        mask_sb = sb("mask_sb", [HALF + NQ, KEYS], U8)
        mask_halves = sb("mask_halves", [P, KH], U8)
        ends = sb("ends", [P, 3])
        row_count = sb("row_count", [NQ, 1])
        row_any = sb("row_any", [NQ, 1])
        row_any_bf = sb("row_any_bf", [NQ, 1], BF16)
        alive = sb("alive", [U, 1])
        verdict = sb("verdict", [1, 16])
        verdict_i = sb("verdict_i", [1, 2], I32)
        row_any_halves = sb("row_any_halves", [P, 1])
        ctx_sb = sb("ctx_sb", [P, DM])
        ctxT_sb = sb("ctxT_sb", [P, KC, P])
        KB = sb("KB", [P, NB, NG, WIN])
        VB = sb("VB", [P, NB, J, OC])
        x_sb = sb("x_sb", [U, 2, DM])
        ln1_st = sb("ln1_st", [U, 2, 6])
        ln1_mv = sb("ln1_mv", [U, 2, 2])
        ln1_r = sb("ln1_r", [U, 3, 2])
        xn = sb("xn", [U, 2, DM])
        xnT = sb("xnT", [P, 2, KC, 2, U], F16)
        QT = sb("QT", [P, NB, J, HG, NQ])
        top = sb("top", [U, NB, HP * J * S])
        probs = sb("probs", [U, NB, HP * J * S, WIN])
        PT = sb("PT", [P, NB, HP * J, U])
        O_sb = sb("O_sb", [U, NB, HP * J, OC])
        O_rec = sb("O_rec", [U, NB, HP * J, S])
        On = sb("On", [U, NB, HP * J, S, DH])
        on_junk = sb("on_junk", [U, 2, DM], BF16)
        on_sq = sb("on_sq", [U, 2])
        on_all = sb("on_all", [P, 2])
        on_root = sb("on_root", [P, 2])
        on_scale = sb("on_scale", [P, 2])
        un_on = sb("un_on", [P, 2])
        OT = sb("OT", [P, 2, 2, HG, 2, NQ], F16)
        xr = sb("xr", [U, 2, DM])
        x1 = sb("x1", [U, 2, DM])
        ln2_st = sb("ln2_st", [U, 2, 6])
        ln2_mv = sb("ln2_mv", [U, 2, 2])
        ln2_r = sb("ln2_r", [U, 2, 2])
        h = sb("h", [U, 2, DM])
        h_abs = sb("h_abs", [U, 2, DM], BF16)
        h_sum = sb("h_sum", [U, 2])
        hT = sb("hT", [P, 2, KC, 2, U], F16)
        act = sb("act", [P, 2, NE, KC, 2 * U], F16)
        squares = act[:].rearrange("p s e k t -> p (s e k t)").bitcast(F32)
        act_t = sb("act_t", [P, 2, 2, 2 * U])
        silu_u = sb("silu_u", [P, 2, 2, 2 * U])
        gt = sb("gt", [U, 16, 2])
        best = sb("best", [U, 2, 2])
        sc = sb("sc", [U, 2, NE])
        wins = sb("wins", [U, 2, NE])
        rank_hot = sb("rank_hot", [U, 2, 2, NE])
        picked = sb("picked", [U, 2, 2, NE])
        coef2 = sb("coef2", [U, 2, 2, NE])
        coef = sb("coef", [U, 2, NE])
        coef_down = sb("coef_down", [U, 2, NE])
        b2_part = sb("b2_part", [U, 2, DM])
        b2_sum = sb("b2_sum", [U, 2, DM])
        y = sb("y", [U, 2, DM])
        g_ctx = sb("g_ctx", [P, DM])
        g_ctxT = sb("g_ctxT", [P, KC, P])
        g_KB = sb("g_KB", [P, NB, NG, WIN])
        g_VB = sb("g_VB", [P, NB, J, OC])
        g_top = sb("g_top", [U, NB, HP * J * S])
        g_new = sb("g_new", [U, HP * J * S])
        g_decay = sb("g_decay", [U, HP * J * S])

        bank_full = [sem(f"bank_full{i}") for i in range(8)]
        bank_free = [sem(f"bank_free{i}") for i in range(8)]
        mask_loaded = sem("mask_loaded")
        mask_again = sem("mask_again")
        halves_cleared = sem("halves_cleared")
        halves_loaded = sem("halves_loaded")
        rows_counted = sem("rows_counted")
        wkv_loaded = sem("wkv_loaded")
        wq_loaded = sem("wq_loaded")
        wo_loaded = sem("wo_loaded")
        w1_loaded = sem("w1_loaded")
        norms_summed = sem("norms_summed")
        norm_step = sem("norm_step")
        norms_ready = sem("norms_ready")
        roots_ready = sem("roots_ready")
        scales_ready = sem("scales_ready")
        w_hi = sem("w_hi")
        w_lo = sem("w_lo")
        gate_weights = sem("gate_weights")
        xT_hi = sem("xT_hi")
        hT_hi = sem("hT_hi")
        acted = sem("acted")
        act_hi = sem("act_hi")
        w2_loaded = sem("w2_loaded")
        gate_loaded = sem("gate_loaded")
        small_loaded = sem("small_loaded")
        setup_pool = sem("setup_pool")
        consts_ready = sem("consts_ready")
        mask_step = sem("mask_step")
        ends_ready = sem("ends_ready")
        ends_turned = sem("ends_turned")
        verdict_ready = sem("verdict_ready")
        row_any_ready = sem("row_any_ready")
        alive_turned = sem("alive_turned")
        alive_ready = sem("alive_ready")
        bias_ready = sem("bias_ready")
        gains_ready = sem("gains_ready")
        ctx_loaded = sem("ctx_loaded")
        ctx_read = sem("ctx_read")
        x_loaded = sem("x_loaded")
        xr_loaded = sem("xr_loaded")
        ln1_stats = sem("ln1_stats")
        ln1_mean = sem("ln1_mean")
        ln1_step = sem("ln1_step")
        ln1_rstd = sem("ln1_rstd")
        xn_ready = sem("xn_ready")
        top_ready = sem("top_ready")
        probs_ready = sem("probs_ready")
        sums_inverted = sem("sums_inverted")
        on_ready = sem("on_ready")
        on_squared = sem("on_squared")
        on_rooted = sem("on_rooted")
        on_step = sem("on_step")
        on_scaled = sem("on_scaled")
        OT_hi = sem("OT_hi")
        ln2_stats = sem("ln2_stats")
        ln2_mean = sem("ln2_mean")
        ln2_step = sem("ln2_step")
        ln2_rstd = sem("ln2_rstd")
        h_ready = sem("h_ready")
        h_summed = sem("h_summed")
        gate_step = sem("gate_step")
        logits_ready = sem("logits_ready")
        gate_exp = sem("gate_exp")
        ranks_ready = sem("ranks_ready")
        coef_ready = sem("coef_ready")
        silu_tanh = sem("silu_tanh")
        act_ready = sem("act_ready")
        b2_step = sem("b2_step")
        y_ready = sem("y_ready")
        y_stored = sem("y_stored")
        waits_carried = sem("waits_carried")
        g_loaded = sem("g_loaded")
        g_pe = sem("g_pe")
        g_act = sem("g_act")
        g_dve = sem("g_dve")
        g_cleared = sem("g_cleared")
        g_scaled = sem("g_scaled")

        block = stack.enter_context(nc.Block())

        def full(eng, turn, item):
            eng.wait_ge(bank_full[BANK[item]], turn.before(item) + 1)
            return bank_free[BANK[item]]

        def taken(eng, turn, item):
            eng.wait_ge(bank_free[BANK[item]], turn.before(item) + 1)

        def scale_of(c):
            col = N_Q if c < WO else N_O if c < W1 else (N_W1 if c < W2 else N_W2) + (c - W1) // KC % NE
            return scale[:, col:col + 1]

        def own(j):
            return slice(HALF * j, HALF * (j + 1))

        def other(j):
            return slice(HALF * (1 - j), HALF * (1 - j) + NQ)

        G_PE = 3 + 3 * NB
        G_ACT = 1 + 2 * NB
        G_DVE = 3 + 6 * NB

        def carried(eng):
            eng.sem_inc(waits_carried, 1)

        def general(eng, flag, D, body):
            with eng.If(flag > 0):
                with eng.Fori(0, WINDOWS) as c:
                    body(D * (WINDOWS + 1) + c, c * WIN, False)
                body(D * (WINDOWS + 1) + WINDOWS, LAST, True)

        @block.sync
        def _(sp):
            sp.dma_start(x_sb[:], x_v[0]).then_inc(x_loaded, 16)
            sp.dma_start(mask_sb[0:NQ, :], mask).then_inc(mask_loaded, 16)
            sp.wait_ge(halves_cleared, 1)
            for half in range(2):
                sp.dma_start(mask_halves[HALF * half:HALF * half + NQ, :],
                             mask[:, KH * half:KH * (half + 1)]).then_inc(halves_loaded, 16)
            sp.dma_start(w_slots[:, WQ + 2:WO + 2, :], wq).then_inc(wq_loaded, 16)
            sp.dma_start(mask_sb[HALF:HALF + NQ, :], mask).then_inc(mask_again, 16)
            sp.dma_start(wk_sb[:], wk).then_inc(wkv_loaded, 16)
            sp.dma_start(wv_sb[:], wv).then_inc(wkv_loaded, 16)
            for dst, src in ((b1_sb[:], b1), (gr_sb[:], gate_r.broadcast_to([U, NE])),
                             (gb_sb[:], gate_b.broadcast_to([U, NE])), (gains[:, 0:1], g_attn.broadcast_to([U, 1])),
                             (gains[:, 1:2], g_ffn.broadcast_to([U, 1])),
                             (b2_sb[:].rearrange("p e d -> p (e d)"), b2.broadcast_to([U, NE * DM]))):
                sp.dma_start(dst, src).then_inc(small_loaded, 16)
            sp.wait_ge(verdict_ready, 1)
            start = sp.value_load(verdict_i[0:1, 0:1], min_val=0, max_val=LAST)

            def load_context(N):
                for b in range(NB):
                    sp.dma_start(ctx_sb[WIN * b:WIN * (b + 1), :], ctx_v[N, b, bass.ds(start, WIN), :]).then_inc(ctx_loaded, 16)

            def body(turn, ahead=True):
                D = turn.D
                if turn.this:
                    if turn.kind != "first":
                        sp.wait_ge(ln2_stats, 2 * D)
                        carried(sp)
                    sp.dma_start(xr[:], x_v[D]).then_inc(xr_loaded, 16)
                if turn.kind == "first":
                    sp.dma_start(w_slots[:, W1 + 2:W2 + 2, :], w1).then_inc(w1_loaded, 16)
                    sp.dma_start(w_slots[:, W2 + 2:CHUNKS + 2, :], w2).then_inc(w2_loaded, 16)
                if ahead:
                    sp.wait_ge(ctx_read, D + 2)
                    carried(sp)
                    load_context(D + 2)
                    sp.wait_ge(xn_ready, 2 * (D + 2))
                    carried(sp)
                    sp.dma_start(x_sb[:], x_v[D + 2]).then_inc(x_loaded, 16)
                if turn.this:
                    def window(n, first_key, last):
                        sp.wait_ge(g_pe, n * G_PE + 1)
                        carried(sp)
                        for b in range(NB):
                            sp.dma_start(g_ctx[WIN * b:WIN * (b + 1), :],
                                         ctx_v[D, b, bass.ds(first_key, WIN), :]).then_inc(g_loaded, 16)

                    general(sp, flag, D, window)
                if turn.prev:
                    sp.wait_ge(y_ready, 2 * D)
                    carried(sp)
                    sp.dma_start(out_v[D - 1], y[:]).then_inc(y_stored, 16)

            sp.sem_inc(y_stored, 1)
            load_context(0)
            flag = sp.value_load(verdict_i[0:1, 1:2], min_val=0, max_val=1)
            sp.dma_start(w_slots[:, WO + 2:W1 + 2, :], wo).then_inc(wo_loaded, 16)
            body(Turn("lead", -1))
            body(Turn("first", 0))
            with sp.Fori(1, DUOS - 2) as D:
                body(Turn("mid", D))
            body(Turn("mid", DUOS - 2), ahead=False)
            body(Turn("last", DUOS - 1), ahead=False)
            body(Turn("tail", DUOS), ahead=False)
            sp.wait_ge(y_stored, 16 * DUOS + 1)

        @block.gpsimd
        def _(pool):
            steps = [0]
            g = nc.gpsimd

            def norm_one(N):
                pool.wait_ge(ln1_mean, 2 * N + 2)
                g.tensor_tensor(ln1_r[:, 0, :], ln1_mv[:, :, 1], eps_col[:], ALU.add).then_inc(ln1_step, 1)
                pool.wait_ge(ln1_step, 2 * N + 1)
                g.tensor_tensor(ln1_r[:, 1, :], ln1_r[:, 0, :], minus_half[0:U, 0:2], ALU.pow).then_inc(ln1_step, 1)
                pool.wait_ge(ln1_step, 2 * N + 2)
                g.tensor_tensor(ln1_r[:, 2, :], ln1_r[:, 1, :], alive[:].broadcast_to([U, 2]), ALU.mult).then_inc(ln1_rstd, 1)

            def roots(n, a, b):
                pool.wait_ge(norms_ready, n + 1)
                g.tensor_tensor(root[:, a:b], sq_all[:, a:b], minus_half[:, a:b], ALU.pow).then_inc(roots_ready, 1)

            def lead_norm():
                pool.wait_ge(alive_ready, 1)
                norm_one(0)
                roots(0, N_Q, N_O)

            def made(ins):
                steps[0] += 1
                ins.then_inc(setup_pool, 1)
                pool.wait_ge(setup_pool, steps[0])

            def keep(t, op, fill, base, pattern, mult):
                made(g.affine_select(out=t, in_=t, compare_op=op, fill=fill, base=base, pattern=pattern,
                                     channel_multiplier=mult))

            g.memset(mask_halves[:], 0).then_inc(halves_cleared, 1)
            g.memset(minus_half[:], -0.5)
            g.memset(eps_col[:], LN_EPS)
            g.memset(ident[:], 0.0)
            g.memset(ones[:], 1.0)
            g.memset(half_ident[:], 0.0)
            made(g.memset(pair_ident[:], 0.0))
            g.affine_select(out=half_ident[:], in_=half_ident[:], compare_op=ALU.not_equal, fill=1.0, base=0,
                            pattern=[[0, J], [-1, HALF]], channel_multiplier=1)
            keep(pair_ident[:].rearrange("p (a q) -> p a q", a=2), ALU.not_equal, 1.0, 0, [[0, 2], [-1, NQ]], 1)
            made(g.iota(key_up, [[1, KH]], base=1, channel_multiplier=0, allow_small_or_imprecise_dtypes=True))
            keep(ident[:], ALU.not_equal, 1.0, 0, [[-1, P]], 1)
            lead_norm()
            g.memset(group_sel[:], 1.0)
            g.memset(s_sel[:], 1.0)
            g.memset(text_sel[:], 1.0 / ((NQ - VIS) * DM))
            g.memset(vision_sel[:], 1.0 / (VIS * DM))
            g.memset(first_sel[:], 0.0)
            for t in (QT, KB, g_KB, g_VB):
                g.memset(t[:], 0.0)
            made(g.memset(VB[:], 0.0))
            keep(group_sel[:], ALU.is_ge, 0.0, 0, [[-DH, NG]], 1)
            keep(group_sel[:], ALU.is_ge, 0.0, DH - 1, [[DH, NG]], -1)
            keep(s_sel[:], ALU.is_ge, 0.0, 0, [[-WIN, S]], 1)
            keep(s_sel[:], ALU.is_ge, 0.0, WIN - 1, [[WIN, S]], -1)
            keep(text_sel[:], ALU.is_ge, 0.0, -VIS, [[-NQ, 2], [0, NQ]], 1)
            keep(text_sel[:], ALU.is_ge, 0.0, NQ - 1, [[NQ, 2], [0, NQ]], -1)
            keep(vision_sel[:], ALU.is_ge, 0.0, 0, [[-NQ, 2], [0, NQ]], 1)
            keep(vision_sel[:], ALU.is_ge, 0.0, VIS - 1, [[NQ, 2], [0, NQ]], -1)
            keep(first_sel[:], ALU.not_equal, 1.0, 0, [[-NQ, 2], [0, NQ]], 1)
            for values in (g_VB, VB):
                last = g.tensor_copy(values[:, :, :, S * DH:].rearrange("p b j s -> p (b j) s"),
                                     s_sel[:].unsqueeze(1).broadcast_to([P, NB * J, S]))
            last.then_inc(consts_ready, 1)

            def body(turn):
                D = turn.D

                def finish(u):
                    taken(pool, turn, f"dn{NE * u + NE - 1}")
                    g.tensor_tensor(y[:, u, :], y[:, u, :], b2_sum[:, u, :], ALU.add).then_inc(y_ready, 1)

                if turn.next and turn.kind != "lead":
                    norm_one(D + 1)
                if turn.this:
                    for u in range(2):
                        pool.wait_ge(sums_inverted, 2 * D + u + 1)
                        for b in (2 * u, 2 * u + 1):
                            last = g.tensor_tensor(On[:, b],
                                                   O_sb[:, b, :, 0:S * DH].rearrange("p t (s d) -> p t s d", s=S),
                                                   O_rec[:, b].unsqueeze(3).broadcast_to([U, HP * J, S, DH]), ALU.mult)
                        last.then_inc(on_ready, 1)
                    if turn.kind == "first":
                        roots(1, N_O, N_W2)
                    taken(pool, turn, "on_norm")
                    g.tensor_tensor(on_root[:], on_all[:], minus_half[:, 0:2], ALU.pow).then_inc(on_rooted, 1)
                if turn.prev:
                    pool.wait_ge(coef_ready, D)
                    for u in range(2):
                        for e in range(NE):
                            n = 10 * (D - 1) + 5 * u + 2 * e
                            g.tensor_tensor((b2_part if e else b2_sum)[:, u, :], b2_sb[:, e, :],
                                            coef[:, u, e:e + 1].broadcast_to([U, DM]), ALU.mult).then_inc(b2_step, 1)
                            if e == 0:
                                pool.wait_ge(b2_step, n + 1)
                            else:
                                pool.wait_ge(b2_step, n)
                                g.tensor_tensor(b2_sum[:, u, :], b2_sum[:, u, :], b2_part[:, u, :], ALU.add).then_inc(b2_step, 1)
                                pool.wait_ge(b2_step, n + 1)
                    finish(0)
                if turn.this:
                    for u in range(2):
                        pool.wait_ge(ln2_mean, 2 * D + u + 1)
                        g.tensor_tensor(ln2_r[:, u, 0:1], ln2_mv[:, u, 1:2], eps_col[:, 0:1], ALU.add).then_inc(ln2_step, 1)
                        pool.wait_ge(ln2_step, 2 * D + u + 1)
                        g.tensor_tensor(ln2_r[:, u, 1:2], ln2_r[:, u, 0:1], minus_half[0:U, 0:1], ALU.pow).then_inc(ln2_rstd, 1)
                if turn.prev:
                    finish(1)
                if turn.kind == "first":
                    roots(2, N_W2, NORMS)

            over_turns(pool, body)

        @block.scalar
        def _(sca):
            a = nc.scalar
            sca.dma_start(gw_sb[:], gate_w).then_inc(gate_loaded, 16)
            squared = [0]

            def square_sum(col, src):
                n = src.free_size()
                if squared[0]:
                    sca.wait_ge(norms_summed, squared[0])
                a.activation(squares[:, 0:n], src, ACT.Square, accum_out=sq[:, col:col + 1]).then_inc(norms_summed, 1)
                squared[0] += 1

            def slots(c0, n):
                return w_slots[:, c0 + 2:c0 + 2 + n, :].rearrange("p c n -> p (c n)")

            def round_weights(c0, c1, n):
                sca.wait_ge(scales_ready, n)
                for c in range(c0, c1):
                    if c >= 2:
                        sca.wait_ge(w_lo, c - 1)
                    a.activation(w_split[:, c, 0, :], w_slots[:, c + 2, :], ACT.Copy,
                                 scale=scale_of(c)).then_inc(w_hi, 1)

            sca.wait_ge(mask_loaded, 16)
            a.activation(rows_junk, mask_sb[0:NQ, :], ACT.Copy, accum_out=row_count[:]).then_inc(rows_counted, 1)
            sca.wait_ge(rows_counted, 1)
            sca.wait_ge(gate_loaded, 16)
            square_sum(N_Q + 1, gw_sb[:])
            sca.wait_ge(wq_loaded, 16)
            square_sum(N_Q, slots(WQ, KC))
            round_weights(WQ, WO, 1)


            def body(turn):
                D = turn.D

                def exps(b):
                    taken(sca, turn, f"S{b}")
                    a.activation(probs[:, b], probs[:, b], ACT.Exp).then_inc(probs_ready, 1)

                def up(i, func, bias, unscale):
                    full(sca, turn, f"up{i}")
                    if i >= 2:
                        sca.wait_ge(act_ready, 6 * (D - 1) + i - 1)
                    for m in range(2):
                        k = 2 * (i % 2) + m
                        ins = a.activation(act_t[:, i % 2, m, :], bank[BANK[f"up{i}"]][:, m * 2 * U:(m + 1) * 2 * U], func,
                                           bias=bias[:, k:k + 1], scale=unscale)
                    return ins

                def round_act(i, src):
                    e, half = divmod(i, 2)
                    a.activation(act[:, 0, e, 2 * half:2 * half + 2, :].rearrange("p m t -> p (m t)"),
                                 src[:, i % 2].rearrange("p m t -> p (m t)"), ACT.Copy,
                                 scale=scale[:, N_ACT + e:N_ACT + e + 1]).then_inc(act_hi, 1)

                def turned_x():
                    for u in range(2):
                        full(sca, turn, f"xT{u}")
                        a.activation(xnT[:, 0, :, u, :], bank[BANK[f"xT{u}"]][:, 0:KC * U].rearrange("p (k t) -> p k t", k=KC),
                                     ACT.Copy, scale=LN_SCALE).then_inc(xT_hi, 1)

                def on_squares():
                    for u in range(2):
                        sca.wait_ge(on_ready, 2 * D + u + 1)
                        a.activation(on_junk[:, u, :], On[:, 2 * u:2 * u + 2].rearrange("p b t s d -> p (b t s d)"),
                                     ACT.Square, accum_out=on_sq[:, u:u + 1]).then_inc(on_squared, 1)

                def queries():
                    for i in range(2):
                        free = full(sca, turn, f"Q{i}")
                        for j in range(J):
                            last = a.activation(QT[own(j), :, j, 2 * i:2 * i + 2, :].rearrange("p b c q -> p c b q"),
                                                bank[BANK[f"Q{i}"]][own(j), 0:4 * U].rearrange("p (c b q) -> p c b q", c=2, b=NB),
                                                ACT.Copy, scale=un_q[own(j), 0:1])
                        last.then_inc(free, 1)

                if turn.kind == "lead":
                    turned_x()
                    sca.wait_ge(small_loaded, 16 * 6)
                    a.activation(tanh_g[:], gains[:], ACT.Tanh).then_inc(gains_ready, 1)
                    a.activation(b1_half[:], b1_sb[:, 2, :], ACT.Copy, scale=0.5).then_inc(gains_ready, 1)
                    sca.wait_ge(verdict_ready, 1)
                    flags.append(sca.value_load(verdict_i[0:1, 1:2], min_val=0, max_val=1))
                if turn.next:
                    free = full(sca, turn, "ctxT")
                    a.activation(ctxT_sb[:].rearrange("p k n -> p (k n)"), bank[BANK["ctxT"]][:], ACT.Copy).then_inc(free, 1)
                if turn.kind == "lead":
                    sca.wait_ge(consts_ready, 1)
                    for j in range(J):
                        r = other(j)
                        a.activation(QT[r, :, j, :, :], ident[r, r].unsqueeze(1).unsqueeze(1).broadcast_to([NQ, NB, HG, NQ]),
                                     ACT.Copy)
                    queries()
                if turn.prev:
                    for u in range(2):
                        full(sca, turn, f"hT{u}")
                        a.activation(hT[:, 0, :, u, :], bank[BANK[f"hT{u}"]][:, 0:KC * U].rearrange("p (k t) -> p k t", k=KC),
                                     ACT.Copy, scale=LN_SCALE).then_inc(hT_hi, 1)
                if turn.this:
                    exps(0)
                    exps(1)
                if turn.prev:
                    for i in (0, 1):
                        up(i, ACT.Tanh, b1_sb[:, 0, :], un_up[:, 0:1]).then_inc(bank_free[BANK[f"up{i}"]], 1)
                    for i in (0, 1):
                        taken(sca, turn, f"up{i}")
                        round_act(i, act_t)
                if turn.this:
                    exps(2)
                    exps(3)
                if turn.second:
                    round_weights(W1 + 2 * KC, W2, 2)
                if turn.kind == "first":
                    sca.wait_ge(wo_loaded, 16)
                    square_sum(N_O, slots(WO, HG))
                    sca.wait_ge(w1_loaded, 16)
                    for e in range(NE):
                        square_sum(N_ACT + e, b1_sb[:, e, :])
                    for e in range(NE - 1):
                        square_sum(N_W1 + e, slots(W1 + e * KC, KC))
                if turn.prev:
                    sca.wait_ge(logits_ready, D)
                    a.activation(sc[:], sc[:], ACT.Exp).then_inc(gate_exp, 1)
                if turn.second:
                    round_weights(W2, W2 + KC, 3)
                if turn.this:
                    def window(n, first_key, last):
                        sca.wait_ge(g_pe, n * G_PE + 2)
                        a.activation(g_ctxT[:].rearrange("p k n -> p (k n)"), bank[0][:], ACT.Copy).then_inc(g_act, 1)
                        for b in range(NB):
                            sca.wait_ge(g_dve, n * G_DVE + 3 + 6 * b + 5)
                            a.activation(g_decay[:], g_decay[:], ACT.Exp).then_inc(g_act, 1)
                            a.activation(probs[:, b], probs[:, b], ACT.Exp).then_inc(g_act, 1)

                    general(sca, flags[0], D, window)
                if turn.prev:
                    for i in (2, 3):
                        up(i, ACT.Gelu, b1_sb[:, 1, :], un_up[:, 1:2]).then_inc(bank_free[BANK[f"up{i}"]], 1)
                    for i in (2, 3):
                        taken(sca, turn, f"up{i}")
                        round_act(i, act_t)
                if turn.second:
                    round_weights(W2 + KC, W2 + 2 * KC, 3)
                if turn.next and turn.kind != "lead":
                    turned_x()
                if turn.prev:
                    for i in (4, 5):
                        up(i, ACT.Tanh, b1_half, un_up[:, NE:NE + 1]).then_inc(silu_tanh, 1)
                if turn.this and turn.kind != "first":
                    on_squares()
                if turn.second:
                    round_weights(W2 + 2 * KC, CHUNKS, 3)
                if turn.prev:
                    for i in (4, 5):
                        sca.wait_ge(acted, 2 * (D - 1) + i - 3)
                        round_act(i, silu_u)
                if turn.kind == "first":
                    square_sum(N_W1 + NE - 1, slots(W1 + (NE - 1) * KC, KC))
                    on_squares()
                    sca.wait_ge(w2_loaded, 16)
                    square_sum(N_W2, slots(W2, KC))
                    round_weights(WO, W1, 2)
                if turn.next and turn.kind == "mid":
                    queries()
                if turn.this:
                    sca.wait_ge(on_scaled, D + 1)
                    for u in range(2):
                        full(sca, turn, f"OT{u}")
                        for b in range(2):
                            last = a.activation(OT[:, 0, u, :, b, :],
                                                bank[BANK[f"OT{u}"]][:, b * HG * NQ:(b + 1) * HG * NQ].rearrange("p (c q) -> p c q", c=HG),
                                                ACT.Copy, scale=on_scale[:, u:u + 1])
                        last.then_inc(OT_hi, 1)
                if turn.kind == "first":
                    queries()
                    round_weights(W1, W1 + KC, 2)
                    for e in range(1, NE):
                        square_sum(N_W2 + e, slots(W2 + e * KC, KC))
                if turn.this:
                    for u in range(2):
                        sca.wait_ge(h_ready, 2 * D + u + 1)
                        a.activation(h_abs[:, u, :], h[:, u, :], ACT.Abs, accum_out=h_sum[:, u:u + 1]).then_inc(h_summed, 1)
                if turn.kind == "first":
                    round_weights(W1 + KC, W1 + 2 * KC, 2)

            flags = []
            over_turns(sca, body)

        @block.vector
        def _(dve):
            v = nc.vector
            dve.sem_inc(g_dve, 1)
            steps = [0]

            def step(ins):
                steps[0] += 1
                ins.then_inc(mask_step, 1)
                dve.wait_ge(mask_step, steps[0])

            def norm_stats(u, src, st, mv, stats, mean, n):
                v.bn_stats(st[:, u, :], src[:, u, :]).then_inc(stats, 1)
                dve.wait_ge(stats, n)
                carried(dve)
                v.bn_aggr(mv[:, u, :], st[:, u, :]).then_inc(mean, 1)

            norm_steps = [0]

            def nstep(ins):
                norm_steps[0] += 1
                ins.then_inc(norm_step, 1)
                dve.wait_ge(norm_step, norm_steps[0])

            def scales(n, a, b):
                dve.wait_ge(roots_ready, n + 1)
                nstep(v.tensor_scalar(scale[:, a:b].bitcast(U32), root[:, a:b].bitcast(U32), EXPONENT, None, ALU.bitwise_and))
                nstep(v.tensor_scalar(scale[:, a:b], scale[:, a:b], TOP_SCALE, None, ALU.mult))
                nstep(v.reciprocal(unscale[:, a:b], scale[:, a:b]))

            def split_weights(c0, c1):
                for c in range(c0, c1):
                    dve.wait_ge(w_hi, c + 1)
                    v.scalar_tensor_tensor(w_split[:, c, 1, :], w_slots[:, c + 2, :], scale_of(c),
                                           w_split[:, c, 0, :], ALU.mult, ALU.subtract).then_inc(w_lo, 1)

            def normalise(N):
                dve.wait_ge(ln1_rstd, N + 1)
                for u in range(2):
                    v.tensor_scalar(xn[:, u, :], x_sb[:, u, :], ln1_mv[:, u, 0:1], ln1_r[:, 2, u:u + 1],
                                    ALU.subtract, ALU.mult).then_inc(xn_ready, 1)

            lead = Turn("lead", -1)
            v.memset(ends[:], -1.0)
            dve.wait_ge(x_loaded, 16)
            norm_stats(0, x_sb, ln1_st, ln1_mv, ln1_stats, ln1_mean, 1)
            dve.wait_ge(halves_loaded, 32)
            dve.wait_ge(setup_pool, 3)
            step(v.scalar_tensor_tensor(seen_at, key_up, float(-KH - 1), mask_halves[:], ALU.add, ALU.mult))
            step(v.tensor_reduce(ends[:, 0:1], seen_at, AX.X, ALU.min))
            dve.wait_ge(rows_counted, 1)
            step(v.tensor_scalar(row_any[:], row_count[:], 0.0, None, ALU.is_gt))
            v.tensor_copy(row_any_bf[:], row_any[:]).then_inc(row_any_ready, 1)
            v.tensor_scalar(ends[0:NQ, 2:3], row_any[:], -1.0, None, ALU.mult)
            norm_stats(1, x_sb, ln1_st, ln1_mv, ln1_stats, ln1_mean, 2)
            dve.wait_ge(alive_turned, 1)
            v.tensor_copy(row_any_halves[:], bank[5][:, 1:2])
            v.tensor_copy(alive[:], bank[5][0:U, 0:1]).then_inc(alive_ready, 1)
            step(v.tensor_tensor(seen_at, mask_halves[:], key_up, ALU.mult))
            free = full(dve, lead, "norms_q")
            v.tensor_scalar(sq_all[:, N_Q:N_O], bank[BANK["norms_q"]][:, 0:2], TINY, None, ALU.max).then_inc(free, 1)
            taken(dve, lead, "norms_q")
            dve.sem_inc(norms_ready, 1)
            step(v.tensor_reduce(ends[:, 1:2], seen_at, AX.X, ALU.max))
            v.tensor_scalar(ends[:, 0:1], ends[:, 0:1], -1.0, None, ALU.mult)
            v.memset(verdict[:], 0.0).then_inc(ends_ready, 1)
            scales(0, N_Q, N_O)
            v.tensor_scalar(un_q[:, 0:1], unscale[:, N_Q:N_Q + 1], DH ** -0.5 / LN_SCALE, None, ALU.mult)
            v.tensor_scalar(un_q[:, 1:2], unscale[:, N_Q + 1:N_Q + 2], 1.0 / LN_SCALE, None, ALU.mult).then_inc(scales_ready, 1)
            normalise(0)
            dve.wait_ge(ends_turned, 1)
            step(v.tensor_reduce(verdict[:, 0:6], bank[7][0:1, 0:3 * P].rearrange("p (e q) -> p e q", q=HALF), AX.X, ALU.max))
            outer, inner, both = verdict[:, 0:4:3], verdict[:, 1:3], verdict[:, 6:8]
            step(v.tensor_scalar(both, outer, 0.0, float(KH), ALU.is_gt, ALU.mult))
            step(v.tensor_tensor(both, both, outer, ALU.add))
            step(v.tensor_tensor(both, both, inner, ALU.max))
            v.tensor_scalar(verdict[:, 8:9], verdict[:, 6:7], -1.0, float(KEYS), ALU.mult, ALU.add)
            v.tensor_scalar(verdict[:, 11:12], verdict[:, 4:5], 1.0, None, ALU.add)
            step(v.tensor_tensor(verdict[:, 10:11], verdict[:, 6:7], verdict[:, 7:8], ALU.add))
            v.tensor_scalar(verdict[:, 9:10], verdict[:, 8:9], float(LAST), None, ALU.min)
            step(v.tensor_scalar(verdict[:, 12:13], verdict[:, 10:11], float(-KEYS - WIN), None, ALU.add))
            step(v.tensor_tensor(verdict[:, 13:14], verdict[:, 12:13], verdict[:, 11:12], ALU.max))
            step(v.tensor_scalar(verdict[:, 14:15], verdict[:, 13:14], 0.0, None, ALU.is_gt))
            v.tensor_copy(verdict_i[:, 0:1], verdict[:, 9:10])
            v.tensor_copy(verdict_i[:, 1:2], verdict[:, 14:15]).then_inc(verdict_ready, 1)
            def take_bias(dst, first_key):
                for j in range(J):
                    r = other(j)
                    last = v.tensor_scalar(dst[r, :, S * j:S * (j + 1), :],
                                           mask_sb[r, bass.ds(first_key, WIN)].unsqueeze(1).unsqueeze(1)
                                           .broadcast_to([NQ, NB, S, WIN]), row_any_halves[r, 0:1], BIG, ALU.subtract, ALU.mult)
                return last

            split_weights(WQ, WO)

            def turned_x(turn):
                for u in range(2):
                    free = full(dve, turn, f"xT{u}")
                    dve.wait_ge(xT_hi, 2 * (turn.D + 1) + u + 1)
                    v.scalar_tensor_tensor(xnT[:, 1, :, u, :], bank[BANK[f"xT{u}"]][:, 0:KC * U].rearrange("p (k t) -> p k t", k=KC),
                                           LN_SCALE, xnT[:, 0, :, u, :], ALU.mult, ALU.subtract).then_inc(free, 1)

            turned_x(lead)
            dve.wait_ge(verdict_ready, 1)
            start = dve.value_load(verdict_i[0:1, 0:1], min_val=0, max_val=LAST)
            flag = dve.value_load(verdict_i[0:1, 1:2], min_val=0, max_val=1)

            dve.wait_ge(alive_ready, 1)
            dve.wait_ge(mask_again, 16)
            dve.wait_ge(consts_ready, 1)
            take_bias(KB, start).then_inc(bias_ready, 1)

            def spread_keys(dst, src):
                for j in range(J):
                    r = own(j)
                    last = v.tensor_tensor(dst[r, :, S * j:S * (j + 1), :],
                                           src[r, 0:P].rearrange("p (b k) -> p b k", b=NB).unsqueeze(2)
                                           .broadcast_to([HALF, NB, S, WIN]),
                                           group_sel[r, S * j:S * (j + 1)].unsqueeze(1).unsqueeze(3)
                                           .broadcast_to([HALF, NB, S, WIN]), ALU.mult)
                return last

            def spread_values(dst, src):
                src = src[:, 0:P].rearrange("p (j s d) -> p j s d", j=J, s=S)
                for b in range(NB):
                    for s in range(S):
                        last = v.tensor_copy(dst[WIN * s:WIN * (s + 1), b, :, DH * s:DH * (s + 1)],
                                             src[WIN * b:WIN * (b + 1), :, s, :])
                return last

            def body(turn):
                D = turn.D

                def scores(b):
                    src = bank[b][0:U, :].rearrange("p (t k) -> p t k", k=WIN)
                    free = full(dve, turn, f"S{b}")
                    v.tensor_reduce(top[:, b, :], src, AX.X, ALU.max).then_inc(top_ready, 1)
                    dve.wait_ge(top_ready, NB * D + b + 1)
                    v.tensor_tensor(probs[:, b], src, top[:, b, :].unsqueeze(2).broadcast_to([U, HP * J * S, WIN]),
                                    ALU.subtract).then_inc(free, 1)

                def take_probs(b):
                    free = full(dve, turn, f"PT{b}")
                    v.tensor_copy(PT[:, b].rearrange("p t q -> p (t q)"), bank[b][:, 0:HP * J * U]).then_inc(free, 1)

                def take_output(b):
                    free = full(dve, turn, f"O{b}")
                    v.tensor_copy(O_sb[:, b].rearrange("p t c -> p (t c)"), bank[b][0:U, 0:HP * J * OC]).then_inc(free, 1)

                def down(i):
                    u, e = divmod(i, NE)
                    free = full(dve, turn, f"dn{i}")
                    if e:
                        taken(dve, turn, f"dn{i - 1}")
                    v.scalar_tensor_tensor(y[:, u, :], bank[BANK[f"dn{i}"]][0:U, :], coef_down[:, u, e:e + 1],
                                           (y if e else x1)[:, u, :],
                                           ALU.mult, ALU.add).then_inc(free, 1)

                def next_keys():
                    free = full(dve, turn, "K")
                    spread_keys(KB, bank[BANK["K"]]).then_inc(free, 1)

                def next_values():
                    free = full(dve, turn, "V")
                    spread_values(VB, bank[BANK["V"]]).then_inc(free, 1)

                def split_act(i, src):
                    e, half = divmod(i, 2)
                    hi, lo = (act[:, s, e, 2 * half:2 * half + 2, :].rearrange("p m t -> p (m t)") for s in range(2))
                    dve.wait_ge(act_hi, 6 * (D - 1) + i + 1)
                    v.scalar_tensor_tensor(lo, src[:, i % 2].rearrange("p m t -> p (m t)"), scale[:, N_ACT + e:N_ACT + e + 1],
                                           hi, ALU.mult, ALU.subtract).then_inc(act_ready, 1)

                if turn.kind == "lead":
                    nstep(v.tensor_scalar(gw_split[:, 0, :], gw_sb[:], scale[:, N_Q + 1:N_Q + 2], None, ALU.mult))
                    v.scalar_tensor_tensor(gw_split[:, 1, :], gw_sb[:], scale[:, N_Q + 1:N_Q + 2], gw_split[:, 0, :],
                                           ALU.mult, ALU.subtract).then_inc(gate_weights, 1)
                    dve.wait_ge(consts_ready, 1)
                    next_keys()
                    next_values()

                def next_stats():
                    N = D + 1
                    dve.wait_ge(x_loaded, 16 * (N + 1))
                    for u in range(2):
                        norm_stats(u, x_sb, ln1_st, ln1_mv, ln1_stats, ln1_mean, 2 * N + u + 1)

                def attention_norm():
                    free = full(dve, turn, "on_norm")
                    v.tensor_scalar(on_all[:], bank[BANK["on_norm"]][:, 0:2], TINY, None, ALU.max).then_inc(free, 1)

                def attention_scale():
                    dve.wait_ge(on_rooted, D + 1)
                    v.tensor_scalar(on_scale[:].bitcast(U32), on_root[:].bitcast(U32), EXPONENT, None,
                                    ALU.bitwise_and).then_inc(on_step, 1)
                    dve.wait_ge(on_step, 3 * D + 1)
                    v.tensor_scalar(on_scale[:], on_scale[:], TOP_SCALE, None, ALU.mult).then_inc(on_step, 1)
                    dve.wait_ge(on_step, 3 * D + 2)
                    v.reciprocal(un_on[:], on_scale[:]).then_inc(on_step, 1)
                    dve.wait_ge(on_step, 3 * D + 3)
                    v.tensor_scalar(un_on[0:U, :], un_on[0:U, :], un_o[0:U, 0:1], None, ALU.mult).then_inc(on_scaled, 1)

                gate_steps = [0]

                def gstep(ins):
                    gate_steps[0] += 1
                    ins.then_inc(gate_step, 1)
                    dve.wait_ge(gate_step, GATE_STEPS * (D - 1) + gate_steps[0])

                if turn.this:
                    scores(0)
                    scores(1)
                if turn.prev:
                    for u in range(2):
                        free = full(dve, turn, f"hT{u}")
                        dve.wait_ge(hT_hi, 2 * (D - 1) + u + 1)
                        v.scalar_tensor_tensor(hT[:, 1, :, u, :],
                                               bank[BANK[f"hT{u}"]][:, 0:KC * U].rearrange("p (k t) -> p k t", k=KC),
                                               LN_SCALE, hT[:, 0, :, u, :], ALU.mult, ALU.subtract).then_inc(free, 1)
                if turn.this:
                    scores(2)
                    scores(3)
                if turn.prev:
                    free = full(dve, turn, "gate")
                    src = bank[BANK["gate"]]
                    gstep(v.tensor_scalar(gt[:, 0, :], src[0:U, 10:12], 1e-8, None, ALU.add))
                    gstep(v.reciprocal(gt[:, 1, :], gt[:, 0, :]))
                    gstep(v.tensor_tensor(gt[:, 2, :], src[0:U, 8:10], gt[:, 1, :], ALU.mult))
                    gstep(v.tensor_tensor(sc[:], gt[:, 2, :].unsqueeze(2).broadcast_to([U, 2, NE]),
                                          gr_sb[:].unsqueeze(1).broadcast_to([U, 2, NE]), ALU.mult))
                    v.scalar_tensor_tensor(sc[:], src[0:U, 0:2 * NE].rearrange("p (u e) -> p u e", u=2), un_q[0:U, 1:2],
                                           sc[:], ALU.mult, ALU.add).then_inc(free, 1)
                    taken(dve, turn, "gate")
                    gstep(v.tensor_tensor(sc[:], sc[:], gb_sb[:].unsqueeze(1).broadcast_to([U, 2, NE]), ALU.add))
                    gstep(v.tensor_reduce(gt[:, 3, :], sc[:], AX.X, ALU.max))
                    v.tensor_tensor(sc[:], sc[:], gt[:, 3, :].unsqueeze(2).broadcast_to([U, 2, NE]),
                                    ALU.subtract).then_inc(logits_ready, 1)
                if turn.next and turn.kind == "mid":
                    next_keys()
                    next_stats()
                if turn.this:
                    take_probs(0)
                    take_probs(1)
                    take_output(0)
                    take_output(1)
                if turn.kind == "first":
                    next_stats()
                if turn.second:
                    split_weights(W1 + 2 * KC, W2)
                if turn.this:
                    take_probs(2)
                    take_probs(3)
                if turn.second:
                    split_weights(W2, W2 + KC)
                if turn.next and turn.kind != "lead":
                    normalise(D + 1)
                if turn.prev:
                    split_act(0, act_t)
                    split_act(1, act_t)
                if turn.this:
                    take_output(2)
                    take_output(3)
                    taken(dve, turn, "O2")
                    taken(dve, turn, "O3")
                    carried(dve)

                    def window(n, first_key, last):
                        k = [0]

                        def gdo(ins, wait=True):
                            k[0] += 1
                            ins.then_inc(g_dve, 1)
                            if wait:
                                dve.wait_ge(g_dve, n * G_DVE + k[0] + 1)

                        if last:
                            take_bias(g_KB, first_key).then_inc(bias_ready, 1)
                            dve.wait_ge(bias_ready, D + 2)
                            for j in range(J):
                                ins = v.memset(g_KB[other(j), :, S * j:S * (j + 1), 0:OVERLAP], -BIG)
                            gdo(ins)
                        else:
                            gdo(take_bias(g_KB, first_key))
                        dve.wait_ge(g_pe, n * G_PE + 3)
                        gdo(spread_keys(g_KB, bank[1]))
                        dve.wait_ge(g_pe, n * G_PE + 4)
                        gdo(spread_values(g_VB, bank[2]))
                        for b in range(NB):
                            src = bank[3][0:U, :].rearrange("p (t k) -> p t k", k=WIN)
                            dve.wait_ge(g_pe, n * G_PE + 4 + 3 * b + 1)
                            gdo(v.tensor_reduce(g_new[:], src, AX.X, ALU.max))
                            gdo(v.tensor_tensor(g_new[:], g_new[:], g_top[:, b, :], ALU.max))
                            gdo(v.tensor_tensor(g_decay[:], g_top[:, b, :], g_new[:], ALU.subtract))
                            v.tensor_copy(g_top[:, b, :], g_new[:])
                            gdo(v.tensor_tensor(probs[:, b], src, g_new[:].unsqueeze(2).broadcast_to([U, HP * J * S, WIN]),
                                                ALU.subtract))
                            dve.wait_ge(g_pe, n * G_PE + 4 + 3 * b + 2)
                            gdo(v.tensor_copy(PT[:, b].rearrange("p t q -> p (t q)"), bank[0][:, 0:HP * J * U]))
                            dve.wait_ge(g_act, n * G_ACT + 1 + 2 * b + 1)
                            for t in range(HP * J):
                                v.tensor_tensor(O_sb[:, b, t, 0:S * DH].rearrange("p (s d) -> p s d", s=S),
                                                O_sb[:, b, t, 0:S * DH].rearrange("p (s d) -> p s d", s=S),
                                                g_decay[:, S * t:S * (t + 1)].unsqueeze(2).broadcast_to([U, S, DH]), ALU.mult)
                            v.tensor_tensor(O_sb[:, b, :, S * DH:], O_sb[:, b, :, S * DH:],
                                            g_decay[:].rearrange("p (t s) -> p t s", s=S), ALU.mult).then_inc(g_scaled, 1)
                            dve.wait_ge(g_scaled, n * NB + b + 1)
                            dve.wait_ge(g_pe, n * G_PE + 4 + 3 * b + 3)
                            gdo(v.tensor_tensor(O_sb[:, b].rearrange("p t c -> p (t c)"), O_sb[:, b].rearrange("p t c -> p (t c)"),
                                                bank[1][0:U, 0:HP * J * OC], ALU.add))
                        carried(dve)
                        assert k[0] == G_DVE

                    with dve.If(flag > 0):
                        v.memset(g_top[:], -3e38)
                        v.memset(O_sb[:], 0.0).then_inc(g_cleared, 1)
                        dve.wait_ge(g_cleared, D + 1)
                        carried(dve)
                        with dve.Fori(0, WINDOWS) as c:
                            window(D * (WINDOWS + 1) + c, c * WIN, False)
                        window(D * (WINDOWS + 1) + WINDOWS, LAST, True)
                    for u in range(2):
                        v.reciprocal(O_rec[:, 2 * u:2 * u + 2].rearrange("p b t s -> p (b t) s"),
                                     O_sb[:, 2 * u:2 * u + 2, :, S * DH:].rearrange("p b t s -> p (b t) s")).then_inc(sums_inverted, 1)
                if turn.kind == "first":
                    next_keys()
                if turn.second:
                    split_weights(W2 + KC, W2 + 2 * KC)
                if turn.next and turn.kind != "lead":
                    turned_x(turn)
                    next_values()
                if turn.prev:
                    dve.wait_ge(gate_exp, D)
                    gstep(v.tensor_reduce(gt[:, 4, :], sc[:], AX.X, ALU.add))
                    gstep(v.reciprocal(gt[:, 5, :], gt[:, 4, :]))
                    gstep(v.tensor_tensor(sc[:], sc[:], gt[:, 5, :].unsqueeze(2).broadcast_to([U, 2, NE]), ALU.mult))
                    v.tensor_tensor(gt[:, 6, :], sc[:, :, 0], sc[:, :, 1], ALU.is_ge)
                    v.tensor_tensor(gt[:, 7, :], sc[:, :, 1], sc[:, :, 2], ALU.is_ge)
                    gstep(v.tensor_tensor(gt[:, 8, :], sc[:, :, 0], sc[:, :, 2], ALU.is_ge))
                    v.tensor_tensor(wins[:, :, 0], gt[:, 6, :], gt[:, 8, :], ALU.add)
                    v.tensor_tensor(wins[:, :, 1], gt[:, 7, :], gt[:, 6, :], ALU.subtract)
                    gstep(v.tensor_tensor(wins[:, :, 2], gt[:, 7, :], gt[:, 8, :], ALU.add))
                    v.tensor_scalar(wins[:, :, 1], wins[:, :, 1], 1.0, None, ALU.add)
                    gstep(v.tensor_scalar(wins[:, :, 2], wins[:, :, 2], -1.0, 2.0, ALU.mult, ALU.add))
                    v.tensor_scalar(rank_hot[:, :, 0, :], wins[:], 2.0, None, ALU.is_equal)
                    v.tensor_scalar(rank_hot[:, :, 1, :], wins[:], 1.0, None, ALU.is_equal).then_inc(ranks_ready, 1)
                    dve.wait_ge(ranks_ready, D)
                    gstep(v.tensor_tensor(picked[:], rank_hot[:], sc[:].unsqueeze(2).broadcast_to([U, 2, 2, NE]), ALU.mult))
                    gstep(v.tensor_reduce(best[:], picked[:], AX.X, ALU.add))
                    gstep(v.tensor_tensor(gt[:, 11, :], best[:, :, 0], best[:, :, 1], ALU.add))
                    gstep(v.tensor_scalar(gt[:, 11, :], gt[:, 11, :], 1e-8, None, ALU.add))
                    gstep(v.reciprocal(gt[:, 12, :], gt[:, 11, :]))
                    gstep(v.tensor_scalar(gt[:, 12, :], gt[:, 12, :], tanh_g[:, 1:2], None, ALU.mult))
                    gstep(v.tensor_tensor(best[:], best[:], gt[:, 12, :].unsqueeze(2).broadcast_to([U, 2, 2]), ALU.mult))
                    split_act(2, act_t)
                    split_act(3, act_t)
                    for i in (4, 5):
                        dve.wait_ge(silu_tanh, 2 * (D - 1) + i - 3)
                        for m in range(2):
                            k = 2 * (i - 4) + m
                            ins = v.tensor_scalar(silu_u[:, i % 2, m, :], bank[BANK[f"up{i}"]][:, m * 2 * U:(m + 1) * 2 * U],
                                                  un_up[:, NE:NE + 1], b1_half[:, k:k + 1], ALU.mult, ALU.add)
                        ins.then_inc(bank_free[BANK[f"up{i}"]], 1)
                        taken(dve, turn, f"up{i}")
                        v.scalar_tensor_tensor(silu_u[:, i % 2], act_t[:, i % 2], 1.0, silu_u[:, i % 2],
                                               ALU.add, ALU.mult).then_inc(acted, 1)
                if turn.kind == "first":
                    free = full(dve, turn, "norms_up")
                    src = bank[BANK["norms_up"]]
                    v.tensor_scalar(sq_all[:, N_O:N_ACT], src[:, 0:1 + NE], TINY, None, ALU.max)
                    nstep(v.tensor_scalar(sq_all[:, N_ACT:N_W2], src[:, 1:1 + NE], 2.0 * DM, None, ALU.mult))
                    v.scalar_tensor_tensor(sq_all[:, N_ACT:N_W2], src[:, 1 + NE:1 + 2 * NE], 2.0, sq_all[:, N_ACT:N_W2],
                                           ALU.mult, ALU.add).then_inc(free, 1)
                    taken(dve, turn, "norms_up")
                    nstep(v.tensor_scalar(sq_all[:, N_ACT:N_W2], sq_all[:, N_ACT:N_W2], TINY, None, ALU.max))
                    v.tensor_scalar(sq_all[:, N_ACT:N_ACT + 1], sq_all[:, N_ACT:N_ACT + 1], 1.0, None, ALU.min).then_inc(norms_ready, 1)
                    scales(1, N_O, N_W2)
                    dve.wait_ge(gains_ready, 2)
                    v.tensor_tensor(un_o[0:U, :], unscale[0:U, N_O:N_O + 1], tanh_g[:, 0:1], ALU.mult)
                    v.tensor_scalar(un_up[:, 0:NE], unscale[:, N_W1:N_ACT], 1.0 / LN_SCALE, None, ALU.mult)
                    v.tensor_scalar(un_up[:, NE:NE + 1], unscale[:, N_ACT - 1:N_ACT], 0.5 / LN_SCALE, None,
                                    ALU.mult).then_inc(scales_ready, 1)
                if turn.kind == "first":
                    attention_norm()
                    attention_scale()
                    split_weights(WO, W1)
                if turn.second:
                    split_weights(W2 + 2 * KC, CHUNKS)
                if turn.prev:
                    split_act(4, silu_u)
                    split_act(5, silu_u)
                if turn.prev:
                    free = full(dve, turn, "rank")
                    v.tensor_tensor(coef2[:], bank[BANK["rank"]][0:U, 0:4 * NE].rearrange("p (u r e) -> p u r e", u=2, r=2),
                                    best[:].unsqueeze(3).broadcast_to([U, 2, 2, NE]), ALU.mult).then_inc(free, 1)
                    taken(dve, turn, "rank")
                    v.tensor_tensor(coef[:], coef2[:, :, 0, :], coef2[:, :, 1, :], ALU.add).then_inc(coef_ready, 1)
                    dve.wait_ge(coef_ready, D)
                    gstep(v.tensor_tensor(coef_down[:], coef[:], un_down[0:U, :].unsqueeze(1).broadcast_to([U, 2, NE]), ALU.mult))
                if turn.prev:
                    dve.wait_ge(y_stored, 16 * (D - 1) + 1)
                    carried(dve)
                    down(0)
                if turn.this and turn.kind != "first":
                    attention_norm()
                    attention_scale()
                if turn.prev:
                    down(1)
                    down(2)
                if turn.this:
                    for u in range(2):
                        free = full(dve, turn, f"OT{u}")
                        dve.wait_ge(OT_hi, 2 * D + u + 1)
                        for b in range(2):
                            last = v.scalar_tensor_tensor(
                                OT[:, 1, u, :, b, :],
                                bank[BANK[f"OT{u}"]][:, b * HG * NQ:(b + 1) * HG * NQ].rearrange("p (c q) -> p c q", c=HG),
                                on_scale[:, u:u + 1], OT[:, 0, u, :, b, :], ALU.mult, ALU.subtract)
                        last.then_inc(free, 1)
                if turn.prev:
                    down(3)
                    down(4)
                if turn.kind == "first":
                    split_weights(W1, W1 + KC)
                if turn.this:
                    dve.wait_ge(xr_loaded, 16 * (D + 1))
                    for u in range(2):
                        free = full(dve, turn, f"W{u}")
                        v.scalar_tensor_tensor(x1[:, u, :], bank[BANK[f"W{u}"]][0:U, :], un_on[0:U, u:u + 1], xr[:, u, :],
                                               ALU.mult, ALU.add).then_inc(free, 1)
                        taken(dve, turn, f"W{u}")
                        norm_stats(u, x1, ln2_st, ln2_mv, ln2_stats, ln2_mean, 2 * D + u + 1)
                if turn.prev:
                    down(2 * NE - 1)
                if turn.this:
                    for u in range(2):
                        dve.wait_ge(ln2_rstd, 2 * D + u + 1)
                        v.tensor_scalar(h[:, u, :], x1[:, u, :], ln2_mv[:, u, 0:1], ln2_r[:, u, 1:2],
                                        ALU.subtract, ALU.mult).then_inc(h_ready, 1)
                if turn.kind == "first":
                    free = full(dve, turn, "norms_down")
                    v.tensor_scalar(sq_all[:, N_W2:NORMS], bank[BANK["norms_down"]][:, 0:NE], TINY, None,
                                    ALU.max).then_inc(free, 1)
                    taken(dve, turn, "norms_down")
                    dve.sem_inc(norms_ready, 1)
                    scales(2, N_W2, NORMS)
                    v.tensor_tensor(un_down[:], unscale[:, N_W2:NORMS], unscale[:, N_ACT:N_W2], ALU.mult).then_inc(scales_ready, 1)
                    split_weights(W1 + KC, W1 + 2 * KC)
                assert gate_steps[0] == GATE_STEPS * turn.prev

            GATE_STEPS = 20
            over_turns(dve, body)

        @block.tensor
        def _(pe):
            t = nc.tensor
            pe.sem_inc(g_pe, 1)
            pe.wait_ge(setup_pool, 2)
            pe.wait_ge(row_any_ready, 1)
            t.matmul(bank[5][:, 1:2], half_ident[:].rearrange("p j q -> p (j q)"), row_any_bf[:], start=True, stop=True)
            t.matmul(bank[5][0:U, 0:1], pair_ident[:], row_any_bf[:], start=True, stop=True).then_inc(alive_turned, 1)
            pe.wait_ge(setup_pool, 4)

            def find_window():
                pe.wait_ge(ends_ready, 1)
                for e in range(3):
                    last = t.transpose(bank[7][0:1, e * P:(e + 1) * P], ends[:, e:e + 1], ident[:])
                last.then_inc(ends_turned, 1)

            def transposes(dst, src, rows):
                for k in range(KC):
                    last = t.transpose(dst[:, k * rows:(k + 1) * rows], src[:, k * P:(k + 1) * P], ident[0:rows, 0:rows])
                return last

            def chain(dst, pairs):
                for i, (left, right) in enumerate(pairs):
                    last = t.matmul(dst, left, right, start=i == 0, stop=i == len(pairs) - 1)
                return last

            def split_chain(dst, pairs):
                for i, (left, right) in enumerate(pairs):
                    t.matmul(dst, left(0), right(0), start=i == 0, stop=False)
                    t.matmul(dst, left(0), right(1), start=False, stop=False)
                    last = t.matmul(dst, left(1), right(0), start=False, stop=i == len(pairs) - 1)
                return last

            def score_item(dst, keys, b):
                for hp in range(HP):
                    for j in range(J):
                        c = (hp * J + j) * P
                        last = t.matmul(dst[0:U, c:c + P], QT[:, b, j, 2 * hp:2 * hp + 2, :].rearrange("p c q -> p (c q)"),
                                        keys[:, b, S * j:S * (j + 1), :], start=True, stop=True)
                return last

            def probs_item(dst, b):
                for i in range(HP * J):
                    last = t.transpose(dst[:, i * U:(i + 1) * U],
                                       probs[:, b, S * i:S * (i + 1), :].rearrange("p s k -> p (s k)"), ident[0:U, 0:U])
                return last

            def output_item(dst, values, b):
                for i in range(HP * J):
                    last = t.matmul(dst[0:U, i * OC:(i + 1) * OC], PT[:, b, i, :], values[:, b, i % J, :], start=True, stop=True)
                return last

            def key_item(dst, turned, context_read=None):
                for k in range(KC):
                    last = t.matmul(dst[:, 0:P], wk_sb[:, k, :], turned[:, k, :], start=k == 0, stop=k == KC - 1)
                    if k == 0 and context_read is not None:
                        last.then_inc(context_read, 1)
                return last

            def value_item(dst, turned):
                return chain(dst[:, 0:P], [(turned[:, k, :], wv_sb[:, k, :]) for k in range(KC)])

            def body(turn):
                D = turn.D

                def item(name):
                    at = turn.before(name)
                    if not (isinstance(at, int) and at == 0):
                        pe.wait_ge(bank_free[BANK[name]], at)
                    return bank[BANK[name]]

                def done(name, ins):
                    ins.then_inc(bank_full[BANK[name]], 1)

                def do_scores(b):
                    done(f"S{b}", score_item(item(f"S{b}"), KB, b))

                def do_probs(b):
                    dst = item(f"PT{b}")
                    pe.wait_ge(probs_ready, NB * D + b + 1)
                    done(f"PT{b}", probs_item(dst, b))

                def do_output(b):
                    done(f"O{b}", output_item(item(f"O{b}"), VB, b))

                def do_up(i):
                    dst = item(f"up{i}")
                    e, half = divmod(i, 2)
                    if half == 0:
                        pe.wait_ge(w_lo, W1 + (e + 1) * KC)
                    for m in range(2):
                        k0 = 2 * half + m
                        last = split_chain(dst[:, m * 2 * U:(m + 1) * 2 * U],
                                           [(lambda s, k=k: w_split[:, W1 + e * KC + k, s, k0 * P:(k0 + 1) * P],
                                             lambda s, k=k: hT[:, s, k, :, :].rearrange("p u t -> p (u t)"))
                                            for k in range(KC)])
                    done(f"up{i}", last)

                def do_down(i):
                    u, e = divmod(i, NE)
                    dst = item(f"dn{i}")
                    if u == 0:
                        pe.wait_ge(w_lo, W2 + (e + 1) * KC)
                        pe.wait_ge(act_ready, 6 * (D - 1) + 2 * e + 2)
                    done(f"dn{i}", split_chain(dst[0:U, :], [(lambda s, k=k: act[:, s, e, k, u * U:(u + 1) * U],
                                                              lambda s, k=k: w_split[:, W2 + e * KC + k, s, :])
                                                             for k in range(KC)]))

                def do_queries(items=range(2)):
                    for i in items:
                        dst = item(f"Q{i}")
                        taken(pe, turn, "xT0")
                        taken(pe, turn, "xT1")
                        for m in range(2):
                            c = 2 * i + m
                            last = split_chain(dst[:, m * 2 * U:(m + 1) * 2 * U],
                                               [(lambda s, k=k: w_split[:, WQ + k, s, c * P:(c + 1) * P],
                                                 lambda s, k=k: xnT[:, s, k, :, :].rearrange("p u t -> p (u t)"))
                                                for k in range(KC)])
                        done(f"Q{i}", last)

                def do_norms(name, a, b):
                    dst = item(name)
                    pe.wait_ge(norms_summed, b)
                    done(name, t.matmul(dst[:, 0:b - a], ones[:], sq[:, a:b], start=True, stop=True))

                def do_on_norm():
                    dst = item("on_norm")
                    pe.wait_ge(on_squared, 2 * D + 2)
                    done("on_norm", t.matmul(dst[:, 0:2], ones[0:U, :], on_sq[:], start=True, stop=True))

                def turn_x():
                    for u in range(2):
                        dst = item(f"xT{u}")
                        pe.wait_ge(xn_ready, 2 * (D + 1) + u + 1)
                        done(f"xT{u}", transposes(dst, xn[:, u, :], U))

                def turn_context():
                    dst = item("ctxT")
                    pe.wait_ge(ctx_loaded, 16 * NB * (D + 2))
                    done("ctxT", transposes(dst, ctx_sb, P))

                def do_keys():
                    dst = item("K")
                    taken(pe, turn, "ctxT")
                    done("K", key_item(dst, ctxT_sb, ctx_read))

                def do_values():
                    dst = item("V")
                    taken(pe, turn, "ctxT")
                    done("V", value_item(dst, ctxT_sb))

                if turn.kind == "lead":
                    do_norms("norms_q", N_Q, N_O)
                    find_window()
                    turn_x()
                    pe.wait_ge(verdict_ready, 1)
                    flags.append(pe.value_load(verdict_i[0:1, 1:2], min_val=0, max_val=1))
                    turn_context()
                    pe.wait_ge(w_lo, WO)
                    do_queries([0])
                    pe.wait_ge(wkv_loaded, 32)
                    do_keys()
                    do_values()
                    do_queries([1])
                    pe.wait_ge(consts_ready, 1)
                    pe.wait_ge(bias_ready, 1)
                    pe.wait_ge(gate_weights, 1)
                    return

                if turn.next:
                    turn_context()
                if turn.this:
                    for name in ("Q0", "K", "V") + (() if turn.next else ("Q1",)):
                        pe.wait_ge(bank_free[BANK[name]], turn.before(None, BANK[name]))
                    do_scores(0)
                    do_scores(1)
                if turn.prev:
                    for u in range(2):
                        dst = item(f"hT{u}")
                        pe.wait_ge(h_ready, 2 * (D - 1) + u + 1)
                        done(f"hT{u}", transposes(dst, h[:, u, :], U))
                if turn.this:
                    do_scores(2)
                    do_scores(3)
                if turn.next:
                    do_keys()
                if turn.prev:
                    dst = item("gate")
                    taken(pe, turn, "hT0")
                    taken(pe, turn, "hT1")
                    pe.wait_ge(h_summed, 2 * D)
                    for u in range(2):
                        split_chain(dst[0:U, u * NE:(u + 1) * NE], [(lambda s, k=k: hT[:, s, k, u, :],
                                                                     lambda s, k=k: gw_split[:, s, k * NE:(k + 1) * NE])
                                                                    for k in range(KC)])
                    t.matmul(dst[0:U, 8:10], text_sel[:].rearrange("p a q -> p (a q)"), h_sum[:], start=True, stop=True)
                    done("gate", t.matmul(dst[0:U, 10:12], vision_sel[:].rearrange("p a q -> p (a q)"), h_sum[:],
                                          start=True, stop=True))
                if turn.prev:
                    do_up(0)
                    do_up(1)
                if turn.this:
                    do_probs(0)
                    do_probs(1)
                if turn.prev:
                    do_up(2)
                if turn.this:
                    do_output(0)
                    do_output(1)
                    do_probs(2)
                    do_probs(3)
                if turn.prev:
                    do_up(3)
                if turn.this:
                    do_output(2)
                    do_output(3)

                    def window(n, first_key, last):
                        pe.wait_ge(g_loaded, 16 * NB * (n + 1))
                        pe.wait_ge(g_dve, n * G_DVE + 1)
                        transposes(bank[0], g_ctx, P).then_inc(g_pe, 1)
                        pe.wait_ge(g_act, n * G_ACT + 1)
                        key_item(bank[1], g_ctxT).then_inc(g_pe, 1)
                        value_item(bank[2], g_ctxT).then_inc(g_pe, 1)
                        pe.wait_ge(g_dve, n * G_DVE + 3)
                        for b in range(NB):
                            score_item(bank[3], g_KB, b).then_inc(g_pe, 1)
                            pe.wait_ge(g_act, n * G_ACT + 1 + 2 * b + 2)
                            probs_item(bank[0], b).then_inc(g_pe, 1)
                            pe.wait_ge(g_dve, n * G_DVE + 4 + 6 * b + 5)
                            output_item(bank[1], g_VB, b).then_inc(g_pe, 1)

                    with pe.If(flags[0] > 0):
                        for b in range(NB):
                            taken(pe, turn, f"O{b}")
                        carried(pe)
                        with pe.Fori(0, WINDOWS) as c:
                            window(D * (WINDOWS + 1) + c, c * WIN, False)
                        window(D * (WINDOWS + 1) + WINDOWS, LAST, True)
                        pe.wait_ge(g_dve, (D + 1) * (WINDOWS + 1) * G_DVE + 1)
                        carried(pe)
                if turn.next:
                    turn_x()
                    do_values()
                if turn.kind == "first":
                    do_norms("norms_up", N_O, N_W2)
                    do_on_norm()
                if turn.prev:
                    do_up(4)
                    do_up(5)
                if turn.next:
                    do_queries()
                if turn.prev:
                    dst = item("rank")
                    pe.wait_ge(ranks_ready, D)
                    done("rank", t.matmul(dst[0:U, 0:4 * NE], first_sel[:].rearrange("p a q -> p (a q)"),
                                          rank_hot[:].rearrange("p u r e -> p (u r e)"), start=True, stop=True))
                    do_down(0)
                if turn.this and turn.kind != "first":
                    do_on_norm()
                if turn.prev:
                    do_down(1)
                    do_down(2)
                if turn.this:
                    for u in range(2):
                        dst = item(f"OT{u}")
                        pe.wait_ge(on_ready, 2 * D + u + 1)
                        for b in range(2):
                            for hp in range(HP):
                                c = (b * HP + hp) * U
                                last = t.transpose(dst[:, c:c + U],
                                                   On[:, 2 * u + b, J * hp:J * (hp + 1)].rearrange("p t s d -> p (t s d)"),
                                                   ident[0:U, 0:U])
                        done(f"OT{u}", last)
                if turn.prev:
                    do_down(3)
                    do_down(4)
                if turn.this:
                    if turn.kind == "first":
                        pe.wait_ge(w_lo, W1)
                    for u in range(2):
                        dst = item(f"W{u}")
                        taken(pe, turn, f"OT{u}")
                        done(f"W{u}", split_chain(dst[0:U, :], [(lambda s, c=c: OT[:, s, u, c].rearrange("p b q -> p (b q)"),
                                                                 lambda s, c=c: w_split[:, WO + c, s, :])
                                                                for c in range(HG)]))
                if turn.prev:
                    do_down(5)
                if turn.kind == "first":
                    do_norms("norms_down", N_W2, NORMS)

            flags = []
            over_turns(pe, body)


def kernel(**inputs):
    import numpy as np
    import concourse.bacc as bacc
    from concourse import mybir as mb
    from concourse.bass_utils import run_bass_kernel_spmd as run

    f = {n: np.asarray(a) for n, a in inputs.items()}
    x = f["x"]
    B, NQ, DM = x.shape
    NG, HG, DH = 8, 4, 16
    KC = DM // P

    def rows(a):
        return a.reshape(-1, P, a.shape[-1]).transpose(1, 0, 2)

    arrays = {
        "x": x.reshape(B * NQ, DM),
        "ctx_rows": f["ctx_4096"],
        "mask": f["mask_SxS2_bk0"],
        "g_attn": f["g_xattn"].reshape(1, 1),
        "g_ffn": f["g_ffn"].reshape(1, 1),
        "wq": rows(f["L0_xattn_w_q"].reshape(NG, HG, DH, DM).transpose(3, 1, 0, 2).reshape(DM, DM)),
        "wk": rows(f["L0_xattn_w_k"].T),
        "wv": rows(f["L0_xattn_w_v"].T),
        "wo": f["L0_xattn_w_out"].reshape(DM, NG, HG, DH).transpose(1, 3, 2, 0).reshape(P, HG, DM),
        "gate_w": rows(f["L0_ffn_gate_w"][:DM]).reshape(P, -1),
        "gate_r": f["L0_ffn_gate_w"][DM:],
        "gate_b": f["L0_ffn_gate_b"].reshape(1, -1),
        "w1": f["L0_ffn_w1"].reshape(3 * KC, P, DM).transpose(1, 0, 2),
        "b1": f["L0_ffn_b1"].reshape(3, KC, P).transpose(2, 0, 1),
        "w2": f["L0_ffn_w2"].reshape(3 * KC, P, DM).transpose(1, 0, 2),
        "b2": f["L0_ffn_b2"].reshape(1, -1),
    }
    arrays = {n: np.ascontiguousarray(a) for n, a in arrays.items()}
    nc = bacc.Bacc("TRN2", target_bir_lowering=False, num_devices=1)
    args = [nc.dram_tensor(n, a.shape, mb.dt.from_np(a.dtype), kind="ExternalInput").ap() for n, a in arrays.items()]
    args.append(nc.dram_tensor("out", (B * NQ, DM), mb.dt.float32, kind="ExternalOutput").ap())
    flamingo_block(nc, *args)
    r = run(nc, [arrays], core_ids=[0])
    return r.results[0]["out"].reshape(B, NQ, DM)
```
